# Optimizing a Trainium2 kernel written in Bass

```python
import numpy as np
import jax
import jax.numpy as jnp

def _softmax(x, axis=-1):
    return jax.nn.softmax(x, axis=axis)

def _gelu(x):
    return jax.nn.gelu(x, approximate=True)

def _silu(x):
    return jax.nn.silu(x)

def _sigmoid(x):
    return jax.nn.sigmoid(x)

def _layernorm(x, axis=-1, eps=1e-05):
    m = jnp.mean(x, axis=axis, keepdims=True)
    v = jnp.var(x, axis=axis, keepdims=True)
    return (x - m) / jnp.sqrt(v + eps)

def _scatter_add(tgt, idx, src, axis=0):
    return tgt.at[idx].add(src)

def _segment_sum(src, seg, n):
    return jax.ops.segment_sum(src, seg, n)
kernel_name = 'mk_decoder_preln_d1_seqx_r4_f7262e'

def setup_inputs(seed: int=0):
    np.random.seed(seed)
    _w = jnp.asarray

    def _rec_inputs():
        import jax
        import jax.numpy as jnp
        _rk = jax.random.key(seed)
        x = 7.22e-05 + 1 * jax.random.normal(jax.random.fold_in(_rk, 1), (1, 2048, 256), jnp.float32)
        _lenS = 2048 - jax.random.randint(jax.random.fold_in(_rk, 7), (1,), 0, max(1, 2048 // 4) + 1, jnp.int32)
        _lenS2 = 1601 - jax.random.randint(jax.random.fold_in(_rk, 8), (1,), 0, max(1, 1601 // 4) + 1, jnp.int32)
        _ctx_1024P = jax.random.normal(jax.random.fold_in(_rk, 11), (1, 16, 256), jnp.float32)
        _ctx_1024c = jax.random.dirichlet(jax.random.fold_in(_rk, 511), 0.3 * jnp.ones((16,), jnp.float32), (1, 1601))
        _ctx_1024t = jnp.einsum('bsk,bkd->bsd', _ctx_1024c, _ctx_1024P)
        _ctx_1024t = _ctx_1024t * jax.lax.rsqrt(jnp.mean(jnp.square(_ctx_1024t)) + 1e-12) * 0.953939
        ctx_1024 = 4.13588e-05 + 0.999923 * (_ctx_1024t + 0.3 * jax.random.normal(jax.random.fold_in(_rk, 611), (1, 1601, 256), jnp.float32))
        _validS = jnp.arange(2048)[None, :] < _lenS[:, None]
        _validS2 = jnp.arange(1601)[None, :] < _lenS2[:, None]
        _causal = jnp.tril(jnp.ones((2048, 2048), dtype=bool))
        mask_BxSxS2_ik1 = jnp.where(jnp.broadcast_to(_validS2[:, None, :], (1, 2048, 1601)), 1, 0).astype(jnp.int32)
        return (x, ctx_1024, mask_BxSxS2_ik1)
    x, ctx_1024, mask_BxSxS2_ik1 = _rec_inputs()

    def _L0_attn_setup():
        import jax, jax.numpy as jnp
        from jax import lax
        import numpy as np
        D_MODEL, D_STATE, D_CONV, EXPAND = (256, 16, 4, 2)
        D_INNER = EXPAND * D_MODEL
        BATCH, SEQLEN = (2, 512)

        def _ssm_scan(x_conv, dt, A, B_ssm):
            Bb, L, Di = x_conv.shape
            h0 = jnp.zeros((Bb, Di, A.shape[1]), x_conv.dtype)

            def step(h, inp):
                x_t, dt_t, B_t = inp
                dA = jnp.exp(dt_t[:, :, None] * A)
                h = h * dA + dt_t[:, :, None] * B_t[:, None, :] * x_t[:, :, None]
                return (h, h.sum(axis=2))
            xs = (x_conv.transpose(1, 0, 2), dt.transpose(1, 0, 2), B_ssm.transpose(1, 0, 2))
            _, ys = lax.scan(step, h0, xs)
            return ys.transpose(1, 0, 2)
        key = jax.random.key(seed)
        ks = jax.random.split(key, 8)
        sc = lambda k, shape, s: jax.random.normal(k, shape, jnp.float32) * s
        return {'x': jax.random.normal(ks[0], (BATCH, SEQLEN, D_MODEL), jnp.float32), 'W_in': sc(ks[1], (D_MODEL, 2 * D_INNER), 0.02), 'conv_w': sc(ks[2], (D_INNER, D_CONV), 0.1), 'conv_b': jnp.zeros((D_INNER,), jnp.float32), 'W_x': sc(ks[3], (D_INNER, 2 * D_STATE), 0.02), 'W_dt': sc(ks[4], (D_STATE, D_INNER), 0.1), 'b_dt': jnp.zeros((D_INNER,), jnp.float32), 'A_log': jnp.log(jax.random.uniform(ks[5], (D_INNER, D_STATE), jnp.float32, 0.0001, 1.0)), 'D': jnp.ones((D_INNER,), jnp.float32), 'W_out': sc(ks[6], (D_INNER, D_MODEL), 0.02)}
    _L0_attn_all = _L0_attn_setup()
    _L0_attn_in = {k: v for k, v in _L0_attn_all.items() if k in ('W_in', 'conv_w', 'conv_b', 'W_x', 'W_dt', 'b_dt', 'A_log', 'D', 'W_out')}
    del _L0_attn_all

    def _L0_xattn_setup():
        import jax, jax.numpy as jnp
        import numpy as np
        B, S, E, A = (4, 512, 256, 256)
        key = jax.random.key(seed)
        ks = jax.random.split(key, 10)
        bound = 1.0 / np.sqrt(E)
        return {'query': jax.random.normal(ks[0], (B, S, E), dtype=jnp.float32), 'key': jax.random.normal(ks[1], (B, S, E), dtype=jnp.float32), 'value': jax.random.normal(ks[2], (B, S, E), dtype=jnp.float32), 'mask': jax.random.randint(ks[3], (B, S, S), 0, 2, dtype=jnp.int32), 'Wq': jax.random.uniform(ks[4], (A, E), jnp.float32, -bound, bound), 'bq': jax.random.uniform(ks[5], (A,), jnp.float32, -bound, bound), 'Wk': jax.random.uniform(ks[6], (A, E), jnp.float32, -bound, bound), 'bk': jax.random.uniform(ks[7], (A,), jnp.float32, -bound, bound), 'Wv': jax.random.uniform(ks[8], (A, E), jnp.float32, -bound, bound), 'bv': jax.random.uniform(ks[9], (A,), jnp.float32, -bound, bound)}
    _L0_xattn_all = _L0_xattn_setup()
    _L0_xattn_in = {k: v for k, v in _L0_xattn_all.items() if k in ('Wq', 'bq', 'Wk', 'bk', 'Wv', 'bv')}
    del _L0_xattn_all

    def _L0_ffn_setup():
        import jax, jax.numpy as jnp
        import numpy as np
        B, S, H, I, E, TOPK, KS = (4, 1024, 256, 128, 16, 2, 3)
        key = jax.random.key(seed)
        ks = jax.random.split(key, 9)
        sc = 0.02
        return {'hidden_states': jax.random.normal(ks[0], (B, S, H), dtype=jnp.float32), 'router_w': jax.random.normal(ks[1], (H, E), dtype=jnp.float32) * sc, 'router_bias': jnp.zeros((E,), dtype=jnp.float32), 'expert_gate_w': jax.random.normal(ks[2], (E - 1, H, I), dtype=jnp.float32) * sc, 'expert_up_w': jax.random.normal(ks[3], (E - 1, H, I), dtype=jnp.float32) * sc, 'expert_down_w': jax.random.normal(ks[4], (E - 1, I, H), dtype=jnp.float32) * sc, 'conv_w': jax.random.normal(ks[5], (I, H, KS), dtype=jnp.float32) * sc, 'shared_up_w': jax.random.normal(ks[6], (H, I), dtype=jnp.float32) * sc, 'shared_down_w': jax.random.normal(ks[7], (I, H), dtype=jnp.float32) * sc}
    _L0_ffn_all = _L0_ffn_setup()
    _L0_ffn_in = {k: v for k, v in _L0_ffn_all.items() if k in ('router_w', 'router_bias', 'expert_gate_w', 'expert_up_w', 'expert_down_w', 'conv_w', 'shared_up_w', 'shared_down_w')}
    del _L0_ffn_all
    return {'x': x, 'ctx_1024': ctx_1024, 'mask_BxSxS2_ik1': mask_BxSxS2_ik1, 'L0_attn_W_in': _L0_attn_in['W_in'], 'L0_attn_conv_w': _L0_attn_in['conv_w'], 'L0_attn_conv_b': _L0_attn_in['conv_b'], 'L0_attn_W_x': _L0_attn_in['W_x'], 'L0_attn_W_dt': _L0_attn_in['W_dt'], 'L0_attn_b_dt': _L0_attn_in['b_dt'], 'L0_attn_A_log': _L0_attn_in['A_log'], 'L0_attn_D': _L0_attn_in['D'], 'L0_attn_W_out': _L0_attn_in['W_out'], 'L0_xattn_Wq': _L0_xattn_in['Wq'], 'L0_xattn_bq': _L0_xattn_in['bq'], 'L0_xattn_Wk': _L0_xattn_in['Wk'], 'L0_xattn_bk': _L0_xattn_in['bk'], 'L0_xattn_Wv': _L0_xattn_in['Wv'], 'L0_xattn_bv': _L0_xattn_in['bv'], 'L0_ffn_router_w': _L0_ffn_in['router_w'], 'L0_ffn_router_bias': _L0_ffn_in['router_bias'], 'L0_ffn_expert_gate_w': _L0_ffn_in['expert_gate_w'], 'L0_ffn_expert_up_w': _L0_ffn_in['expert_up_w'], 'L0_ffn_expert_down_w': _L0_ffn_in['expert_down_w'], 'L0_ffn_conv_w': _L0_ffn_in['conv_w'], 'L0_ffn_shared_up_w': _L0_ffn_in['shared_up_w'], 'L0_ffn_shared_down_w': _L0_ffn_in['shared_down_w']}

def reference(x, ctx_1024, mask_BxSxS2_ik1, L0_attn_W_in, L0_attn_conv_w, L0_attn_conv_b, L0_attn_W_x, L0_attn_W_dt, L0_attn_b_dt, L0_attn_A_log, L0_attn_D, L0_attn_W_out, L0_xattn_Wq, L0_xattn_bq, L0_xattn_Wk, L0_xattn_bk, L0_xattn_Wv, L0_xattn_bv, L0_ffn_router_w, L0_ffn_router_bias, L0_ffn_expert_gate_w, L0_ffn_expert_up_w, L0_ffn_expert_down_w, L0_ffn_conv_w, L0_ffn_shared_up_w, L0_ffn_shared_down_w):
    import jax
    import jax.numpy as jnp

    def _L0_attn_ref(x, W_in, conv_w, conv_b, W_x, W_dt, b_dt, A_log, D, W_out):
        import jax, jax.numpy as jnp
        from jax import lax
        import numpy as np
        D_MODEL, D_STATE, D_CONV, EXPAND = (256, 16, 4, 2)
        D_INNER = EXPAND * D_MODEL
        BATCH, SEQLEN = (2, 512)

        def _ssm_scan(x_conv, dt, A, B_ssm):
            Bb, L, Di = x_conv.shape
            h0 = jnp.zeros((Bb, Di, A.shape[1]), x_conv.dtype)

            def step(h, inp):
                x_t, dt_t, B_t = inp
                dA = jnp.exp(dt_t[:, :, None] * A)
                h = h * dA + dt_t[:, :, None] * B_t[:, None, :] * x_t[:, :, None]
                return (h, h.sum(axis=2))
            xs = (x_conv.transpose(1, 0, 2), dt.transpose(1, 0, 2), B_ssm.transpose(1, 0, 2))
            _, ys = lax.scan(step, h0, xs)
            return ys.transpose(1, 0, 2)
        Bb, L, _ = x.shape
        xz = x @ W_in
        x_proj, z = jnp.split(xz, 2, axis=-1)
        xc = lax.conv_general_dilated(x_proj.transpose(0, 2, 1), conv_w[:, None, :], window_strides=(1,), padding=[(D_CONV - 1, 0)], feature_group_count=D_INNER, dimension_numbers=('NCH', 'OIH', 'NCH'))
        x_conv = jax.nn.silu(xc.transpose(0, 2, 1) + conv_b)
        x_ssm = x_conv @ W_x
        dt_in, B_ssm = jnp.split(x_ssm, 2, axis=-1)
        dt = jax.nn.softplus(dt_in @ W_dt + b_dt)
        A = -jnp.exp(A_log)
        y = _ssm_scan(x_conv, dt, A, B_ssm)
        y = y + x_conv * D[None, None, :]
        y = y * jax.nn.silu(z)
        return y @ W_out

    def _L0_xattn_ref(query, key, value, mask, Wq, bq, Wk, bk, Wv, bv):
        import jax, jax.numpy as jnp
        import numpy as np
        B, S, E, A = (4, 512, 256, 256)
        scale = jnp.sqrt(jnp.asarray(A, dtype=jnp.float32))
        q = jnp.einsum('bse,ae->bsa', query, Wq) + bq
        k = jnp.einsum('bse,ae->bsa', key, Wk) + bk
        v = jnp.einsum('bse,ae->bsa', value, Wv) + bv
        scores = jnp.einsum('bqa,bka->bqk', q, k) / scale
        scores = jnp.where(mask == 0, jnp.float32(-10000000000.0), scores)
        attn = jax.nn.softmax(scores, axis=-1)
        return jnp.einsum('bqk,bka->bqa', attn, v)

    def _L0_ffn_ref(hidden_states, router_w, router_bias, expert_gate_w, expert_up_w, expert_down_w, conv_w, shared_up_w, shared_down_w):
        import jax, jax.numpy as jnp
        import numpy as np
        B, S, H, I, E, TOPK, KS = (4, 1024, 256, 128, 16, 2, 3)
        b, s, h = hidden_states.shape
        flat = hidden_states.reshape(b * s, h)
        logits = (flat @ router_w).astype(jnp.float32) + router_bias
        probs = jax.nn.softmax(logits, axis=-1)
        top_w, top_i = jax.lax.top_k(probs, TOPK)
        norm_w = top_w / (jnp.sum(top_w, axis=-1, keepdims=True) + 1e-06)
        norm_w = norm_w.astype(hidden_states.dtype)
        combine = jnp.sum(jax.nn.one_hot(top_i, E, dtype=norm_w.dtype) * norm_w[..., None], axis=1)
        routed = combine[:, E - 1:E] * flat
        for e in range(E - 1):
            y = jax.nn.silu(flat @ expert_gate_w[e]) * (flat @ expert_up_w[e]) @ expert_down_w[e]
            routed = routed + combine[:, e:e + 1] * y
        routed = routed.reshape(b, s, h)
        x_ncw = jnp.transpose(hidden_states, (0, 2, 1))
        gate = jax.lax.conv_general_dilated(x_ncw, conv_w, window_strides=(1,), padding=[(KS - 1, 0)], dimension_numbers=('NCW', 'OIW', 'NCW'))
        gate = jnp.transpose(gate, (0, 2, 1))
        shared = jax.nn.silu(gate) * (hidden_states @ shared_up_w) @ shared_down_w
        return shared + routed
    x = x + _L0_attn_ref(_layernorm(x, axis=-1), L0_attn_W_in, L0_attn_conv_w, L0_attn_conv_b, L0_attn_W_x, L0_attn_W_dt, L0_attn_b_dt, L0_attn_A_log, L0_attn_D, L0_attn_W_out)
    x = x + _L0_xattn_ref(_layernorm(x, axis=-1), ctx_1024, ctx_1024, mask_BxSxS2_ik1, L0_xattn_Wq, L0_xattn_bq, L0_xattn_Wk, L0_xattn_bk, L0_xattn_Wv, L0_xattn_bv)
    x = x + _L0_ffn_ref(_layernorm(x, axis=-1), L0_ffn_router_w, L0_ffn_router_bias, L0_ffn_expert_gate_w, L0_ffn_expert_up_w, L0_ffn_expert_down_w, L0_ffn_conv_w, L0_ffn_shared_up_w, L0_ffn_shared_down_w)
    return x

_drawn_inputs = setup_inputs


def setup_inputs(seed=0):
    import zlib

    import numpy as np

    out = dict(_drawn_inputs(seed))
    spreads = {'L0_attn_conv_b': (0.0, 0.1),
     'L0_attn_b_dt': (0.0, 0.1),
     'L0_attn_D': (1.0, 0.2),
     'L0_ffn_router_bias': (0.0, 0.1)}
    factors = {}
    for name, (base, spread) in spreads.items():
        noise = np.random.default_rng([zlib.crc32(name.encode()), seed]).standard_normal(out[name].shape)
        drawn = base * np.exp(spread * noise) if base else spread * noise
        out[name] = jnp.asarray(drawn.astype(out[name].dtype))
    for name, factor in factors.items():
        out[name] = (out[name] * factor).astype(out[name].dtype)
    return out
```

```python
import concourse.bass as bass
from concourse import mybir
from contextlib import ExitStack

F32 = mybir.dt.float32
F32R = mybir.dt.float32r
I32 = mybir.dt.int32
U32 = mybir.dt.uint32
ALU = mybir.AluOpType
ACT = mybir.ActivationFunctionType
AXX = mybir.AxisListType.X
ds = bass.ds

P = 128
BANK = 512
SEQ = 2048
DM = 256
KE = DM // P
NT = SEQ // P
EPS = 1e-5

DI = 512
KM = DI // P
NS = 16
NTAP = 4
HALF = SEQ // 2
HT = HALF // P
CH = BANK
CHT = CH // P
QC = P // 32
NG = NS // QC
TILES = KM * NG * QC

SK = 1601
KC = (SK + P - 1) // P
SKP = KC * P
SKE = SK + SK % 2
NEG = -1.0e10
SCALE = 1.0 / 16.0

NE = 16
NX = NE - 1
FI = 128
KS = 3
NCH = SEQ // BANK


def plain(dve, spare, n):
    dve.memset(spare[:, n:n + 1], 0.0)


def chain(eng, sem, base):
    n = [0]

    def link(ins):
        n[0] += 1
        ins.then_inc(sem, 1)
        eng.wait_ge(sem, base + n[0])
    return link, n


def scan_block(nc, x, w, x_res, ident, power, spare, ps):
    LINKS = 30
    ALINKS = 8
    with ExitStack() as ctx:
        def sb(name, shape, dt=F32, stack=ctx):
            return stack.enter_context(nc.sbuf_tensor(name, shape, dt))

        def sem(name):
            return ctx.enter_context(nc.semaphore(name))

        w_in_hi = sb("w_in_hi", [P, KE, 2 * DI], F32R)
        w_in_lo = sb("w_in_lo", [P, KE, 2 * DI], F32R)
        w_x = sb("w_x", [P, KM, 2 * NS])
        w_dt = sb("w_dt", [33, DI])
        w_out = sb("w_out", [P, KM, DM])
        conv_w = sb("conv_w", [P, KM, NTAP])
        conv_b = sb("conv_b", [P, KM])
        d_skip = sb("d_skip", [P, KM])
        a_log = sb("a_log", [P, DI // 32, NS])
        neg_a = sb("neg_a", [P, TILES])
        pick = sb("pick", [P, 32])
        eps = sb("eps", [P, CHT])
        zs = sb("zs", [P, KM, HALF])
        xc = sb("xc", [P, KM, HALF])
        dt = sb("dt", [P, KM, HALF])
        ut = sb("ut", [P, HT, DI])
        bt = sb("bt", [P, HT, NS])
        hlast = sb("hlast", [P, TILES])
        tail = sb("tail", [P, KM, NTAP - 1])
        xs = sb("xs", [33, CH])
        dt_rep = sb("dt_rep", [P, 2, QC, HALF])
        with ExitStack() as front:
            w_raw = sb("w_raw", [P, KE, 2 * DI], F32, front)
            xn = sb("xn", [P, CHT, DM], F32, front)
            stats = sb("stats", [P, CHT, 6], F32, front)
            mv = sb("mv", [P, CHT, 2], F32, front)
            rstd = sb("rstd", [P, CHT], F32, front)
            xnT_hi = sb("xnT_hi", [P, KE, CH], F32R, front)
            xnT_lo = sb("xnT_lo", [P, KE, CH], F32R, front)
            xp = sb("xp", [P, KM, NTAP - 1 + CH], F32, front)
            conv = sb("conv", [P, 2, CH], F32, front)
            sp = sb("sp", [P, KM, CH], F32, front)
            u = sb("u", [P, KM, CH], F32, front)
        with ExitStack() as rings:
            pu = sb("pu", [P, 2, HT, P], F32, rings)
            da = sb("da", [P, 4, HALF], F32, rings)
            h = sb("h", [P, 8, HALF], F32, rings)
        psT = ps[:, 0:2 * BANK].rearrange("p (k n) -> p k n", k=2)
        psM = ps[:, 2 * BANK:4 * BANK].rearrange("p (s n) -> p s n", s=2)
        psG = ps[:, 4 * BANK:8 * BANK].rearrange("p (m n) -> p m n", m=KM)
        psU = ps[:, 0:4 * BANK].rearrange("p (s n) -> p s n", s=2)
        psY = ps[:, 4 * BANK:8 * BANK].rearrange("p (s n) -> p s n", s=2)

        x_in, x_rest, s_win, s_small, s_zero, s_alog = sem("x_in"), sem("x_rest"), sem("w_in_in"), sem("small_in"), sem("zeroed"), sem("alog_in")
        ident_made, ident_ok = sem("ident_made"), sem("ident_ok")
        w_ready, a_exp, consts_ready = sem("w_in_split"), sem("a_exp"), sem("consts_ready")
        dve_link, act_link = sem("dve_link"), sem("act_link")
        mv_ready, var_eps, rstd_ready = sem("mv_ready"), sem("var_eps"), sem("rstd_ready")
        xn_ready, xnT_ps, hi_ready, lo_ready = sem("xn_ready"), sem("xnT_ps"), sem("xnT_hi_ready"), sem("xnT_lo_ready")
        mm_ready, mm_evac = sem("mm_ready"), sem("mm_evac")
        conv_done, xc_ready = sem("conv_done"), sem("xc_ready")
        dtlin_ready, sp_ready, dt_ready, u_ready = sem("dtlin_ready"), sem("sp_ready"), sem("dt_ready"), sem("u_ready")
        uT_ps, ut_ready = sem("uT_ps"), sem("ut_ready")
        rep_in = [sem(f"dt_rep_in{i}") for i in range(2)]
        rep_used = [sem(f"dt_rep_used{i}") for i in range(2)]
        pu_ready = sem("pu_ready")
        transposed = [sem(f"transposed{i}") for i in range(2)]
        exp_ready = sem("exp_ready")
        scanned = [sem(f"scanned{i}") for i in range(4)]
        saved = [sem(f"saved{i}") for i in range(2)]
        summed = [sem(f"summed{i}") for i in range(2)]
        y_evac = [sem(f"y_evac{i}") for i in range(2)]
        gated = sem("gated")
        proj_ps, x1_done = sem("proj_ps"), sem("x1_done")

        block = ctx.enter_context(nc.Block())

        @block.sync
        def _(sp_):
            xv = x[0].rearrange("(n p) d -> p n d", p=P)
            sp_.dma_start(x_res[:, 0:CHT, :], xv[:, 0:CHT, :]).then_inc(x_in, 16)
            sp_.dma_start(w_raw[:, :, :], w["W_in"].rearrange("(k p) n -> p k n", p=P)).then_inc(s_win, 16)
            sp_.dma_start(conv_w[:, :, :], w["conv_w"].rearrange("(m p) k -> p m k", p=P)).then_inc(s_small, 16)
            sp_.dma_start(conv_b[:, :], w["conv_b"].rearrange("(m p) -> p m", p=P), allow_slow_non_contiguous=True).then_inc(s_small, 16)
            sp_.dma_start(d_skip[:, :], w["D"].rearrange("(m p) -> p m", p=P), allow_slow_non_contiguous=True).then_inc(s_small, 16)
            sp_.dma_start(w_x[:, :, :], w["W_x"].rearrange("(m p) n -> p m n", p=P)).then_inc(s_small, 16)
            sp_.dma_start(w_out[:, :, :], w["W_out"].rearrange("(m p) n -> p m n", p=P)).then_inc(s_small, 16)
            for q in range(QC):
                sp_.dma_start(a_log[32 * q:32 * q + 32, :, :],
                              w["A_log"].rearrange("(b p) n -> p b n", p=32)).then_inc(s_alog, 16)
            sp_.wait_ge(s_zero, 1)
            sp_.dma_start(w_dt[0:NS, :], w["W_dt"]).then_inc(s_small, 16)
            sp_.dma_start(w_dt[32:33, :], w["b_dt"].rearrange("(a n) -> a n", a=1)).then_inc(s_small, 16)
            sp_.dma_start(x_res[:, CHT:, :], xv[:, CHT:, :]).then_inc(x_rest, 16)
            for H in range(2):
                sp_.wait_ge(dt_ready, 2 * H + 2)
                for B in range(KM):
                    sp_.wait_ge(rep_used[B % 2], 2 * H + B // 2)
                    for j in range(QC):
                        for q in range(QC):
                            sp_.dma_start(dt_rep[32 * q:32 * q + 32, B % 2, j, :],
                                          dt[32 * j:32 * j + 32, B, :]).then_inc(rep_in[B % 2], 16)

        @block.gpsimd
        def _(pool):
            pool.memset(w_dt[:, :], 0.0).then_inc(s_zero, 1)
            pool.memset(power[:, :], -0.5)
            pool.memset(eps[:, :], EPS)
            pool.memset(ident[:, :], 0.0).then_inc(ident_made, 1)
            pool.wait_ge(ident_made, 1)
            pool.affine_select(out=ident[:, :], in_=ident[:, :], compare_op=ALU.not_equal, fill=1.0, base=0,
                               pattern=[[-1, P]], channel_multiplier=1).then_inc(ident_ok, 1)
            for H in range(2):
                for c in range(2):
                    pool.wait_ge(mv_ready, 2 * H + c + 1)
                    pool.tensor_tensor(rstd[:, :], mv[:, :, 1], eps[:, :], ALU.add).then_inc(var_eps, 1)
                    pool.wait_ge(var_eps, 2 * H + c + 1)
                    pool.tensor_tensor(rstd[:, :], rstd[:, :], power[:, 0:CHT], ALU.pow).then_inc(rstd_ready, 1)
                pool.wait_ge(ut_ready, 2 * H + 2)
                for k in range(TILES):
                    B, g, j = k // 16, k // 4 % 4, k % 4
                    b = B * QC + j
                    pool.wait_ge(transposed[k % 2], H * (TILES // 2) + (k - 2) // 2 + 1)
                    pool.tensor_tensor(
                        pu[:, k % 2, :, :].rearrange("p t (n d) -> p t n d", n=QC),
                        ut[:, :, 32 * b:32 * b + 32].unsqueeze(2).to_broadcast([P, HT, QC, 32]),
                        bt[:, :, QC * g:QC * g + QC].unsqueeze(3).to_broadcast([P, HT, QC, 32]),
                        ALU.mult).then_inc(pu_ready, 1)

        @block.scalar
        def _(act):
            act.wait_ge(s_alog, 16 * QC)
            act.activation(a_log[:, :, :], a_log[:, :, :], ACT.Exp).then_inc(a_exp, 1)
            for H in range(2):
                link, n = chain(act, act_link, H * ALINKS)
                for c in range(2):
                    q = 2 * H + c
                    cols = slice(c * CH, (c + 1) * CH)
                    if c == 0:
                        act.wait_ge(x1_done, HT * H)
                    act.wait_ge(consts_ready, 1)
                    act.wait_ge(conv_done, KM * q)
                    link(act.activation(xp[:, :, 0:NTAP - 1], tail[:, :, :], ACT.Copy))
                    act.wait_ge(xnT_ps, q + 1)
                    for k in range(KE):
                        act.activation(xnT_hi[:, k, :], psT[:, k, :], ACT.Copy).then_inc(hi_ready, 1)

                    def evac(i, out, src, func):
                        act.wait_ge(mm_ready, 10 * q + i + 1)
                        return act.activation(out, src, func).then_inc(mm_evac, 1)
                    for m in range(KM):
                        evac(m, xp[:, m, NTAP - 1:], psM[:, m % 2, :], ACT.Copy)
                    act.wait_ge(mm_evac, 10 * q + KM)
                    link(act.activation(tail[:, :, :], xp[:, :, CH:], ACT.Copy))
                    for m in range(KM):
                        evac(KM + m, zs[:, m, cols], psM[:, m % 2, :], ACT.Silu)
                        act.wait_ge(conv_done, KM * q + m + 1)
                        act.activation(xc[:, m, cols], conv[:, m % 2, :], ACT.Silu).then_inc(xc_ready, 1)
                    evac(8, xs[0:32, :], psM[0:32, 0, :], ACT.Copy)
                    evac(9, bt[:, c * CHT:(c + 1) * CHT, :],
                         psM[:, 1, 0:CHT * 32].rearrange("p (t n) -> p t n", t=CHT)[:, :, NS:2 * NS], ACT.Copy)
                    act.wait_ge(dtlin_ready, q + 1)
                    link(act.activation(sp[:, :, :], psG, ACT.Abs))
                    link(act.activation(sp[:, :, :], sp[:, :, :], ACT.Exp, scale=-1.0))
                    act.activation(sp[:, :, :], sp[:, :, :], ACT.Ln, bias=1.0).then_inc(sp_ready, 1)
                    act.wait_ge(uT_ps, q + 1)
                    act.activation(ut[:, c * CHT:(c + 1) * CHT, :], psG, ACT.Copy).then_inc(ut_ready, 1)

                def save(s):
                    for j in range(QC):
                        act.wait_ge(scanned[j], H * 16 + s + 1)
                    act.activation(hlast[:, 4 * s:4 * s + 4], h[:, 4 * (s % 2):4 * (s % 2) + 4, HALF - 1],
                                   ACT.Copy).then_inc(saved[s % 2], 1)
                for k in range(TILES):
                    B, s, j = k // 16, k // 4, k % 4
                    if k == 0:
                        act.wait_ge(ut_ready, 2 * H + 2)
                    if k % 16 == 0:
                        act.wait_ge(rep_in[B % 2], (2 * H + B // 2 + 1) * 16 * QC * QC)
                    act.wait_ge(scanned[k % 4], H * 16 + (k - 4) // 4 + 1)
                    act.activation(da[:, k % 4, :], dt_rep[:, B % 2, j, :], ACT.Exp,
                                   scale=neg_a[:, k:k + 1]).then_inc(exp_ready, 1)
                    if k % 16 == 15:
                        act.wait_ge(exp_ready, H * TILES + k + 1)
                        act.sem_inc(rep_used[B % 2], 1)
                    if j == 1 and s >= 1:
                        save(s - 1)
                save(TILES // 4 - 1)
                assert n[0] == ALINKS

        @block.vector
        def _(dve):
            setup, _n = chain(dve, w_ready, 0)
            dve.memset(tail[:, :, :], 0.0)
            dve.memset(hlast[:, :], 0.0)
            dve.memset(xs[32:33, :], 1.0)
            dve.wait_ge(ident_ok, 1)
            for q in range(QC):
                dve.tensor_copy(pick[32 * q:32 * q + 32, :], ident[32 * q:32 * q + 32, 32 * q:32 * q + 32])
            dve.wait_ge(s_win, 16)
            setup(dve.tensor_copy(w_in_hi[:, :, :], w_raw[:, :, :]))
            dve.tensor_tensor(w_in_lo[:, :, :], w_raw[:, :, :], w_in_hi[:, :, :].bitcast(F32),
                              ALU.subtract).then_inc(w_ready, 1)
            dve.wait_ge(w_ready, 2)
            dve.wait_ge(a_exp, 1)
            for q in range(QC):
                rows = slice(32 * q, 32 * q + 32)
                dst = neg_a[rows, :].rearrange("p (b g j) -> p b g j", b=KM, g=NG)
                src = a_log[rows, :, :].rearrange("p (b j) (g n) -> p n b g j", b=KM, n=QC)[:, q]
                last = dve.tensor_scalar(dst, src, -1.0, None, ALU.mult)
            last.then_inc(consts_ready, 1)
            dve.wait_ge(s_small, 16 * 7)
            for H in range(2):
                link, n = chain(dve, dve_link, H * LINKS)
                for c in range(2):
                    q = 2 * H + c
                    cols = slice(c * CH, (c + 1) * CH)
                    if c == 0:
                        dve.wait_ge(x_in, 16)
                    else:
                        dve.wait_ge(x_rest, 16)
                    dve.wait_ge(xnT_ps, q)
                    for t in range(CHT):
                        last = dve.bn_stats(stats[:, t, :], x_res[:, ds(q * CHT + t, 1), :])
                    link(last)
                    plain(dve, spare, 0)
                    for t in range(CHT):
                        last = dve.bn_aggr(mv[:, t, :], stats[:, t, :])
                    last.then_inc(mv_ready, 1)
                    dve.wait_ge(rstd_ready, q + 1)
                    for t in range(CHT):
                        last = dve.tensor_scalar(xn[:, t, :], x_res[:, ds(q * CHT + t, 1), :].rearrange("p a d -> p (a d)"),
                                                 mv[:, t, 0:1], rstd[:, t:t + 1], ALU.subtract, ALU.mult)
                    last.then_inc(xn_ready, 1)
                    for k in range(KE):
                        dve.wait_ge(hi_ready, 2 * q + k + 1)
                        dve.tensor_tensor(xnT_lo[:, k, :], psT[:, k, :], xnT_hi[:, k, :].bitcast(F32),
                                          ALU.subtract).then_inc(lo_ready, 1)
                    for m in range(KM):
                        dve.wait_ge(mm_evac, 10 * q + m + 1)
                        dve.wait_ge(xc_ready, KM * q + max(m - 1, 0))
                        acc = conv[:, m % 2, :]
                        link(dve.tensor_scalar(acc, xp[:, m, 0:CH], conv_w[:, m, 0:1], conv_b[:, m:m + 1],
                                               ALU.mult, ALU.add))
                        for k in range(1, NTAP):
                            last = dve.scalar_tensor_tensor(acc, xp[:, m, k:k + CH], conv_w[:, m, k:k + 1], acc,
                                                            ALU.mult, ALU.add)
                            if k < NTAP - 1:
                                link(last)
                        last.then_inc(conv_done, 1)
                    dve.wait_ge(sp_ready, q + 1)
                    dve.scalar_tensor_tensor(dt[:, :, cols], psG, 0.0, sp[:, :, :], ALU.max, ALU.add).then_inc(dt_ready, 1)
                    dve.wait_ge(dt_ready, q + 1)
                    dve.wait_ge(uT_ps, q)
                    dve.tensor_tensor(u[:, :, :], dt[:, :, cols], xc[:, :, cols], ALU.mult).then_inc(u_ready, 1)

                def gate(B):
                    dve.wait_ge(summed[1], H * 8 + 2 * B + 2)
                    y = psY[:, B % 2, :]
                    link(dve.scalar_tensor_tensor(xc[:, B, :], xc[:, B, :], d_skip[:, B:B + 1], y, ALU.mult, ALU.add))
                    dve.tensor_tensor(zs[:, B, :], xc[:, B, :], zs[:, B, :], ALU.mult).then_inc(gated, 1)
                for k in range(TILES):
                    s, j = k // 4, k % 4
                    if j == 0:
                        dve.wait_ge(summed[s % 2], H * 8 + (s - 2) // 2 + 1)
                        dve.wait_ge(saved[s % 2], H * 8 + (s - 2) // 2 + 1)
                    dve.wait_ge(transposed[k % 2], H * (TILES // 2) + k // 2 + 1)
                    dve.wait_ge(exp_ready, H * TILES + k + 1)
                    dve.tensor_tensor_scan(h[:, 4 * (s % 2) + j, :], da[:, k % 4, :], psU[:, k % 2, :],
                                           hlast[:, k:k + 1], ALU.mult, ALU.add).then_inc(scanned[k % 4], 1)
                    if k % 16 == 4 and k > 16:
                        gate(k // 16 - 1)

                gate(KM - 1)
                for t in range(HT):
                    dve.wait_ge(proj_ps, HT * H + t + 1)
                    row = x_res[:, ds(H * HT + t, 1), :].rearrange("p a d -> p (a d)")
                    dve.tensor_tensor(row, psM[:, t % 2, 0:DM], row, ALU.add).then_inc(x1_done, 1)
                assert n[0] == LINKS, n

        @block.tensor
        def _(pe):
            pe.wait_ge(ident_ok, 1)
            pe.wait_ge(w_ready, 2)
            pe.wait_ge(consts_ready, 1)
            pe.wait_ge(s_small, 16 * 7)
            for H in range(2):
                for c in range(2):
                    q = 2 * H + c
                    pe.wait_ge(x1_done, HT * H)
                    pe.wait_ge(xn_ready, q + 1)
                    pe.wait_ge(lo_ready, 2 * q)
                    for t in range(CHT):
                        for k in range(KE):
                            last = pe.transpose(psT[:, k, t * P:(t + 1) * P], xn[:, t, k * P:(k + 1) * P], ident[:, :])
                    last.then_inc(xnT_ps, 1)
                    pe.wait_ge(lo_ready, 2 * q + 2)
                    for m in range(2 * KM):
                        pe.wait_ge(mm_evac, 10 * q + max(m - 1, 0))
                        i = 0
                        for k in range(KE):
                            for a, b in ((w_in_hi, xnT_hi), (w_in_hi, xnT_lo), (w_in_lo, xnT_hi)):
                                last = pe.matmul(psM[:, m % 2, :], a[:, k, m * P:(m + 1) * P], b[:, k, :],
                                                 start=(i == 0), stop=(i == 3 * KE - 1))
                                i += 1
                        last.then_inc(mm_ready, 1)
                    pe.wait_ge(xc_ready, KM * q + KM)
                    pe.wait_ge(mm_evac, 10 * q + 7)
                    for k in range(KM):
                        last = pe.matmul(psM[0:32, 0, :], w_x[:, k, :], xc[:, k, c * CH:(c + 1) * CH],
                                         start=(k == 0), stop=(k == KM - 1))
                    last.then_inc(mm_ready, 1)
                    pe.wait_ge(ut_ready, q)
                    pe.wait_ge(mm_evac, 10 * q + 9)
                    for m in range(KM):
                        last = pe.matmul(psG[:, m, :], w_dt[:, m * P:(m + 1) * P], xs[:, :], start=True, stop=True)
                    last.then_inc(dtlin_ready, 1)
                    for t in range(CHT):
                        last = pe.transpose(psM[:, 1, t * 32:(t + 1) * 32], xs[0:32, t * P:(t + 1) * P], ident[0:32, 0:32])
                    last.then_inc(mm_ready, 1)
                    pe.wait_ge(u_ready, q + 1)
                    for t in range(CHT):
                        for m in range(KM):
                            last = pe.transpose(psG[:, t, m * P:(m + 1) * P], u[:, m, t * P:(t + 1) * P], ident[:, :])
                    last.then_inc(uT_ps, 1)

                def add_states(s):
                    B, g = s // 4, s % 4
                    if g == 0:
                        pe.wait_ge(gated, 4 * H + max(B - 1, 0))
                    for j in range(QC):
                        pe.wait_ge(scanned[j], H * 16 + s + 1)
                    for n in range(HALF // BANK):
                        for j in range(QC):
                            last = pe.matmul(psY[32 * j:32 * j + 32, B % 2, n * BANK:(n + 1) * BANK], pick[:, :],
                                             h[:, 4 * (s % 2) + j, n * BANK:(n + 1) * BANK],
                                             start=(g == 0), stop=(g == NG - 1))
                    last.then_inc(summed[s % 2], 1)
                for k in range(TILES):
                    s, j = k // 4, k % 4
                    if k == 0:
                        pe.wait_ge(ut_ready, 2 * H + 2)
                        pe.wait_ge(mm_evac, 20 * H + 20)
                    pe.wait_ge(pu_ready, H * TILES + k + 1)
                    pe.wait_ge(scanned[(k - 2) % 4], H * 16 + (k - 2) // 4 + 1)
                    for t in range(HT):
                        last = pe.transpose(psU[:, k % 2, t * P:(t + 1) * P], pu[:, k % 2, t, :], ident[:, :])
                    last.then_inc(transposed[k % 2], 1)
                    if j == 1 and s >= 1:
                        add_states(s - 1)
                add_states(TILES // 4 - 1)
                pe.wait_ge(gated, 4 * H + 4)
                for t in range(HT):
                    pe.wait_ge(x1_done, HT * H + max(t - 1, 0))
                    for m in range(KM):
                        last = pe.matmul(psM[:, t % 2, 0:DM], zs[:, m, t * P:(t + 1) * P], w_out[:, m, :],
                                         start=(m == 0), stop=(m == KM - 1))
                    last.then_inc(proj_ps, 1)



def attention_block(nc, ctx_in, mask, w, x_res, xn3, x3_hi, x3_lo, ident, spare, ps):
    GRP = [(g * 4, min(g * 4 + 4, KC)) for g in range((KC + 3) // 4)]
    NGRP = len(GRP)
    SPLIT = [(0, 2 * BANK), (2 * BANK, SK)]
    KCOL = [(a * P, min(b * P, SKP)) for a, b in GRP]
    SCOL = [(n * BANK, min((n + 1) * BANK, SKE)) for n in range(NGRP)]
    with ExitStack() as ctx:
        def sb(name, shape, dt=F32, stack=ctx):
            return stack.enter_context(nc.sbuf_tensor(name, shape, dt))

        def sem(name):
            return ctx.enter_context(nc.semaphore(name))

        k_hi, k_lo = sb("k_hi", [P, KE, SKP], F32R), sb("k_lo", [P, KE, SKP], F32R)
        v_hi, v_lo = sb("v_hi", [P, KC, DM], F32R), sb("v_lo", [P, KC, DM], F32R)
        wqT = sb("wqT", [P, KE, DM])
        bq, bk = sb("bq", [P, KE]), sb("bk", [P, KE])
        bv = sb("bv", [P, DM])
        w_raw = sb("w_qkv_raw", [P, 3, KE, DM])
        xqT = sb("xqT", [P, KE, P])
        q_hi, q_lo = sb("q_hi", [P, 2, KE, P], F32R), sb("q_lo", [P, 2, KE, P], F32R)
        stats = sb("attn_stats", [P, NT, 6])
        mv = sb("attn_mv", [P, NT, 2])
        xn2 = sb("xn2", [P, 2, DM])
        xn3s = sb("xn3s", [P, 2, DM])
        stats3, mv3s, rstd3s = sb("stats3", [P, 2, 6]), sb("mv3s", [P, 2, 2]), sb("rstd3s", [P, 2])
        rstd = sb("attn_rstd", [P, NT])
        eps = sb("eps3", [P, 1])
        powers = sb("attn_powers", [P, NT])
        mx, nb, rs, rinv = sb("mx", [P, 2]), sb("nb", [P, 2]), sb("rs", [P, 2]), sb("rinv", [P, 2])
        mask_sb = sb("mask_sb", [P, 2, SK], I32)
        with ExitStack() as prep:
            c_raw = sb("c_raw", [P, KC, DM], F32, prep)
            c_hi, c_lo = sb("c_hi", [P, KE, SKP], F32R, prep), sb("c_lo", [P, KE, SKP], F32R, prep)
            wk_hi, wk_lo = sb("wk_hi", [P, KE, DM], F32R, prep), sb("wk_lo", [P, KE, DM], F32R, prep)
            wv_hi, wv_lo = sb("wv_hi", [P, KE, DM], F32R, prep), sb("wv_lo", [P, KE, DM], F32R, prep)
        with ExitStack() as rings:
            sc = sb("sc", [P, 2, SK], F32, rings)
            pr = sb("pr", [P, 2, SKP], F32, rings)
            p_hi, p_lo = sb("p_hi", [P, 2, KC, P], F32R, rings), sb("p_lo", [P, 2, KC, P], F32R, rings)

        bank = [ps[:, n * BANK:(n + 1) * BANK] for n in range(8)]
        psS = ps[:, 0:4 * BANK]
        psP = bank[4:6]
        psA, psO = bank[6], bank[7]

        w_in, b_in, c_in, c_zero = sem("wqkv_in"), sem("bqkv_in"), sem("ctx_in"), sem("ctx_zeroed")
        mask_in = [sem(f"mask_in{i}") for i in range(2)]
        mv2, ve2, rstd2, xn2_ready, bv_added = sem("mv2"), sem("ve2"), sem("rstd2"), sem("xn2_ready"), sem("bv_added")
        prep_ps, prep_hi, prep_lo = sem("prep_ps"), sem("prep_hi"), sem("prep_lo")
        pad_zero = sem("pad_zeroed")
        xq_ps, xq_ready, q_ps, qhi_ready, qlo_ready = sem("xq_ps"), sem("xq_ready"), sem("q_ps"), sem("qhi_ready"), sem("qlo_ready")
        filled, scores_ps, masked, nb_ready, exp_done = sem("filled"), sem("scores_ps"), sem("masked"), sem("nb_ready"), sem("exp_done")
        pt_ps, pthi_ready, ptlo_ready, pv_ps = sem("pt_ps"), sem("pthi_ready"), sem("ptlo_ready"), sem("pv_ps")
        xn3_kept = sem("xn3_kept")
        x2_ready, mv3, ve3, rstd3, xn3_ready = sem("x2_ready"), sem("mv3"), sem("ve3"), sem("rstd3"), sem("xn3_ready")
        x3_ps, x3hi_ready, x3lo_ready = sem("x3_ps"), sem("x3hi_ready"), sem("x3lo_ready")
        dve_link = sem("dve_link_b")
        MASK_LINKS, X2_LINKS = 2, 3

        wq_items = [(bank[0].rearrange("p (k n) -> p k n", k=KE), wqT[:, :, :], None, None)]
        wkv_items = [(bank[n].rearrange("p (k n) -> p k n", k=KE), hi[:, :, :], lo[:, :, :], None)
                     for n, (hi, lo) in ((1, (wk_hi, wk_lo)), (2, (wv_hi, wv_lo)))]
        ctx_items = [(bank[(3 + n) % 8][:, 0:b - a], c_hi[:, k, a:b], c_lo[:, k, a:b], None)
                     for n, (k, (a, b)) in enumerate([(k, ab) for k in range(KE) for ab in KCOL])]
        k_items = [(bank[(3 + n) % 8][:, 0:b - a], k_hi[:, m, a:b], k_lo[:, m, a:b], bk[:, m:m + 1])
                   for n, (m, (a, b)) in enumerate([(m, ab) for m in range(KE) for ab in KCOL])]
        v_items = [(bank[(3 + n) % 8][:, 0:DM], v_hi[:, c, :], v_lo[:, c, :], None) for n in range(KC) for c in [n]]
        items = wq_items + wkv_items + ctx_items + k_items + v_items

        block = ctx.enter_context(nc.Block())

        def tiles(eng, step):
            for i in range(-2, 4):
                step(i, i // 2, i % 2)
            with eng.Fori(2, NT // 2 - 1) as I:
                for p in range(2):
                    step(2 * I + p, I, p)
            for i in range(NT - 2, NT + 3):
                step(i, i // 2, i % 2)

        def on(i, d, lo=0, hi=NT):
            return not isinstance(i, int) or lo <= i + d < hi

        @block.sync
        def _(sp_):
            sp_.wait_ge(c_zero, 1)
            sp_.dma_start(c_raw[:, 0:KC - 1, :], ctx_in[0, 0:(KC - 1) * P, :].rearrange("(n p) d -> p n d", p=P)).then_inc(c_in, 16)
            sp_.dma_start(c_raw[0:SK - (KC - 1) * P, KC - 1, :], ctx_in[0, (KC - 1) * P:, :]).then_inc(c_in, 16)
            for n, name in enumerate(("Wq", "Wk", "Wv")):
                sp_.dma_start(w_raw[:, n, :, :], w[name].rearrange("(k p) e -> p k e", p=P)).then_inc(w_in, 16)
            for t, name in ((bq, "bq"), (bk, "bk")):
                sp_.dma_start(t[:, :], w[name].rearrange("(k p) -> p k", p=P), allow_slow_non_contiguous=True).then_inc(b_in, 16)
            sp_.dma_start(bv[:, :], w["bv"].rearrange("(a n) -> a n", a=1).to_broadcast([P, DM])).then_inc(b_in, 16)

            def step(i, n, par):
                if on(i, 0):
                    if not isinstance(i, int) or i >= 2:
                        sp_.wait_ge(masked, 2 * (i - 1))
                    sp_.dma_start(mask_sb[:, par, :], mask[0, ds(i * P, P), :]).then_inc(mask_in[par], 16)
            tiles(sp_, step)

        @block.gpsimd
        def _(pool):
            pool.memset(c_raw[:, KC - 1, :], 0.0).then_inc(c_zero, 1)
            pool.memset(eps[:, :], EPS)
            pool.memset(powers[:, :], -0.5).then_inc(ve2, 1)
            pool.wait_ge(mv2, 1)
            pool.tensor_scalar(rstd[:, :], mv[:, :, 1], EPS, None, ALU.add).then_inc(ve2, 1)
            pool.wait_ge(ve2, 2)
            pool.tensor_tensor(rstd[:, :], rstd[:, :], powers[:, :], ALU.pow).then_inc(rstd2, 1)
            pool.wait_ge(b_in, 48)
            pool.wait_ge(prep_lo, len(items) - 1)
            pool.wait_ge(prep_ps, len(items))
            for par in range(2):
                pool.memset(pr[:, par, SK:], 0.0).then_inc(pad_zero, 1)

            def step(i, n, par):
                if on(i, 0):
                    if not isinstance(i, int) or i >= 1:
                        pool.wait_ge(exp_done, i)
                    pool.wait_ge(xn2_ready, i + 1)
                    row = x_res[:, ds(i, 1), :].rearrange("p a d -> p (a d)")
                    pool.tensor_tensor(row, row, bv[:, :], ALU.add).then_inc(bv_added, 1)
                if on(i, 1):
                    pool.memset(sc[:, 1 - par, :], NEG / SCALE).then_inc(filled, 1)
                if on(i, -2):
                    pool.wait_ge(mv3, i - 1)
                    pool.tensor_tensor(rstd3s[:, par:par + 1], mv3s[:, par, 1:2], eps[:, :], ALU.add).then_inc(ve3, 1)
                    pool.wait_ge(ve3, i - 1)
                    pool.tensor_tensor(rstd3s[:, par:par + 1], rstd3s[:, par:par + 1], powers[:, 0:1], ALU.pow).then_inc(rstd3, 1)
            tiles(pool, step)

        @block.scalar
        def _(act):
            act.wait_ge(b_in, 48)
            for n, (src, hi, lo, bias) in enumerate(items):
                act.wait_ge(prep_ps, n + 1)
                if bias is None:
                    act.activation(hi, src, ACT.Copy).then_inc(prep_hi, 1)
                else:
                    act.activation(hi, src, ACT.Identity, bias=bias).then_inc(prep_hi, 1)

            def p_high(i, par, first, last):
                if on(i, -1):
                    for g in range(first, last):
                        a, b = GRP[g]
                        act.wait_ge(pt_ps, NGRP * (i - 1) + g + 1)
                        act.activation(p_hi[:, 1 - par, a:b, :], psP[g % 2][:, 0:(b - a) * P], ACT.Copy).then_inc(pthi_ready, 1)

            def step(i, n, par):
                if on(i, -1) and (not isinstance(i, int) or i >= 3):
                    act.wait_ge(pv_ps, i - 2)
                p_high(i, par, 0, 2)
                if on(i, -3):
                    act.wait_ge(x3_ps, i - 2)
                    act.activation(x3_hi[:, :, ds((i - 3) * P + KS - 1, P)], psA[:, 0:KE * P].rearrange("p (k n) -> p k n", k=KE),
                                   ACT.Copy).then_inc(x3hi_ready, 1)
                p_high(i, par, 2, NGRP)
                if on(i, 1):
                    act.wait_ge(xq_ps, i + 2)
                    act.activation(xqT[:, :, :], psA[:, 0:KE * P].rearrange("p (k n) -> p k n", k=KE), ACT.Copy).then_inc(xq_ready, 1)
                    act.wait_ge(q_ps, i + 2)
                    if not isinstance(i, int) or i >= 1:
                        act.wait_ge(scores_ps, 2 * i)
                    for m in range(KE):
                        act.activation(q_hi[:, 1 - par, m, :], psA[:, (KE + m) * P:(KE + m + 1) * P], ACT.Identity,
                                       bias=bq[:, m:m + 1]).then_inc(qhi_ready, 1)
                if on(i, -3):
                    act.activation(xn3[:, ds(i - 3, 1), :].rearrange("p a d -> p (a d)"), xn3s[:, 1 - par, :],
                                   ACT.Copy).then_inc(xn3_kept, 1)
                if on(i, 0):
                    act.wait_ge(nb_ready, i + 1)
                    if isinstance(i, int) and i < 2:
                        act.wait_ge(pad_zero, 2)
                    else:
                        act.wait_ge(pt_ps, NGRP * (i - 1))
                    if not isinstance(i, int) or i >= 2:
                        act.wait_ge(x2_ready, i - 1)
                    act.activation(pr[:, par, 0:SK], sc[:, par, :], ACT.Exp, bias=nb[:, par:par + 1], scale=SCALE,
                                   accum_out=rs[:, par:par + 1]).then_inc(exp_done, 1)
            tiles(act, step)

        @block.vector
        def _(dve):
            for t in range(NT):
                last = dve.bn_stats(stats[:, t, :], x_res[:, t, :])
            last.then_inc(dve_link, 1)
            dve.wait_ge(dve_link, 1)
            for t in range(NT):
                last = dve.bn_aggr(mv[:, t, :], stats[:, t, :])
            last.then_inc(mv2, 1)
            dve.wait_ge(rstd2, 1)
            dve.memset(x3_hi[:, :, 0:KS - 1].bitcast(U32), 0)
            dve.memset(x3_lo[:, :, 0:KS - 1].bitcast(U32), 0)
            done = 0
            for n, (src, hi, lo, bias) in enumerate(items):
                if lo is None:
                    continue
                dve.wait_ge(prep_hi, n + 1)
                if bias is None:
                    dve.tensor_tensor(lo, src, hi.bitcast(F32), ALU.subtract).then_inc(prep_lo, 1)
                else:
                    dve.scalar_tensor_tensor(lo, src, bias, hi.bitcast(F32), ALU.add, ALU.subtract).then_inc(prep_lo, 1)
                done += 1
            def p_low(i, par, first, last):
                if on(i, -1):
                    for g in range(first, last):
                        a, b = GRP[g]
                        dve.wait_ge(pthi_ready, NGRP * (i - 1) + g + 1)
                        dve.tensor_tensor(p_lo[:, 1 - par, a:b, :], psP[g % 2][:, 0:(b - a) * P],
                                          p_hi[:, 1 - par, a:b, :].bitcast(F32), ALU.subtract).then_inc(ptlo_ready, 1)

            def step(i, n, par):
                if on(i, -1) and (not isinstance(i, int) or i >= 3):
                    dve.wait_ge(pv_ps, i - 2)
                p_low(i, par, 0, 2)
                if on(i, -3):
                    dve.wait_ge(x3hi_ready, i - 2)
                    cols = ds((i - 3) * P + KS - 1, P)
                    dve.tensor_tensor(x3_lo[:, :, cols], psA[:, 0:KE * P].rearrange("p (k n) -> p k n", k=KE),
                                      x3_hi[:, :, cols].bitcast(F32), ALU.subtract).then_inc(x3lo_ready, 1)
                p_low(i, par, 2, NGRP)
                if on(i, -2):
                    row = x_res[:, ds(i - 2, 1), :].rearrange("p a d -> p (a d)")
                    dve.wait_ge(exp_done, i - 1)
                    dve.reciprocal(rinv[:, par:par + 1], rs[:, par:par + 1]).then_inc(x2_link, 1)
                    dve.wait_ge(x2_link, 3 * i - 5)
                    dve.wait_ge(pv_ps, i - 1)
                    dve.wait_ge(bv_added, i - 1)
                    dve.scalar_tensor_tensor(row, psO[:, 0:DM], rinv[:, par:par + 1], row, ALU.mult, ALU.add).then_inc(x2_ready, 1)
                    dve.wait_ge(x2_ready, i - 1)
                    plain(dve, spare, 3)
                    dve.bn_stats(stats3[:, par, :], row).then_inc(x2_link, 1)
                    dve.wait_ge(x2_link, 3 * i - 4)
                    plain(dve, spare, 4)
                    dve.bn_aggr(mv3s[:, par, :], stats3[:, par, :]).then_inc(mv3, 1)
                if on(i, 0):
                    dve.wait_ge(filled, i + 1)
                    dve.wait_ge(mask_in[par], 16 * (n + 1))
                    for s, (a, b) in enumerate(SPLIT):
                        dve.wait_ge(scores_ps, 2 * i + s + 1)
                        plain(dve, spare, 1 + s)
                        dve.copy_predicated(sc[:, par, a:b], mask_sb[:, par, a:b], psS[:, a:b]).then_inc(masked, 1)
                    dve.wait_ge(masked, 2 * i + 2)
                    dve.reduce_max(mx[:, par:par + 1], sc[:, par, :], AXX).then_inc(dve_link, 1)
                    dve.wait_ge(dve_link, i + 2)
                    dve.tensor_scalar(nb[:, par:par + 1], mx[:, par:par + 1], -SCALE, None, ALU.mult).then_inc(nb_ready, 1)
                if on(i, -2):
                    dve.wait_ge(mv3, i - 1)
                    dve.wait_ge(rstd3, i - 1)
                    if not isinstance(i, int) or i >= 4:
                        dve.wait_ge(x3_ps, i - 3)
                        dve.wait_ge(xn3_kept, i - 3)
                    dve.tensor_scalar(xn3s[:, par, :], x_res[:, ds(i - 2, 1), :].rearrange("p a d -> p (a d)"),
                                      mv3s[:, par, 0:1], rstd3s[:, par:par + 1],
                                      ALU.subtract, ALU.mult).then_inc(x2_link, 1)
                if on(i, 1):
                    dve.wait_ge(qhi_ready, KE * (i + 2))
                    for m in range(KE):
                        dve.scalar_tensor_tensor(q_lo[:, 1 - par, m, :], psA[:, (KE + m) * P:(KE + m + 1) * P], bq[:, m:m + 1],
                                                 q_hi[:, 1 - par, m, :].bitcast(F32), ALU.add, ALU.subtract).then_inc(qlo_ready, 1)
                if on(i, 2):
                    if not isinstance(i, int) or i >= 0:
                        dve.wait_ge(xq_ps, i + 1)
                    dve.tensor_scalar(xn2[:, par, :], x_res[:, ds(i + 2, 1), :].rearrange("p a d -> p (a d)"),
                                      mv[:, ds(i + 2, 1), 0:1].rearrange("p a d -> p (a d)"), rstd[:, ds(i + 2, 1)],
                                      ALU.subtract, ALU.mult).then_inc(xn2_ready, 1)
            x2_link = xn3_ready
            tiles(dve, step)

        @block.tensor
        def _(pe):
            def products(out, stat, mov, first, last):
                for n, (a, b) in enumerate(((0, 0), (0, 1), (1, 0))):
                    mm = pe.matmul(out, stat[a], mov[b], start=first and n == 0, stop=last and n == 2)
                return mm

            n = [0]

            bank_of = ([0, 1, 2] + [(3 + j) % 8 for j in range(len(ctx_items))]
                       + [(3 + j) % 8 for j in range(len(k_items))] + [(3 + j) % 8 for j in range(len(v_items))])

            def take():
                at = n[0]
                before = [i for i in range(at) if bank_of[i] == bank_of[at]]
                if before:
                    pe.wait_ge(prep_hi, before[-1] + 1)
                    if before[-1] > 0:
                        pe.wait_ge(prep_lo, before[-1])
                n[0] += 1
                return items[at][0]
            pe.wait_ge(w_in, 48)
            for m in range(3):
                out = take()
                for a in range(KE):
                    for k in range(KE):
                        last = pe.transpose(out[:, k, a * P:(a + 1) * P], w_raw[:, m, a, k * P:(k + 1) * P], ident[:, :])
                last.then_inc(prep_ps, 1)
            pe.wait_ge(c_in, 32)
            for k in range(KE):
                for a, b in GRP:
                    out = take()
                    for c in range(a, b):
                        last = pe.transpose(out[:, (c - a) * P:(c - a + 1) * P], c_raw[:, c, k * P:(k + 1) * P], ident[:, :])
                    last.then_inc(prep_ps, 1)
            pe.wait_ge(prep_lo, 2 + len(ctx_items))
            for m in range(KE):
                for a, b in KCOL:
                    out = take()
                    for k in range(KE):
                        last = products(out, (wk_hi[:, k, m * P:(m + 1) * P], wk_lo[:, k, m * P:(m + 1) * P]),
                                        (c_hi[:, k, a:b], c_lo[:, k, a:b]), k == 0, k == KE - 1)
                    last.then_inc(prep_ps, 1)
            for c in range(KC):
                out = take()
                for k in range(KE):
                    last = products(out, (c_hi[:, k, c * P:(c + 1) * P], c_lo[:, k, c * P:(c + 1) * P]),
                                    (wv_hi[:, k, :], wv_lo[:, k, :]), k == 0, k == KE - 1)
                last.then_inc(prep_ps, 1)
            pe.wait_ge(prep_hi, len(items))
            pe.wait_ge(prep_lo, len(items) - 1)

            def p_transposed(i, par, first, last_):
                if on(i, -1):
                    if first == 0:
                        pe.wait_ge(exp_done, i)
                    for g in range(first, last_):
                        a, b = GRP[g]
                        if not isinstance(i, int) or i > 1 or g > 1:
                            pe.wait_ge(ptlo_ready, NGRP * (i - 1) + g - 1)
                        for c in range(a, b):
                            last = pe.transpose(psP[g % 2][:, (c - a) * P:(c - a + 1) * P],
                                                pr[:, 1 - par, c * P:(c + 1) * P], ident[:, :])
                        last.then_inc(pt_ps, 1)

            def scores(i, par, first, last_):
                if on(i, 0):
                    if first == 0:
                        pe.wait_ge(qlo_ready, KE * (i + 1))
                    for s in range(first, last_):
                        a, b = SCOL[s]
                        if s % 2 == 0 and (not isinstance(i, int) or i >= 1):
                            pe.wait_ge(masked, 2 * (i - 1) + s // 2 + 1)
                        for k in range(KE):
                            last = products(psS[:, a:b], (q_hi[:, par, k, :], q_lo[:, par, k, :]),
                                            (k_hi[:, k, a:b], k_lo[:, k, a:b]), k == 0, k == KE - 1)
                        if s % 2 == 1:
                            last.then_inc(scores_ps, 1)

            def step(i, n, par):
                p_transposed(i, par, 0, 2)
                if on(i, -3):
                    pe.wait_ge(xn3_ready, 3 * (i - 2))
                    if on(i, 0):
                        pe.wait_ge(qlo_ready, KE * (i + 1))
                    if not isinstance(i, int) or i >= 4:
                        pe.wait_ge(x3lo_ready, i - 3)
                    for k in range(KE):
                        last = pe.transpose(psA[:, k * P:(k + 1) * P], xn3s[:, 1 - par, k * P:(k + 1) * P], ident[:, :])
                    last.then_inc(x3_ps, 1)
                scores(i, par, 0, 1)
                p_transposed(i, par, 2, NGRP)
                if on(i, 1):
                    if not isinstance(i, int) or i >= 3:
                        pe.wait_ge(x3lo_ready, i - 2)
                    if not isinstance(i, int) or i >= 0:
                        pe.wait_ge(qlo_ready, KE * (i + 1))
                    pe.wait_ge(xn2_ready, i + 2)
                    for k in range(KE):
                        last = pe.transpose(psA[:, k * P:(k + 1) * P], xn2[:, 1 - par, k * P:(k + 1) * P], ident[:, :])
                    last.then_inc(xq_ps, 1)
                scores(i, par, 1, NGRP)
                if on(i, 1):
                    pe.wait_ge(xq_ready, i + 2)
                    for m in range(KE):
                        for k in range(KE):
                            last = pe.matmul(psA[:, (KE + m) * P:(KE + m + 1) * P], wqT[:, k, m * P:(m + 1) * P], xqT[:, k, :],
                                             start=(k == 0), stop=(k == KE - 1))
                    last.then_inc(q_ps, 1)
                if on(i, -1):
                    if not isinstance(i, int) or i >= 2:
                        pe.wait_ge(x2_ready, i - 1)
                    for g, (a, b) in enumerate(GRP):
                        pe.wait_ge(ptlo_ready, NGRP * (i - 1) + g + 1)
                        for c in range(a, b):
                            last = products(psO[:, 0:DM], (p_hi[:, 1 - par, c, :], p_lo[:, 1 - par, c, :]),
                                            (v_hi[:, c, :], v_lo[:, c, :]), c == 0, c == KC - 1)
                    last.then_inc(pv_ps, 1)
            tiles(pe, step)



def expert_block(nc, w, x_res, xn3, x3_hi, x3_lo, ident, ps, out):
    WE = 2 * KE * FI + DM
    RING = 3
    ITEMS = NE
    with ExitStack() as ctx:
        def sb(name, shape, dt=F32, stack=ctx):
            return stack.enter_context(nc.sbuf_tensor(name, shape, dt))

        def sem(name):
            return ctx.enter_context(nc.semaphore(name))

        sg, t1 = sb("sg", [P, 2, BANK]), sb("t1", [P, 2, BANK])
        h_hi, h_lo = sb("h_hi", [P, 2, BANK], F32R), sb("h_lo", [P, 2, BANK], F32R)
        w_raw = sb("w_exp_raw", [P, RING, WE])
        w_hi, w_lo = sb("w_exp_hi", [P, NX, WE], F32R), sb("w_exp_lo", [P, NX, WE], F32R)
        cv_hi, cv_lo = sb("cv_hi", [P, KS, KE, FI], F32R), sb("cv_lo", [P, KS, KE, FI], F32R)
        sh_raw = sb("sh_raw", [P, KE * FI + DM])
        sh_hi, sh_lo = sb("sh_hi", [P, KE * FI + DM], F32R), sb("sh_lo", [P, KE * FI + DM], F32R)
        r_w, r_b = sb("r_w", [P, KE, NE]), sb("r_b", [P, NE])
        lg = sb("lg", [P, NT, NE])
        top, top_at = sb("top", [P, NT, 8]), sb("top_at", [P, NT, 8], U32)
        at_f, ids = sb("at_f", [P, NT, 2]), sb("ids", [P, NE])
        ex = sb("ex", [P, NT, NE])
        sm, pp, den = sb("sm", [P, NT]), sb("pp", [P, 2, NT]), sb("den", [P, NT])
        cmb, cmb_hi = sb("cmb", [P, NT, 2 * NE]), sb("cmb_hi", [P, NT, NE], F32R)
        cT = sb("cT", [2 * NE, SEQ], F32R)
        row = sb("row", [2 * NE, NE, P], F32R)
        oT = sb("oT", [P, KE, BANK])
        with ExitStack() as early:
            cv_raw = sb("cv_raw", [P, DM, KS], F32, early)
        o_sb = sb("o_sb", [P, 2, 2, DM])

        bank = [ps[:, n * BANK:(n + 1) * BANK] for n in range(8)]
        psG, psU, psC, psO = bank[0:2], bank[2:4], bank[4:6], bank[6:8]

        w_in = [sem(f"w_exp_in{i}") for i in range(RING)]
        sh_in, r_in, cv_in = sem("sh_in"), sem("r_in"), sem("cv_in")
        whi_ready, w_ready = sem("w_exp_hi_ready"), sem("w_exp_ready")
        sh_split, cv_ps, cv_split = sem("sh_split"), sem("cv_ps"), sem("cv_split")
        ids_made, row_made = sem("ids_made"), sem("row_made")
        lg_ps, lg_max, lg_exp, cmb_ready, cT_ps, cT_ready = (sem("lg_ps"), sem("lg_max"), sem("lg_exp"), sem("cmb_ready"),
                                                             sem("cT_ps"), sem("cT_ready"))
        route_link = sem("route_link")
        gate_ps, up_ps, c_ps, sg_ready, t1_ready, t2_ready = (sem("gate_ps"), sem("up_ps"), sem("c_ps"), sem("sg_ready"),
                                                              sem("t1_ready"), sem("t2_ready"))
        hhi_ready, h_ready, down_done = sem("hhi_ready"), sem("h_ready"), sem("down_done")
        oT_ready, oB_ps, o_ready = sem("oT_ready"), sem("oB_ps"), sem("o_ready")
        stored = [sem(f"stored{i}") for i in range(2)]

        block = ctx.enter_context(nc.Block())

        @block.sync
        def _(sp_):
            sp_.dma_start(r_w[:, :, :], w["router_w"].rearrange("(k p) n -> p k n", p=P)).then_inc(r_in, 16)
            sp_.dma_start(r_b[:, :], w["router_bias"].rearrange("(a n) -> a n", a=1).to_broadcast([P, NE])).then_inc(r_in, 16)

            def load(e, slot):
                dst = w_raw[:, slot, :]
                n = KE * FI
                sp_.dma_start(dst[:, 0:n].rearrange("p (k n) -> p k n", k=KE),
                              w["expert_gate_w"][ds(e, 1), :, :].rearrange("a (k p) n -> p (a k) n", p=P)).then_inc(w_in[slot], 16)
                sp_.dma_start(dst[:, n:2 * n].rearrange("p (k n) -> p k n", k=KE),
                              w["expert_up_w"][ds(e, 1), :, :].rearrange("a (k p) n -> p (a k) n", p=P)).then_inc(w_in[slot], 16)
                sp_.dma_start(dst[:, 2 * n:], w["expert_down_w"][ds(e, 1), :, :].rearrange("a p n -> p (a n)")).then_inc(w_in[slot], 16)
            for e in range(RING):
                load(e, e)
            n = KE * FI
            sp_.dma_start(sh_raw[:, 0:n].rearrange("p (k n) -> p k n", k=KE),
                          w["shared_up_w"].rearrange("(k p) n -> p k n", p=P)).then_inc(sh_in, 16)
            sp_.dma_start(sh_raw[:, n:], w["shared_down_w"]).then_inc(sh_in, 16)
            sp_.dma_start(cv_raw[:, :, :], w["conv_w"]).then_inc(cv_in, 16)
            with sp_.Fori(1, NX // RING) as E:
                for slot in range(RING):
                    sp_.wait_ge(w_ready, RING * E + slot - RING + 1)
                    load(RING * E + slot, slot)
            with sp_.Fori(0, NCH) as c:
                for t in range(2):
                    sp_.wait_ge(o_ready, 2 * c + t + 1)
                    sp_.dma_start(out[0, ds(c * BANK + t * 2 * P, 2 * P), :].rearrange("(n p) d -> p n d", p=P),
                                  o_sb[:, t, :, :]).then_inc(stored[t], 16)
            for t in range(2):
                sp_.wait_ge(stored[t], 16 * NCH)

        @block.gpsimd
        def _(pool):
            pool.iota(ids[:, :], pattern=[[1, NE]], base=0, channel_multiplier=0,
                      allow_small_or_imprecise_dtypes=True).then_inc(ids_made, 1)
            pool.memset(row[:, :, :].bitcast(F32), 0.0).then_inc(row_made, 1)
            for n in range(2):
                pool.wait_ge(row_made, n + 1)
                pool.affine_select(out=row[:, :, :], in_=row[:, :, :].bitcast(F32), compare_op=ALU.not_equal, fill=1.0, base=-NE * n,
                                   pattern=[[-1, NE], [0, P]], channel_multiplier=1).then_inc(row_made, 1)
            with pool.Fori(0, NX // RING) as E:
                for slot in range(RING):
                    e = RING * E + slot
                    pool.wait_ge(w_in[slot], 48 * (E + 1))
                    hi = w_hi[:, ds(e, 1), :].rearrange("p a n -> p (a n)")
                    lo = w_lo[:, ds(e, 1), :].rearrange("p a n -> p (a n)")
                    pool.wait_ge(whi_ready, e + 1)
                    pool.tensor_tensor(lo, w_raw[:, slot, :], hi.bitcast(F32), ALU.subtract).then_inc(w_ready, 1)

        @block.scalar
        def _(act):
            act.wait_ge(lg_max, 1)
            act.activation(ex[:, :, :], ex[:, :, :], ACT.Exp).then_inc(lg_exp, 1)
            act.activation(pp[:, 1, :], pp[:, 1, :], ACT.Exp).then_inc(lg_exp, 1)
            act.wait_ge(cT_ps, 1)
            act.activation(cT[:, :], ps[0:2 * NE, 4 * BANK:8 * BANK], ACT.Copy).then_inc(cT_ready, 1)
            def hi_part(c, e):
                i = c * ITEMS + e
                act.wait_ge(t2_ready, i + 1)
                if e >= 2:
                    act.wait_ge(down_done, i - 1)
                act.activation(h_hi[:, e % 2, :], t1[:, e % 2, :], ACT.Copy).then_inc(hhi_ready, 1)
            with act.Fori(0, NCH) as c:
                for e in range(ITEMS):
                    i = c * ITEMS + e
                    s = e % 2
                    act.wait_ge(gate_ps, i + 1)
                    if e >= 2:
                        act.wait_ge(t1_ready, i - 1)
                    act.activation(sg[:, s, :], psG[s], ACT.Silu).then_inc(sg_ready, 1)
                    hi_part(c, e)
                act.wait_ge(down_done, (c + 1) * ITEMS)
                act.activation(oT[:, :, :], ps[:, 6 * BANK:8 * BANK], ACT.Copy).then_inc(oT_ready, 1)

        @block.vector
        def _(dve):
            def routed_hi(e, slot, n):
                dve.wait_ge(w_in[slot], n)
                dve.tensor_copy(w_hi[:, ds(e, 1), :].rearrange("p a n -> p (a n)"), w_raw[:, slot, :]).then_inc(whi_ready, 1)
            for e in range(RING):
                routed_hi(e, e, 48)
            dve.wait_ge(lg_ps, 1)
            dve.wait_ge(r_in, 32)
            link, n = chain(dve, route_link, 0)
            link(dve.tensor_tensor(lg[:, :, :], bank[4][:, 0:NT * NE].rearrange("p (t e) -> p t e", t=NT),
                                   r_b[:, :].unsqueeze(1).to_broadcast([P, NT, NE]), ALU.add))
            for t in range(NT):
                last = dve.max(top[:, t, :], lg[:, t, :])
            link(last)
            dve.tensor_tensor(ex[:, :, :], lg[:, :, :], top[:, :, 0:1].to_broadcast([P, NT, NE]), ALU.subtract)
            dve.tensor_tensor(pp[:, 1, :], top[:, :, 1], top[:, :, 0], ALU.subtract).then_inc(lg_max, 1)
            for t in range(NT):
                last = dve.max_index(top_at[:, t, :], top[:, t, :], lg[:, t, :])
            link(last)
            link(dve.tensor_copy(at_f[:, :, :], top_at[:, :, 0:2]))
            dve.wait_ge(lg_exp, 2)
            link(dve.reduce_sum(sm[:, :], ex[:, :, :], AXX))
            link(dve.reciprocal(pp[:, 0, :], sm[:, :]))
            link(dve.tensor_tensor(pp[:, 1, :], pp[:, 1, :], pp[:, 0, :], ALU.mult))
            link(dve.scalar_tensor_tensor(den[:, :], pp[:, 0, :], 1e-6, pp[:, 1, :], ALU.add, ALU.add))
            link(dve.reciprocal(den[:, :], den[:, :]))
            link(dve.tensor_tensor(pp[:, :, :], pp[:, :, :], den[:, :].unsqueeze(1).to_broadcast([P, 2, NT]), ALU.mult))
            dve.wait_ge(ids_made, 1)
            idb = ids[:, :].unsqueeze(1).to_broadcast([P, NT, NE])
            for n2, dst in ((0, cmb[:, :, 0:NE]), (1, ex[:, :, :])):
                link(dve.tensor_tensor(dst, idb, at_f[:, :, n2:n2 + 1].to_broadcast([P, NT, NE]), ALU.is_equal))
                link(dve.tensor_tensor(dst, dst, pp[:, n2, :].unsqueeze(2).to_broadcast([P, NT, NE]), ALU.mult))
            link(dve.tensor_tensor(cmb[:, :, 0:NE], cmb[:, :, 0:NE], ex[:, :, :], ALU.add))
            for t in range(NT):
                dve.scalar_tensor_tensor(x_res[:, t, :], xn3[:, t, :], cmb[:, t, NX:NE], x_res[:, t, :], ALU.mult, ALU.add)
            link(dve.tensor_copy(cmb_hi[:, :, :], cmb[:, :, 0:NE]))
            link(dve.tensor_tensor(cmb[:, :, NE:], cmb[:, :, 0:NE], cmb_hi[:, :, :].bitcast(F32), ALU.subtract))
            dve.tensor_copy(cmb[:, :, 0:NE], cmb_hi[:, :, :].bitcast(F32)).then_inc(cmb_ready, 1)
            with dve.Fori(1, NX // RING) as E:
                for slot in range(RING):
                    routed_hi(RING * E + slot, slot, 48 * (E + 1))
            dve.wait_ge(sh_in, 32)
            dve.tensor_copy(sh_hi[:, :], sh_raw[:, :]).then_inc(sh_split, 1)
            dve.wait_ge(sh_split, 1)
            dve.tensor_tensor(sh_lo[:, :], sh_raw[:, :], sh_hi[:, :].bitcast(F32), ALU.subtract).then_inc(sh_split, 1)
            for k in range(KE):
                src = bank[2 + k][:, 0:KS * P].rearrange("p (t n) -> p t n", t=KS)
                dve.wait_ge(cv_ps, k + 1)
                dve.tensor_copy(cv_hi[:, :, k, :], src).then_inc(cv_split, 1)
                dve.wait_ge(cv_split, 2 * k + 1)
                dve.tensor_tensor(cv_lo[:, :, k, :], src, cv_hi[:, :, k, :].bitcast(F32), ALU.subtract).then_inc(cv_split, 1)
            with dve.Fori(0, NCH) as c:
                for e in range(ITEMS):
                    i = c * ITEMS + e
                    s = e % 2
                    dve.wait_ge(up_ps, i + 1)
                    dve.wait_ge(sg_ready, i + 1)
                    dve.tensor_tensor(t1[:, s, :], sg[:, s, :], psU[s], ALU.mult).then_inc(t1_ready, 1)
                    dve.wait_ge(t1_ready, i + 1)
                    if e < NX:
                        dve.wait_ge(c_ps, c * NX + e + 1)
                        dve.tensor_tensor(t1[:, s, :], t1[:, s, :], psC[s], ALU.mult).then_inc(t2_ready, 1)
                    else:
                        dve.sem_inc(t2_ready, 1)
                    dve.wait_ge(hhi_ready, i + 1)
                    dve.tensor_tensor(h_lo[:, s, :], t1[:, s, :], h_hi[:, s, :].bitcast(F32), ALU.subtract).then_inc(h_ready, 1)
                for t in range(2):
                    dve.wait_ge(oB_ps, 2 * c + t + 1)
                    dve.tensor_tensor(o_sb[:, t, :, :], psC[t].rearrange("p (n d) -> p n d", n=2),
                                      x_res[:, ds(CHT * c + 2 * t, 2), :], ALU.add).then_inc(o_ready, 1)
                for t in range(2):
                    dve.wait_ge(stored[t], 16 * (c + 1))

        @block.tensor
        def _(pe):
            def products(out, pairs, first, last):
                todo = [(st[a], mv_[b]) for st, mv_ in pairs for a, b in ((0, 0), (0, 1), (1, 0))]
                for n, (a, b) in enumerate(todo):
                    mm = pe.matmul(out, a, b, start=first and n == 0, stop=last and n == len(todo) - 1)
                return mm
            x3 = (x3_hi, x3_lo)
            pe.wait_ge(r_in, 32)
            for t in range(NT):
                cols = slice(KS - 1 + t * P, KS - 1 + (t + 1) * P)
                for n, (k, part) in enumerate([(k, part) for k in range(KE) for part in x3]):
                    last = pe.matmul(bank[4][:, t * NE:(t + 1) * NE], part[:, k, cols].bitcast(F32), r_w[:, k, :],
                                     start=(n == 0), stop=(n == 2 * KE - 1))
            last.then_inc(lg_ps, 1)
            pe.wait_ge(cv_in, 16)
            for k in range(KE):
                for tap in range(KS):
                    last = pe.transpose(bank[2 + k][:, tap * P:(tap + 1) * P], cv_raw[:, k * P:(k + 1) * P, tap], ident[:, :])
                last.then_inc(cv_ps, 1)
            pe.wait_ge(cmb_ready, 1)
            for t in range(NT):
                last = pe.transpose(ps[0:2 * NE, 4 * BANK + t * P:4 * BANK + (t + 1) * P], cmb[:, t, :], ident[:, :])
            last.then_inc(cT_ps, 1)
            pe.wait_ge(cT_ready, 1)
            pe.wait_ge(row_made, 3)
            pe.wait_ge(cv_split, 4)
            pe.wait_ge(sh_split, 2)
            with pe.Fori(0, NCH) as c:
                def cols(shift=KS - 1):
                    return ds(c * BANK + shift, BANK)

                def down(e):
                    i = c * ITEMS + e
                    pe.wait_ge(h_ready, i + 1)
                    for m in range(KE):
                        sl = slice(2 * KE * FI + m * P, 2 * KE * FI + (m + 1) * P)
                        wd = ((w_hi[:, e, sl], w_lo[:, e, sl]) if e < NX else
                              (sh_hi[:, KE * FI + m * P:KE * FI + (m + 1) * P], sh_lo[:, KE * FI + m * P:KE * FI + (m + 1) * P]))
                        last = products(psO[m], [(wd, (h_hi[:, e % 2, :], h_lo[:, e % 2, :]))], e == 0, e == ITEMS - 1)
                    last.then_inc(down_done, 1)
                for e in range(ITEMS):
                    i = c * ITEMS + e
                    s = e % 2
                    mov = [(x3_hi[:, k, cols()], x3_lo[:, k, cols()]) for k in range(KE)]
                    if e < NX:
                        pe.wait_ge(w_ready, e + 1)
                        gate, up = ([(tuple(x[:, e, (o + k) * FI:(o + k + 1) * FI] for x in (w_hi, w_lo)), mov[k])
                                     for k in range(KE)] for o in (0, KE))
                    else:
                        gate = [(tuple(x[:, tap, k, :] for x in (cv_hi, cv_lo)), (x3_hi[:, k, cols(tap)], x3_lo[:, k, cols(tap)]))
                                for tap in range(KS) for k in range(KE)]
                        up = [(tuple(x[:, k * FI:(k + 1) * FI] for x in (sh_hi, sh_lo)), mov[k]) for k in range(KE)]
                    if e >= 2:
                        pe.wait_ge(sg_ready, i - 1)
                    products(psG[s], gate, True, True).then_inc(gate_ps, 1)
                    if e >= 2:
                        pe.wait_ge(t2_ready, i - 1)
                    if e == 1:
                        pe.wait_ge(t1_ready, i)
                    products(psU[s], up, True, True).then_inc(up_ps, 1)
                    for n in ((), (0, 1), *((n,) for n in range(2, NX)), ())[e]:
                        pe.matmul(psC[n % 2], row[:, n, :], cT[:, ds(c * BANK, BANK)], start=True, stop=True).then_inc(c_ps, 1)
                    if e >= 1:
                        down(e - 1)
                down(ITEMS - 1)
                pe.wait_ge(oT_ready, c + 1)
                pe.wait_ge(t2_ready, c * ITEMS + ITEMS)
                for t in range(2):
                    for r in range(2):
                        for k in range(KE):
                            last = pe.transpose(psC[t][:, r * DM + k * P:r * DM + (k + 1) * P],
                                                oT[:, k, (2 * t + r) * P:(2 * t + r + 1) * P], ident[:, :])
                    last.then_inc(oB_ps, 1)


def decoder_layer(nc, ins, out):
    with ExitStack() as keep:
        x_res = keep.enter_context(nc.sbuf_tensor("x_res", [P, NT, DM], F32))
        ident = keep.enter_context(nc.sbuf_tensor("ident", [P, P], F32))
        power = keep.enter_context(nc.sbuf_tensor("power", [P, CHT], F32))
        spare = keep.enter_context(nc.sbuf_tensor("spare", [P, 5], F32))
        ps = keep.enter_context(nc.psum_tensor("ps", [P, 8 * BANK], F32))

        def part(prefix):
            return {k[len(prefix):]: v for k, v in ins.items() if k.startswith(prefix)}
        scan_block(nc, ins["x"], part("L0_attn_"), x_res, ident, power, spare, ps)
        x3_hi = keep.enter_context(nc.sbuf_tensor("x3_hi", [P, KE, KS - 1 + SEQ], F32R))
        x3_lo = keep.enter_context(nc.sbuf_tensor("x3_lo", [P, KE, KS - 1 + SEQ], F32R))
        with nc.sbuf_tensor("xn3", [P, NT, DM], F32) as xn3:
            attention_block(nc, ins["ctx_1024"], ins["mask_BxSxS2_ik1"], part("L0_xattn_"), x_res, xn3, x3_hi, x3_lo,
                            ident, spare, ps)
        expert_block(nc, part("L0_ffn_"), x_res, xn3, x3_hi, x3_lo, ident, ps, out)


def kernel(**inputs):
    import numpy as _np
    import concourse.bacc as _bacc
    from concourse import mybir as _mybir
    from concourse.bass_utils import run_bass_kernel_spmd as _run

    nc = _bacc.Bacc("TRN2", target_bir_lowering=False, num_devices=1)
    arrays, ins = {}, {}
    for name, value in inputs.items():
        a = _np.ascontiguousarray(value)
        arrays[f"in_{name}_dram"] = a
        ins[name] = nc.dram_tensor(f"in_{name}_dram", a.shape, _mybir.dt.from_np(a.dtype), kind="ExternalInput").ap()
    out = nc.dram_tensor("out_0_dram", (1, SEQ, DM), F32, kind="ExternalOutput").ap()
    decoder_layer(nc, ins, out)
    r = _run(nc, [arrays], core_ids=[0])
    return r.results[0]["out_0_dram"]
```

```python
import concourse.bass as bass
from concourse import mybir
from contextlib import ExitStack

F32 = mybir.dt.float32
F32R = mybir.dt.float32r
I32 = mybir.dt.int32
U32 = mybir.dt.uint32
ALU = mybir.AluOpType
ACT = mybir.ActivationFunctionType
AXX = mybir.AxisListType.X
ds = bass.ds

P = 128
BANK = 512
SEQ = 2048
DM = 256
KE = DM // P
NT = SEQ // P
EPS = 1e-5

DI = 512
KM = DI // P
NS = 16
NTAP = 4
CH = BANK
CHT = CH // P
NQ = SEQ // CH
QC = P // 32
NG = NS // QC
TILES = KM * NG * QC
STEPS = KM * NG

NPU, NDA, NU, NH = 6, 8, 4, 3
PE_XNT, PE_X, PE_PROJ, PE_Z = 3, (8, 10, 12, 14), (14, 18, 22, 24), (24, 25, 27, 29)
PE_XS, PE_BT, PE_V, PE_UT = (37, 38, 39, 40), 43, (44, 45, 47, 48), (55, 59, 60, 61)
ACT_HI, ACT_X, ACT_Z, ACT_SILU, ACT_XS = 4, (14, 16, 18, 20), (32, 34, 36, 38), 38, 43
ACT_BT, ACT_V, ACT_SP, ACT_UT = 48, (49, 50, 51, 52), 53, (60, 61, 62, 63)
DVE_LO, DVE_CONV, DVE_RES, DVE_DT = 4, (9, 11, 13, 15), (17, 19, 21, 23), 53
DVE_MOM, DVE_XN, POOL_RSTD = 49, 58, 62

SK = 1601
KC = (SK + P - 1) // P
SKP = KC * P
SKE = SK + SK % 2
NEG = -1.0e10
SCALE = 1.0 / 16.0

NE = 16
NX = NE - 1
FI = 128
KS = 3
NCH = SEQ // BANK


def plain(dve, spare, n):
    dve.memset(spare[:, n:n + 1], 0.0)


def chain(eng, sem, base):
    n = [0]

    def link(ins):
        n[0] += 1
        ins.then_inc(sem, 1)
        eng.wait_ge(sem, base + n[0])
    return link, n


def scan_block(nc, x, w, x_res, ident, power, spare, ps):
    with ExitStack() as ctx:
        def sb(name, shape, dt=F32, stack=ctx):
            return stack.enter_context(nc.sbuf_tensor(name, shape, dt))

        def sem(name):
            return ctx.enter_context(nc.semaphore(name))

        w_in_hi = sb("w_in_hi", [P, KE, 2 * DI], F32R)
        w_in_lo = sb("w_in_lo", [P, KE, 2 * DI], F32R)
        w_x = sb("w_x", [P, KM, 2 * NS])
        w_dt = sb("w_dt", [33, DI])
        w_out = sb("w_out", [P, KM, DM])
        conv_w = sb("conv_w", [P, KM, NTAP])
        conv_b = sb("conv_b", [P, KM])
        d_skip = sb("d_skip", [P, KM])
        a_log = sb("a_log", [P, DI // 32, NS])
        neg_a = sb("neg_a", [P, TILES])
        pick = sb("pick", [P, 32])
        eps = sb("eps", [P, CHT])
        zs = sb("zs", [P, 2, KM, CH])
        xc = sb("xc", [P, 2, KM, CH])
        dt = sb("dt", [P, 2, KM, CH])
        ut = sb("ut", [P, 2, CHT, DI])
        bt = sb("bt", [P, 2, CHT, NS])
        hlast = sb("hlast", [P, TILES])
        xs = sb("xs", [33, CH])
        dt_rep = sb("dt_rep", [P, 2, QC, CH])
        xn = sb("xn", [P, CHT, DM])
        stats = sb("stats", [P, CHT, 6])
        mv = sb("mv", [P, CHT, 2])
        rstd = sb("rstd", [P, CHT])
        xnT_hi = sb("xnT_hi", [P, KE, CH], F32R)
        xnT_lo = sb("xnT_lo", [P, KE, CH], F32R)
        xp = sb("xp", [P, KM, NTAP - 1 + CH])
        sp = sb("sp", [P, KM, CH])
        u = sp
        pu = sb("pu", [P, NPU, CHT, P])
        da = sb("da", [P, NDA, CH])
        with ExitStack() as early:
            w_raw = sb("w_raw", [P, KE, 2 * DI], F32, early)
        with ExitStack() as late:
            h = sb("h", [P, NH * QC, CH], F32, late)
        psF = ps[:, 0:2 * BANK].rearrange("p (s n) -> p s n", s=2)
        psY = ps[:, 2 * BANK:4 * BANK].rearrange("p (s n) -> p s n", s=2)
        psU = ps[:, 4 * BANK:8 * BANK].rearrange("p (s n) -> p s n", s=NU)

        x_in, x_rest, s_win, s_small, s_zero, s_alog = sem("x_in"), sem("x_rest"), sem("w_in_in"), sem("small_in"), sem("zeroed"), sem("alog_in")
        ident_made, ident_ok = sem("ident_made"), sem("ident_ok")
        hi_split, w_ready, a_exp, consts_ready = sem("w_in_hi_split"), sem("w_in_split"), sem("a_exp"), sem("consts_ready")
        dve_link, act_link = sem("dve_link"), sem("act_link")
        mv_ready, var_eps, rstd_ready = sem("mv_ready"), sem("var_eps"), sem("rstd_ready")
        xn_ready, xnT_ps, hi_ready, lo_ready = sem("xn_ready"), sem("xnT_ps"), sem("xnT_hi_ready"), sem("xnT_lo_ready")
        x_ps, x_evac, z_ps, z_evac = sem("x_ps"), sem("x_evac"), sem("z_ps"), sem("z_evac")
        conv_done, xc_ready, zs_ready = sem("conv_done"), sem("xc_ready"), sem("zs_ready")
        xs_ps, xs_ready, bt_ps, bt_ready = sem("xs_ps"), sem("xs_ready"), sem("bt_ps"), sem("bt_ready")
        v_ps, v_evac, sp_ready, dt_ready, u_ready = sem("v_ps"), sem("v_evac"), sem("sp_ready"), sem("dt_ready"), sem("u_ready")
        uT_ps, ut_ready = sem("uT_ps"), sem("ut_ready")
        rep_in = [sem(f"dt_rep_in{i}") for i in range(2)]
        pu_ready, transposed, exp_ready, scanned = sem("pu_ready"), sem("transposed"), sem("exp_ready"), sem("scanned")
        saved, summed, gated = sem("saved"), sem("summed"), sem("gated")
        proj_ps, x1_done = sem("proj_ps"), sem("x1_done")

        block = ctx.enter_context(nc.Block())

        @block.sync
        def _(sp_):
            xv = x[0].rearrange("(n p) d -> p n d", p=P)
            sp_.dma_start(x_res[:, 0:CHT, :], xv[:, 0:CHT, :]).then_inc(x_in, 16)
            sp_.dma_start(w_raw[:, :, :], w["W_in"].rearrange("(k p) n -> p k n", p=P)).then_inc(s_win, 16)
            sp_.dma_start(conv_w[:, :, :], w["conv_w"].rearrange("(m p) k -> p m k", p=P)).then_inc(s_small, 16)
            sp_.dma_start(conv_b[:, :], w["conv_b"].rearrange("(m p) -> p m", p=P), allow_slow_non_contiguous=True).then_inc(s_small, 16)
            sp_.dma_start(d_skip[:, :], w["D"].rearrange("(m p) -> p m", p=P), allow_slow_non_contiguous=True).then_inc(s_small, 16)
            sp_.dma_start(w_x[:, :, :], w["W_x"].rearrange("(m p) n -> p m n", p=P)).then_inc(s_small, 16)
            sp_.wait_ge(s_zero, 1)
            sp_.dma_start(w_dt[0:NS, :], w["W_dt"]).then_inc(s_small, 16)
            sp_.dma_start(w_dt[32:33, :], w["b_dt"].rearrange("(a n) -> a n", a=1)).then_inc(s_small, 16)
            for q in range(QC):
                sp_.dma_start(a_log[32 * q:32 * q + 32, :, :],
                              w["A_log"].rearrange("(b p) n -> p b n", p=32)).then_inc(s_alog, 16)
            sp_.dma_start(x_res[:, CHT:, :], xv[:, CHT:, :]).then_inc(x_rest, 16)
            sp_.dma_start(w_out[:, :, :], w["W_out"].rearrange("(m p) n -> p m n", p=P)).then_inc(s_small, 16)
            for q in range(NQ):
                for B in range(KM):
                    sp_.wait_ge(dt_ready, KM * q + B + 1)
                    if q * KM + B >= 2:
                        sp_.wait_ge(exp_ready, TILES * q + 16 * (B - 1))
                    for j in range(QC):
                        for r in range(QC):
                            sp_.dma_start(dt_rep[32 * r:32 * r + 32, B % 2, j, :],
                                          dt[32 * j:32 * j + 32, q % 2, B, :]).then_inc(rep_in[B % 2], 16)

        @block.gpsimd
        def _(pool):
            pool.memset(w_dt[:, :], 0.0).then_inc(s_zero, 1)
            pool.memset(power[:, :], -0.5)
            pool.memset(eps[:, :], EPS)
            pool.memset(ident[:, :], 0.0).then_inc(ident_made, 1)
            pool.wait_ge(ident_made, 1)
            pool.affine_select(out=ident[:, :], in_=ident[:, :], compare_op=ALU.not_equal, fill=1.0, base=0,
                               pattern=[[-1, P]], channel_multiplier=1).then_inc(ident_ok, 1)

            def inverse_deviation(q):
                pool.wait_ge(mv_ready, q + 1)
                pool.wait_ge(xn_ready, q)
                pool.tensor_tensor(rstd[:, :], mv[:, :, 1], eps[:, :], ALU.add).then_inc(var_eps, 1)
                pool.wait_ge(var_eps, q + 1)
                pool.tensor_tensor(rstd[:, :], rstd[:, :], power[:, 0:CHT], ALU.pow).then_inc(rstd_ready, 1)

            inverse_deviation(0)
            inverse_deviation(1)
            for q in range(NQ):
                pool.wait_ge(bt_ready, q + 1)
                for k in range(TILES):
                    g, t = QC * (k // QC % NG), TILES * q + k
                    b = k // 16 * QC + k % QC
                    if k % 16 == 0:
                        pool.wait_ge(ut_ready, KM * q + k // 16 + 1)
                    if t >= NPU:
                        pool.wait_ge(transposed, t - NPU + 1)
                    pool.tensor_tensor(
                        pu[:, t % NPU, :, :].rearrange("p t (n d) -> p t n d", n=QC),
                        ut[:, q % 2, :, 32 * b:32 * b + 32].unsqueeze(2).to_broadcast([P, CHT, QC, 32]),
                        bt[:, q % 2, :, g:g + QC].unsqueeze(3).to_broadcast([P, CHT, QC, 32]),
                        ALU.mult).then_inc(pu_ready, 1)
                    if k == POOL_RSTD and q + 2 < NQ:
                        inverse_deviation(q + 2)

        @block.scalar
        def _(act):
            link, _n = chain(act, act_link, 0)
            act.wait_ge(s_alog, 16 * QC)
            act.activation(a_log[:, :, :], a_log[:, :, :], ACT.Exp).then_inc(a_exp, 1)

            def front(q, k):
                if k == ACT_HI:
                    act.wait_ge(xnT_ps, q + 1)
                    act.wait_ge(z_ps, KM * q)
                    act.activation(xnT_hi[:, :, :], psF, ACT.Copy).then_inc(hi_ready, 1)
                    act.wait_ge(conv_done, KM * q)
                    if q:
                        link(act.activation(xp[:, :, 0:NTAP - 1], xp[:, :, CH:], ACT.Copy))
                if k in ACT_X:
                    m = ACT_X.index(k)
                    act.wait_ge(x_ps, KM * q + m + 1)
                    act.activation(xp[:, m, NTAP - 1:], psF[:, m % 2, :], ACT.Copy).then_inc(x_evac, 1)
                if k in ACT_Z:
                    m = ACT_Z.index(k)
                    if q >= 2:
                        act.wait_ge(proj_ps, CHT * (q - 1))
                    act.wait_ge(z_ps, KM * q + m + 1)
                    act.activation(zs[:, q % 2, m, :], psF[:, m % 2, :], ACT.Copy).then_inc(z_evac, 1)
                if k == ACT_SILU and q == 0:
                    for m in range(KM):
                        act.wait_ge(conv_done, m + 1)
                        act.activation(xc[:, 0, m, :], xc[:, 0, m, :], ACT.Silu).then_inc(xc_ready, 1)
                elif k == ACT_SILU:
                    act.wait_ge(conv_done, KM * (q + 1))
                    act.activation(xc[:, q % 2, :, :], xc[:, q % 2, :, :], ACT.Silu).then_inc(xc_ready, KM)
                if k == ACT_SILU:
                    act.wait_ge(z_evac, KM * (q + 1))
                    act.activation(zs[:, q % 2, :, :], zs[:, q % 2, :, :], ACT.Silu).then_inc(zs_ready, 1)
                if k == ACT_XS:
                    act.wait_ge(xs_ps, q + 1)
                    act.wait_ge(v_ps, KM * q)
                    act.activation(xs[0:32, :], psF[0:32, 0, :], ACT.Copy).then_inc(xs_ready, 1)
                if k == ACT_BT:
                    act.wait_ge(bt_ps, q + 1)
                    if q >= 2:
                        act.wait_ge(pu_ready, TILES * (q - 1))
                    act.activation(bt[:, q % 2, :, :],
                                   psF[:, 1, 0:CHT * 32].rearrange("p (t n) -> p t n", t=CHT)[:, :, NS:2 * NS],
                                   ACT.Copy).then_inc(bt_ready, 1)
                if k in ACT_V:
                    m = ACT_V.index(k)
                    act.wait_ge(v_ps, KM * q + m + 1)
                    act.wait_ge(u_ready, KM * max(q - 1, 0))
                    act.activation(dt[:, q % 2, m, :], psF[:, m % 2, :], ACT.Copy).then_inc(v_evac, 1)
                if k == ACT_SP:
                    act.wait_ge(v_evac, KM * (q + 1))
                    act.wait_ge(uT_ps, KM * q)
                    link(act.activation(sp[:, :, :], dt[:, q % 2, :, :], ACT.Abs))
                    link(act.activation(sp[:, :, :], sp[:, :, :], ACT.Exp, scale=-1.0))
                    for m in range(KM):
                        act.activation(sp[:, m, :], sp[:, m, :], ACT.Ln, bias=1.0).then_inc(sp_ready, 1)
                if k in ACT_UT:
                    m = ACT_UT.index(k)
                    act.wait_ge(uT_ps, KM * q + m + 1)
                    act.activation(ut[:, q % 2, :, m * P:(m + 1) * P],
                                   psF[:, m % 2, :].rearrange("p (t d) -> p t d", t=CHT), ACT.Copy).then_inc(ut_ready, 1)

            for k in range(TILES):
                front(0, k)
            act.wait_ge(consts_ready, 1)
            for q in range(NQ):
                for k in range(TILES):
                    B, j, t = k // 16, k % QC, TILES * q + k
                    if k % 16 == 0:
                        act.wait_ge(rep_in[B % 2], (2 * q + B // 2 + 1) * 16 * QC * QC)
                    if t >= NDA:
                        act.wait_ge(scanned, t - NDA + 1)
                    act.activation(da[:, t % NDA, :], dt_rep[:, B % 2, j, :], ACT.Exp,
                                   scale=neg_a[:, k:k + 1]).then_inc(exp_ready, 1)
                    if q + 1 < NQ:
                        front(q + 1, k)

        @block.vector
        def _(dve):
            link, _n = chain(dve, dve_link, 0)

            def moments(q):
                dve.wait_ge(x_in if q == 0 else x_rest, 16)
                for t in range(CHT):
                    last = dve.bn_stats(stats[:, t, :], x_res[:, q * CHT + t, :])
                link(last)
                for t in range(CHT):
                    last = dve.bn_aggr(mv[:, t, :], stats[:, t, :])
                last.then_inc(mv_ready, 1)

            def normalize(q):
                dve.wait_ge(rstd_ready, q + 1)
                dve.wait_ge(xnT_ps, q)
                for t in range(CHT):
                    last = dve.tensor_scalar(xn[:, t, :], x_res[:, q * CHT + t, :],
                                             mv[:, t, 0:1], rstd[:, t:t + 1], ALU.subtract, ALU.mult)
                last.then_inc(xn_ready, 1)

            def residual(t):
                row = x_res[:, t, :]
                dve.wait_ge(proj_ps, t + 1)
                dve.tensor_tensor(row, psF[:, t % 2, 0:DM], row, ALU.add).then_inc(x1_done, 1)

            def front(q, k):
                if k in DVE_RES and q >= 2:
                    residual(CHT * (q - 2) + DVE_RES.index(k))
                if q == NQ:
                    return
                if k == DVE_LO:
                    dve.wait_ge(hi_ready, q + 1)
                    dve.tensor_tensor(xnT_lo[:, :, :], psF, xnT_hi[:, :, :].bitcast(F32),
                                      ALU.subtract).then_inc(lo_ready, 1)
                if k in DVE_CONV:
                    m = DVE_CONV.index(k)
                    acc = xc[:, q % 2, m, :]
                    dve.wait_ge(x_evac, KM * q + m + 1)
                    if q >= 2:
                        dve.wait_ge(gated, KM * (q - 1))
                    link(dve.tensor_scalar(acc, xp[:, m, 0:CH], conv_w[:, m, 0:1], conv_b[:, m:m + 1],
                                           ALU.mult, ALU.add))
                    for n in range(1, NTAP):
                        last = dve.scalar_tensor_tensor(acc, xp[:, m, n:n + CH], conv_w[:, m, n:n + 1], acc,
                                                        ALU.mult, ALU.add)
                        if n < NTAP - 1:
                            link(last)
                    last.then_inc(conv_done, 1)
                if k == DVE_DT:
                    for m in range(KM):
                        d = dt[:, q % 2, m, :]
                        dve.wait_ge(sp_ready, KM * q + m + 1)
                        dve.scalar_tensor_tensor(d, d, 0.0, sp[:, m, :], ALU.max, ALU.add).then_inc(dt_ready, 1)
                        dve.wait_ge(dt_ready, KM * q + m + 1)
                        dve.tensor_tensor(u[:, m, :], d, xc[:, q % 2, m, :], ALU.mult).then_inc(u_ready, 1)
                if k == DVE_MOM and q + 1 < NQ:
                    moments(q + 1)
                if k == DVE_XN and q + 1 < NQ:
                    normalize(q + 1)

            def gate(B):
                q, m = B // KM, B % KM
                dve.wait_ge(summed, NG * (B + 1))
                link(dve.scalar_tensor_tensor(xc[:, q % 2, m, :], xc[:, q % 2, m, :], d_skip[:, m:m + 1],
                                              psY[:, B % 2, :], ALU.mult, ALU.add))
                dve.tensor_tensor(zs[:, q % 2, m, :], xc[:, q % 2, m, :], zs[:, q % 2, m, :], ALU.mult).then_inc(gated, 1)

            dve.memset(xp[:, :, 0:NTAP - 1], 0.0)
            dve.memset(hlast[:, :], 0.0)
            dve.memset(xs[32:33, :], 1.0)
            moments(0)
            dve.wait_ge(s_win, 16)
            dve.tensor_copy(w_in_hi[:, :, :], w_raw[:, :, :]).then_inc(hi_split, 1)
            normalize(0)
            dve.wait_ge(hi_split, 1)
            dve.tensor_tensor(w_in_lo[:, :, :], w_raw[:, :, :], w_in_hi[:, :, :].bitcast(F32),
                              ALU.subtract).then_inc(w_ready, 1)
            dve.wait_ge(ident_ok, 1)
            for r in range(QC):
                dve.tensor_copy(pick[32 * r:32 * r + 32, :], ident[32 * r:32 * r + 32, 32 * r:32 * r + 32])
            dve.wait_ge(a_exp, 1)
            for r in range(QC):
                rows = slice(32 * r, 32 * r + 32)
                dst = neg_a[rows, :].rearrange("p (b g j) -> p b g j", b=KM, g=NG)
                src = a_log[rows, :, :].rearrange("p (b j) (g n) -> p n b g j", b=KM, n=QC)[:, r]
                last = dve.tensor_scalar(dst, src, -1.0, None, ALU.mult)
            last.then_inc(consts_ready, 1)
            dve.wait_ge(s_small, 16 * 7)
            for k in range(TILES):
                front(0, k)
            for q in range(NQ):
                for k in range(TILES):
                    s, j, t = STEPS * q + k // QC, k % QC, TILES * q + k
                    if j == 0 and s >= NH:
                        dve.wait_ge(summed, s - NH + 1)
                        if s - NH < STEPS * (NQ - 1):
                            dve.wait_ge(saved, s - NH + 1)
                    dve.wait_ge(transposed, t + 1)
                    dve.wait_ge(exp_ready, t + 1)
                    dve.tensor_tensor_scan(h[:, QC * (s % NH) + j, :], da[:, t % NDA, :], psU[:, t % NU, :],
                                           hlast[:, k:k + 1], ALU.mult, ALU.add).then_inc(scanned, 1)
                    if j == 2 and 1 <= s <= STEPS * (NQ - 1):
                        e = s - 1
                        dve.wait_ge(scanned, QC * s)
                        dve.tensor_copy(hlast[:, QC * (e % STEPS):QC * (e % STEPS) + QC],
                                        h[:, QC * (e % NH):QC * (e % NH) + QC, CH - 1]).then_inc(saved, 1)
                    if k % 16 == 2 and t > 16:
                        gate(t // 16 - 1)
                    front(q + 1, k)
            gate(KM * NQ - 1)
            for t in range(CHT):
                residual(CHT * (NQ - 1) + t)

        @block.tensor
        def _(pe):
            def project(q, t):
                pe.wait_ge(gated, KM * (q + 1))
                for m in range(KM):
                    last = pe.matmul(psF[:, t % 2, 0:DM], zs[:, q % 2, m, t * P:(t + 1) * P], w_out[:, m, :],
                                     start=(m == 0), stop=(m == KM - 1))
                last.then_inc(proj_ps, 1)

            def w_in_product(q, m):
                i = 0
                for n in range(KE):
                    for a, b in ((w_in_hi, xnT_hi), (w_in_hi, xnT_lo), (w_in_lo, xnT_hi)):
                        last = pe.matmul(psF[:, m % 2, :], a[:, n, m * P:(m + 1) * P], b[:, n, :],
                                         start=(i == 0), stop=(i == 3 * KE - 1))
                        i += 1
                return last

            def front(q, k):
                if k in PE_PROJ and q >= 2:
                    t = PE_PROJ.index(k)
                    if q == NQ:
                        pe.wait_ge(ut_ready, KM * NQ)
                    elif t < 2:
                        pe.wait_ge(x_evac, KM * q + 3 + t)
                    if t >= 2:
                        pe.wait_ge(x1_done, CHT * (q - 2) + t - 1)
                    project(q - 2, t)
                if q == NQ:
                    return
                if k == PE_XNT:
                    pe.wait_ge(xn_ready, q + 1)
                    pe.wait_ge(ut_ready, KM * q)
                    for t in range(CHT):
                        for n in range(KE):
                            last = pe.transpose(psF[:, n, t * P:(t + 1) * P], xn[:, t, n * P:(n + 1) * P], ident[:, :])
                    last.then_inc(xnT_ps, 1)
                if k in PE_X:
                    m = PE_X.index(k)
                    pe.wait_ge(lo_ready, q + 1)
                    if m >= 2:
                        pe.wait_ge(x_evac, KM * q + m - 1)
                    w_in_product(q, m).then_inc(x_ps, 1)
                if k in PE_Z:
                    m = PE_Z.index(k)
                    if m < 2:
                        pe.wait_ge(x_evac, KM * q + 3 + m)
                        if q >= 2:
                            pe.wait_ge(x1_done, CHT * (q - 2) + 3 + m)
                    else:
                        pe.wait_ge(z_evac, KM * q + m - 1)
                    w_in_product(q, KM + m).then_inc(z_ps, 1)
                if k in PE_XS:
                    m = PE_XS.index(k)
                    pe.wait_ge(xc_ready, KM * q + m + 1)
                    if m == 0:
                        pe.wait_ge(z_evac, KM * q + 3)
                    last = pe.matmul(psF[0:32, 0, :], w_x[:, m, :], xc[:, q % 2, m, :],
                                     start=(m == 0), stop=(m == KM - 1))
                    if m == KM - 1:
                        last.then_inc(xs_ps, 1)
                if k == PE_BT:
                    pe.wait_ge(xs_ready, q + 1)
                    pe.wait_ge(z_evac, KM * q + 4)
                    for t in range(CHT):
                        last = pe.transpose(psF[:, 1, t * 32:(t + 1) * 32], xs[0:32, t * P:(t + 1) * P], ident[0:32, 0:32])
                    last.then_inc(bt_ps, 1)
                if k in PE_V:
                    m = PE_V.index(k)
                    if m == 1:
                        pe.wait_ge(bt_ready, q + 1)
                    if m >= 2:
                        pe.wait_ge(v_evac, KM * q + m - 1)
                    pe.matmul(psF[:, m % 2, :], w_dt[:, m * P:(m + 1) * P], xs[:, :], start=True,
                              stop=True).then_inc(v_ps, 1)
                if k in PE_UT:
                    m = PE_UT.index(k)
                    pe.wait_ge(u_ready, KM * q + m + 1)
                    if m < 2:
                        pe.wait_ge(v_evac, KM * q + 3 + m)
                    else:
                        pe.wait_ge(ut_ready, KM * q + m - 1)
                    for t in range(CHT):
                        last = pe.transpose(psF[:, m % 2, t * P:(t + 1) * P], u[:, m, t * P:(t + 1) * P], ident[:, :])
                    last.then_inc(uT_ps, 1)

            def add_states(s):
                B, g = s // NG, s % NG
                if g == 0 and B >= 2:
                    pe.wait_ge(gated, B - 1)
                pe.wait_ge(scanned, QC * (s + 1))
                for j in range(QC):
                    last = pe.matmul(psY[32 * j:32 * j + 32, B % 2, :], pick[:, :], h[:, QC * (s % NH) + j, :],
                                     start=(g == 0), stop=(g == NG - 1))
                last.then_inc(summed, 1)

            pe.wait_ge(ident_ok, 1)
            front(0, PE_XNT)
            pe.wait_ge(w_ready, 1)
            pe.wait_ge(consts_ready, 1)
            pe.wait_ge(s_small, 16 * 7)
            for k in range(PE_XNT + 1, TILES):
                front(0, k)
            for q in range(NQ):
                for k in range(TILES):
                    s, j, t = STEPS * q + k // QC, k % QC, TILES * q + k
                    pe.wait_ge(pu_ready, t + 1)
                    if t >= NU:
                        pe.wait_ge(scanned, t - NU + 1)
                    for i in range(CHT):
                        last = pe.transpose(psU[:, t % NU, i * P:(i + 1) * P], pu[:, t % NPU, i, :], ident[:, :])
                    last.then_inc(transposed, 1)
                    if j == 0 and s >= 2:
                        add_states(s - 2)
                    front(q + 1, k)
            add_states(STEPS * NQ - 2)
            add_states(STEPS * NQ - 1)
            for t in range(CHT):
                pe.wait_ge(x1_done, CHT * (NQ - 1) + t - 1)
                project(NQ - 1, t)



def attention_block(nc, ctx_in, mask, w, x_res, xn3, x3_hi, x3_lo, ident, spare, ps):
    GRP = [(g * 4, min(g * 4 + 4, KC)) for g in range((KC + 3) // 4)]
    NGRP = len(GRP)
    SPLIT = [(0, 2 * BANK), (2 * BANK, SK)]
    KCOL = [(a * P, min(b * P, SKP)) for a, b in GRP]
    SCOL = [(n * BANK, min((n + 1) * BANK, SKE)) for n in range(NGRP)]
    with ExitStack() as ctx:
        def sb(name, shape, dt=F32, stack=ctx):
            return stack.enter_context(nc.sbuf_tensor(name, shape, dt))

        def sem(name):
            return ctx.enter_context(nc.semaphore(name))

        k_hi, k_lo = sb("k_hi", [P, KE, SKP], F32R), sb("k_lo", [P, KE, SKP], F32R)
        v_hi, v_lo = sb("v_hi", [P, KC, DM], F32R), sb("v_lo", [P, KC, DM], F32R)
        wqT = sb("wqT", [P, KE, DM])
        bq, bk = sb("bq", [P, KE]), sb("bk", [P, KE])
        bv = sb("bv", [P, DM])
        w_raw = sb("w_qkv_raw", [P, 3, KE, DM])
        xqT = sb("xqT", [P, KE, P])
        q_hi, q_lo = sb("q_hi", [P, 2, KE, P], F32R), sb("q_lo", [P, 2, KE, P], F32R)
        stats = sb("attn_stats", [P, NT, 6])
        mv = sb("attn_mv", [P, NT, 2])
        xn2 = sb("xn2", [P, 2, DM])
        xn3s = sb("xn3s", [P, 2, DM])
        stats3, mv3s, rstd3s = sb("stats3", [P, 2, 6]), sb("mv3s", [P, 2, 2]), sb("rstd3s", [P, 2])
        rstd = sb("attn_rstd", [P, NT])
        eps = sb("eps3", [P, 1])
        powers = sb("attn_powers", [P, NT])
        mx, nb, rs, rinv = sb("mx", [P, 2]), sb("nb", [P, 2]), sb("rs", [P, 2]), sb("rinv", [P, 2])
        mask_sb = sb("mask_sb", [P, 2, SK], I32)
        with ExitStack() as prep:
            c_raw = sb("c_raw", [P, KC, DM], F32, prep)
            c_hi, c_lo = sb("c_hi", [P, KE, SKP], F32R, prep), sb("c_lo", [P, KE, SKP], F32R, prep)
            wk_hi, wk_lo = sb("wk_hi", [P, KE, DM], F32R, prep), sb("wk_lo", [P, KE, DM], F32R, prep)
            wv_hi, wv_lo = sb("wv_hi", [P, KE, DM], F32R, prep), sb("wv_lo", [P, KE, DM], F32R, prep)
        with ExitStack() as rings:
            sc = sb("sc", [P, 2, SK], F32, rings)
            pr = sb("pr", [P, 2, SKP], F32, rings)
            p_hi, p_lo = sb("p_hi", [P, 2, KC, P], F32R, rings), sb("p_lo", [P, 2, KC, P], F32R, rings)

        bank = [ps[:, n * BANK:(n + 1) * BANK] for n in range(8)]
        psS = ps[:, 0:4 * BANK]
        psP = bank[4:6]
        psA, psO = bank[6], bank[7]

        w_in, b_in, c_in, c_zero = sem("wqkv_in"), sem("bqkv_in"), sem("ctx_in"), sem("ctx_zeroed")
        mask_in = [sem(f"mask_in{i}") for i in range(2)]
        mv2, ve2, rstd2, xn2_ready, bv_added = sem("mv2"), sem("ve2"), sem("rstd2"), sem("xn2_ready"), sem("bv_added")
        prep_ps, prep_hi, prep_lo = sem("prep_ps"), sem("prep_hi"), sem("prep_lo")
        pad_zero = sem("pad_zeroed")
        xq_ps, xq_ready, q_ps, qhi_ready, qlo_ready = sem("xq_ps"), sem("xq_ready"), sem("q_ps"), sem("qhi_ready"), sem("qlo_ready")
        filled, scores_ps, masked, nb_ready, exp_done = sem("filled"), sem("scores_ps"), sem("masked"), sem("nb_ready"), sem("exp_done")
        pt_ps, pthi_ready, ptlo_ready, pv_ps = sem("pt_ps"), sem("pthi_ready"), sem("ptlo_ready"), sem("pv_ps")
        xn3_kept = sem("xn3_kept")
        x2_ready, mv3, ve3, rstd3, xn3_ready = sem("x2_ready"), sem("mv3"), sem("ve3"), sem("rstd3"), sem("xn3_ready")
        x3_ps, x3hi_ready, x3lo_ready = sem("x3_ps"), sem("x3hi_ready"), sem("x3lo_ready")
        dve_link = sem("dve_link_b")
        MASK_LINKS, X2_LINKS = 2, 3

        wq_items = [(bank[0].rearrange("p (k n) -> p k n", k=KE), wqT[:, :, :], None, None)]
        wkv_items = [(bank[n].rearrange("p (k n) -> p k n", k=KE), hi[:, :, :], lo[:, :, :], None)
                     for n, (hi, lo) in ((1, (wk_hi, wk_lo)), (2, (wv_hi, wv_lo)))]
        ctx_items = [(bank[(3 + n) % 8][:, 0:b - a], c_hi[:, k, a:b], c_lo[:, k, a:b], None)
                     for n, (k, (a, b)) in enumerate([(k, ab) for k in range(KE) for ab in KCOL])]
        k_items = [(bank[(3 + n) % 8][:, 0:b - a], k_hi[:, m, a:b], k_lo[:, m, a:b], bk[:, m:m + 1])
                   for n, (m, (a, b)) in enumerate([(m, ab) for m in range(KE) for ab in KCOL])]
        v_items = [(bank[(3 + n) % 8][:, 0:DM], v_hi[:, c, :], v_lo[:, c, :], None) for n in range(KC) for c in [n]]
        items = wq_items + wkv_items + ctx_items + k_items + v_items

        block = ctx.enter_context(nc.Block())

        def tiles(eng, step):
            for i in range(-2, 4):
                step(i, i // 2, i % 2)
            with eng.Fori(2, NT // 2 - 1) as I:
                for p in range(2):
                    step(2 * I + p, I, p)
            for i in range(NT - 2, NT + 3):
                step(i, i // 2, i % 2)

        def on(i, d, lo=0, hi=NT):
            return not isinstance(i, int) or lo <= i + d < hi

        @block.sync
        def _(sp_):
            sp_.wait_ge(c_zero, 1)
            sp_.dma_start(c_raw[:, 0:KC - 1, :], ctx_in[0, 0:(KC - 1) * P, :].rearrange("(n p) d -> p n d", p=P)).then_inc(c_in, 16)
            sp_.dma_start(c_raw[0:SK - (KC - 1) * P, KC - 1, :], ctx_in[0, (KC - 1) * P:, :]).then_inc(c_in, 16)
            for n, name in enumerate(("Wq", "Wk", "Wv")):
                sp_.dma_start(w_raw[:, n, :, :], w[name].rearrange("(k p) e -> p k e", p=P)).then_inc(w_in, 16)
            for t, name in ((bq, "bq"), (bk, "bk")):
                sp_.dma_start(t[:, :], w[name].rearrange("(k p) -> p k", p=P), allow_slow_non_contiguous=True).then_inc(b_in, 16)
            sp_.dma_start(bv[:, :], w["bv"].rearrange("(a n) -> a n", a=1).to_broadcast([P, DM])).then_inc(b_in, 16)

            def step(i, n, par):
                if on(i, 0):
                    if not isinstance(i, int) or i >= 2:
                        sp_.wait_ge(masked, 2 * (i - 1))
                    sp_.dma_start(mask_sb[:, par, :], mask[0, ds(i * P, P), :]).then_inc(mask_in[par], 16)
            tiles(sp_, step)

        @block.gpsimd
        def _(pool):
            pool.memset(c_raw[:, KC - 1, :], 0.0).then_inc(c_zero, 1)
            pool.memset(eps[:, :], EPS)
            pool.memset(powers[:, :], -0.5).then_inc(ve2, 1)
            pool.wait_ge(mv2, 1)
            pool.tensor_scalar(rstd[:, :], mv[:, :, 1], EPS, None, ALU.add).then_inc(ve2, 1)
            pool.wait_ge(ve2, 2)
            pool.tensor_tensor(rstd[:, :], rstd[:, :], powers[:, :], ALU.pow).then_inc(rstd2, 1)
            pool.wait_ge(b_in, 48)
            pool.wait_ge(prep_lo, len(items) - 1)
            pool.wait_ge(prep_ps, len(items))
            for par in range(2):
                pool.memset(pr[:, par, SK:], 0.0).then_inc(pad_zero, 1)

            def step(i, n, par):
                if on(i, 0):
                    if not isinstance(i, int) or i >= 1:
                        pool.wait_ge(exp_done, i)
                    pool.wait_ge(xn2_ready, i + 1)
                    row = x_res[:, ds(i, 1), :].rearrange("p a d -> p (a d)")
                    pool.tensor_tensor(row, row, bv[:, :], ALU.add).then_inc(bv_added, 1)
                if on(i, 1):
                    pool.memset(sc[:, 1 - par, :], NEG / SCALE).then_inc(filled, 1)
                if on(i, -2):
                    pool.wait_ge(mv3, i - 1)
                    pool.tensor_tensor(rstd3s[:, par:par + 1], mv3s[:, par, 1:2], eps[:, :], ALU.add).then_inc(ve3, 1)
                    pool.wait_ge(ve3, i - 1)
                    pool.tensor_tensor(rstd3s[:, par:par + 1], rstd3s[:, par:par + 1], powers[:, 0:1], ALU.pow).then_inc(rstd3, 1)
            tiles(pool, step)

        @block.scalar
        def _(act):
            act.wait_ge(b_in, 48)
            for n, (src, hi, lo, bias) in enumerate(items):
                act.wait_ge(prep_ps, n + 1)
                if bias is None:
                    act.activation(hi, src, ACT.Copy).then_inc(prep_hi, 1)
                else:
                    act.activation(hi, src, ACT.Identity, bias=bias).then_inc(prep_hi, 1)

            def p_high(i, par, first, last):
                if on(i, -1):
                    for g in range(first, last):
                        a, b = GRP[g]
                        act.wait_ge(pt_ps, NGRP * (i - 1) + g + 1)
                        act.activation(p_hi[:, 1 - par, a:b, :], psP[g % 2][:, 0:(b - a) * P], ACT.Copy).then_inc(pthi_ready, 1)

            def step(i, n, par):
                if on(i, -1) and (not isinstance(i, int) or i >= 3):
                    act.wait_ge(pv_ps, i - 2)
                p_high(i, par, 0, 2)
                if on(i, -3):
                    act.wait_ge(x3_ps, i - 2)
                    act.activation(x3_hi[:, :, ds((i - 3) * P + KS - 1, P)], psA[:, 0:KE * P].rearrange("p (k n) -> p k n", k=KE),
                                   ACT.Copy).then_inc(x3hi_ready, 1)
                p_high(i, par, 2, NGRP)
                if on(i, 1):
                    act.wait_ge(xq_ps, i + 2)
                    act.activation(xqT[:, :, :], psA[:, 0:KE * P].rearrange("p (k n) -> p k n", k=KE), ACT.Copy).then_inc(xq_ready, 1)
                    act.wait_ge(q_ps, i + 2)
                    if not isinstance(i, int) or i >= 1:
                        act.wait_ge(scores_ps, 2 * i)
                    for m in range(KE):
                        act.activation(q_hi[:, 1 - par, m, :], psA[:, (KE + m) * P:(KE + m + 1) * P], ACT.Identity,
                                       bias=bq[:, m:m + 1]).then_inc(qhi_ready, 1)
                if on(i, -3):
                    act.activation(xn3[:, ds(i - 3, 1), :].rearrange("p a d -> p (a d)"), xn3s[:, 1 - par, :],
                                   ACT.Copy).then_inc(xn3_kept, 1)
                if on(i, 0):
                    act.wait_ge(nb_ready, i + 1)
                    if isinstance(i, int) and i < 2:
                        act.wait_ge(pad_zero, 2)
                    else:
                        act.wait_ge(pt_ps, NGRP * (i - 1))
                    if not isinstance(i, int) or i >= 2:
                        act.wait_ge(x2_ready, i - 1)
                    act.activation(pr[:, par, 0:SK], sc[:, par, :], ACT.Exp, bias=nb[:, par:par + 1], scale=SCALE,
                                   accum_out=rs[:, par:par + 1]).then_inc(exp_done, 1)
            tiles(act, step)

        @block.vector
        def _(dve):
            for t in range(NT):
                last = dve.bn_stats(stats[:, t, :], x_res[:, t, :])
            last.then_inc(dve_link, 1)
            dve.wait_ge(dve_link, 1)
            for t in range(NT):
                last = dve.bn_aggr(mv[:, t, :], stats[:, t, :])
            last.then_inc(mv2, 1)
            dve.wait_ge(rstd2, 1)
            dve.memset(x3_hi[:, :, 0:KS - 1].bitcast(U32), 0)
            dve.memset(x3_lo[:, :, 0:KS - 1].bitcast(U32), 0)
            done = 0
            for n, (src, hi, lo, bias) in enumerate(items):
                if lo is None:
                    continue
                dve.wait_ge(prep_hi, n + 1)
                if bias is None:
                    dve.tensor_tensor(lo, src, hi.bitcast(F32), ALU.subtract).then_inc(prep_lo, 1)
                else:
                    dve.scalar_tensor_tensor(lo, src, bias, hi.bitcast(F32), ALU.add, ALU.subtract).then_inc(prep_lo, 1)
                done += 1
            def p_low(i, par, first, last):
                if on(i, -1):
                    for g in range(first, last):
                        a, b = GRP[g]
                        dve.wait_ge(pthi_ready, NGRP * (i - 1) + g + 1)
                        dve.tensor_tensor(p_lo[:, 1 - par, a:b, :], psP[g % 2][:, 0:(b - a) * P],
                                          p_hi[:, 1 - par, a:b, :].bitcast(F32), ALU.subtract).then_inc(ptlo_ready, 1)

            def step(i, n, par):
                if on(i, -1) and (not isinstance(i, int) or i >= 3):
                    dve.wait_ge(pv_ps, i - 2)
                p_low(i, par, 0, 2)
                if on(i, -3):
                    dve.wait_ge(x3hi_ready, i - 2)
                    cols = ds((i - 3) * P + KS - 1, P)
                    dve.tensor_tensor(x3_lo[:, :, cols], psA[:, 0:KE * P].rearrange("p (k n) -> p k n", k=KE),
                                      x3_hi[:, :, cols].bitcast(F32), ALU.subtract).then_inc(x3lo_ready, 1)
                p_low(i, par, 2, NGRP)
                if on(i, -2):
                    row = x_res[:, ds(i - 2, 1), :].rearrange("p a d -> p (a d)")
                    dve.wait_ge(exp_done, i - 1)
                    dve.reciprocal(rinv[:, par:par + 1], rs[:, par:par + 1]).then_inc(x2_link, 1)
                    dve.wait_ge(x2_link, 3 * i - 5)
                    dve.wait_ge(pv_ps, i - 1)
                    dve.wait_ge(bv_added, i - 1)
                    dve.scalar_tensor_tensor(row, psO[:, 0:DM], rinv[:, par:par + 1], row, ALU.mult, ALU.add).then_inc(x2_ready, 1)
                    dve.wait_ge(x2_ready, i - 1)
                    plain(dve, spare, 3)
                    dve.bn_stats(stats3[:, par, :], row).then_inc(x2_link, 1)
                    dve.wait_ge(x2_link, 3 * i - 4)
                    plain(dve, spare, 4)
                    dve.bn_aggr(mv3s[:, par, :], stats3[:, par, :]).then_inc(mv3, 1)
                if on(i, 0):
                    dve.wait_ge(filled, i + 1)
                    dve.wait_ge(mask_in[par], 16 * (n + 1))
                    for s, (a, b) in enumerate(SPLIT):
                        dve.wait_ge(scores_ps, 2 * i + s + 1)
                        plain(dve, spare, 1 + s)
                        dve.copy_predicated(sc[:, par, a:b], mask_sb[:, par, a:b], psS[:, a:b]).then_inc(masked, 1)
                    dve.wait_ge(masked, 2 * i + 2)
                    dve.reduce_max(mx[:, par:par + 1], sc[:, par, :], AXX).then_inc(dve_link, 1)
                    dve.wait_ge(dve_link, i + 2)
                    dve.tensor_scalar(nb[:, par:par + 1], mx[:, par:par + 1], -SCALE, None, ALU.mult).then_inc(nb_ready, 1)
                if on(i, -2):
                    dve.wait_ge(mv3, i - 1)
                    dve.wait_ge(rstd3, i - 1)
                    if not isinstance(i, int) or i >= 4:
                        dve.wait_ge(x3_ps, i - 3)
                        dve.wait_ge(xn3_kept, i - 3)
                    dve.tensor_scalar(xn3s[:, par, :], x_res[:, ds(i - 2, 1), :].rearrange("p a d -> p (a d)"),
                                      mv3s[:, par, 0:1], rstd3s[:, par:par + 1],
                                      ALU.subtract, ALU.mult).then_inc(x2_link, 1)
                if on(i, 1):
                    dve.wait_ge(qhi_ready, KE * (i + 2))
                    for m in range(KE):
                        dve.scalar_tensor_tensor(q_lo[:, 1 - par, m, :], psA[:, (KE + m) * P:(KE + m + 1) * P], bq[:, m:m + 1],
                                                 q_hi[:, 1 - par, m, :].bitcast(F32), ALU.add, ALU.subtract).then_inc(qlo_ready, 1)
                if on(i, 2):
                    if not isinstance(i, int) or i >= 0:
                        dve.wait_ge(xq_ps, i + 1)
                    dve.tensor_scalar(xn2[:, par, :], x_res[:, ds(i + 2, 1), :].rearrange("p a d -> p (a d)"),
                                      mv[:, ds(i + 2, 1), 0:1].rearrange("p a d -> p (a d)"), rstd[:, ds(i + 2, 1)],
                                      ALU.subtract, ALU.mult).then_inc(xn2_ready, 1)
            x2_link = xn3_ready
            tiles(dve, step)

        @block.tensor
        def _(pe):
            def products(out, stat, mov, first, last):
                for n, (a, b) in enumerate(((0, 0), (0, 1), (1, 0))):
                    mm = pe.matmul(out, stat[a], mov[b], start=first and n == 0, stop=last and n == 2)
                return mm

            n = [0]

            bank_of = ([0, 1, 2] + [(3 + j) % 8 for j in range(len(ctx_items))]
                       + [(3 + j) % 8 for j in range(len(k_items))] + [(3 + j) % 8 for j in range(len(v_items))])

            def take():
                at = n[0]
                before = [i for i in range(at) if bank_of[i] == bank_of[at]]
                if before:
                    pe.wait_ge(prep_hi, before[-1] + 1)
                    if before[-1] > 0:
                        pe.wait_ge(prep_lo, before[-1])
                n[0] += 1
                return items[at][0]
            pe.wait_ge(w_in, 48)
            for m in range(3):
                out = take()
                for a in range(KE):
                    for k in range(KE):
                        last = pe.transpose(out[:, k, a * P:(a + 1) * P], w_raw[:, m, a, k * P:(k + 1) * P], ident[:, :])
                last.then_inc(prep_ps, 1)
            pe.wait_ge(c_in, 32)
            for k in range(KE):
                for a, b in GRP:
                    out = take()
                    for c in range(a, b):
                        last = pe.transpose(out[:, (c - a) * P:(c - a + 1) * P], c_raw[:, c, k * P:(k + 1) * P], ident[:, :])
                    last.then_inc(prep_ps, 1)
            pe.wait_ge(prep_lo, 2 + len(ctx_items))
            for m in range(KE):
                for a, b in KCOL:
                    out = take()
                    for k in range(KE):
                        last = products(out, (wk_hi[:, k, m * P:(m + 1) * P], wk_lo[:, k, m * P:(m + 1) * P]),
                                        (c_hi[:, k, a:b], c_lo[:, k, a:b]), k == 0, k == KE - 1)
                    last.then_inc(prep_ps, 1)
            for c in range(KC):
                out = take()
                for k in range(KE):
                    last = products(out, (c_hi[:, k, c * P:(c + 1) * P], c_lo[:, k, c * P:(c + 1) * P]),
                                    (wv_hi[:, k, :], wv_lo[:, k, :]), k == 0, k == KE - 1)
                last.then_inc(prep_ps, 1)
            pe.wait_ge(prep_hi, len(items))
            pe.wait_ge(prep_lo, len(items) - 1)

            def p_transposed(i, par, first, last_):
                if on(i, -1):
                    if first == 0:
                        pe.wait_ge(exp_done, i)
                    for g in range(first, last_):
                        a, b = GRP[g]
                        if not isinstance(i, int) or i > 1 or g > 1:
                            pe.wait_ge(ptlo_ready, NGRP * (i - 1) + g - 1)
                        for c in range(a, b):
                            last = pe.transpose(psP[g % 2][:, (c - a) * P:(c - a + 1) * P],
                                                pr[:, 1 - par, c * P:(c + 1) * P], ident[:, :])
                        last.then_inc(pt_ps, 1)

            def scores(i, par, first, last_):
                if on(i, 0):
                    if first == 0:
                        pe.wait_ge(qlo_ready, KE * (i + 1))
                    for s in range(first, last_):
                        a, b = SCOL[s]
                        if s % 2 == 0 and (not isinstance(i, int) or i >= 1):
                            pe.wait_ge(masked, 2 * (i - 1) + s // 2 + 1)
                        for k in range(KE):
                            last = products(psS[:, a:b], (q_hi[:, par, k, :], q_lo[:, par, k, :]),
                                            (k_hi[:, k, a:b], k_lo[:, k, a:b]), k == 0, k == KE - 1)
                        if s % 2 == 1:
                            last.then_inc(scores_ps, 1)

            def step(i, n, par):
                p_transposed(i, par, 0, 2)
                if on(i, -3):
                    pe.wait_ge(xn3_ready, 3 * (i - 2))
                    if on(i, 0):
                        pe.wait_ge(qlo_ready, KE * (i + 1))
                    if not isinstance(i, int) or i >= 4:
                        pe.wait_ge(x3lo_ready, i - 3)
                    for k in range(KE):
                        last = pe.transpose(psA[:, k * P:(k + 1) * P], xn3s[:, 1 - par, k * P:(k + 1) * P], ident[:, :])
                    last.then_inc(x3_ps, 1)
                scores(i, par, 0, 1)
                p_transposed(i, par, 2, NGRP)
                if on(i, 1):
                    if not isinstance(i, int) or i >= 3:
                        pe.wait_ge(x3lo_ready, i - 2)
                    if not isinstance(i, int) or i >= 0:
                        pe.wait_ge(qlo_ready, KE * (i + 1))
                    pe.wait_ge(xn2_ready, i + 2)
                    for k in range(KE):
                        last = pe.transpose(psA[:, k * P:(k + 1) * P], xn2[:, 1 - par, k * P:(k + 1) * P], ident[:, :])
                    last.then_inc(xq_ps, 1)
                scores(i, par, 1, NGRP)
                if on(i, 1):
                    pe.wait_ge(xq_ready, i + 2)
                    for m in range(KE):
                        for k in range(KE):
                            last = pe.matmul(psA[:, (KE + m) * P:(KE + m + 1) * P], wqT[:, k, m * P:(m + 1) * P], xqT[:, k, :],
                                             start=(k == 0), stop=(k == KE - 1))
                    last.then_inc(q_ps, 1)
                if on(i, -1):
                    if not isinstance(i, int) or i >= 2:
                        pe.wait_ge(x2_ready, i - 1)
                    for g, (a, b) in enumerate(GRP):
                        pe.wait_ge(ptlo_ready, NGRP * (i - 1) + g + 1)
                        for c in range(a, b):
                            last = products(psO[:, 0:DM], (p_hi[:, 1 - par, c, :], p_lo[:, 1 - par, c, :]),
                                            (v_hi[:, c, :], v_lo[:, c, :]), c == 0, c == KC - 1)
                    last.then_inc(pv_ps, 1)
            tiles(pe, step)



def expert_block(nc, w, x_res, xn3, x3_hi, x3_lo, ident, ps, out):
    WE = 2 * KE * FI + DM
    RING = 3
    ITEMS = NE
    with ExitStack() as ctx:
        def sb(name, shape, dt=F32, stack=ctx):
            return stack.enter_context(nc.sbuf_tensor(name, shape, dt))

        def sem(name):
            return ctx.enter_context(nc.semaphore(name))

        t1 = sb("t1", [P, 2, BANK])
        h_hi, h_lo = sb("h_hi", [P, 2, BANK], F32R), sb("h_lo", [P, 2, BANK], F32R)
        oT = sb("oT", [P, KE, BANK])
        sg = sb("sg", [P, 2, BANK])
        w_raw = sb("w_exp_raw", [P, RING, WE])
        w_hi, w_lo = sb("w_exp_hi", [P, NX, WE], F32R), sb("w_exp_lo", [P, NX, WE], F32R)
        cv_hi, cv_lo = sb("cv_hi", [P, KS, KE, FI], F32R), sb("cv_lo", [P, KS, KE, FI], F32R)
        sh_raw = sb("sh_raw", [P, KE * FI + DM])
        sh_hi, sh_lo = sb("sh_hi", [P, KE * FI + DM], F32R), sb("sh_lo", [P, KE * FI + DM], F32R)
        r_w, r_b = sb("r_w", [P, KE, 32]), sb("r_b", [P, NE])
        lg = sb("lg", [P, NT, NE])
        top, top_at = sb("top", [P, NT, 8]), sb("top_at", [P, NT, 8], U32)
        at_f, ids = sb("at_f", [P, NT, 2]), sb("ids", [P, NE])
        ex = sb("ex", [P, NT, NE])
        sm, pp, den = sb("sm", [P, NT]), sb("pp", [P, 2, NT]), sb("den", [P, NT])
        w_same = sb("w_same", [P, NT])
        cmb, cmb_hi = sb("cmb", [P, NT, 2 * NE]), sb("cmb_hi", [P, NT, NE], F32R)
        cT = sb("cT", [2 * NE, SEQ], F32R)
        row = sb("row", [2 * NE, NE, P], F32R)
        with ExitStack() as early:
            cv_raw = sb("cv_raw", [P, DM, KS], F32, early)
        o_sb = sb("o_sb", [P, 2, 2, DM])

        bank = [ps[:, n * BANK:(n + 1) * BANK] for n in range(8)]
        psG, psU, psC, psO = bank[0:2], bank[2:4], bank[4:6], bank[6:8]

        w_in = [sem(f"w_exp_in{i}") for i in range(RING)]
        r_zero, lgT_ps, lgT_ready, same_done = sem("r_zeroed"), sem("lgT_ps"), sem("lgT_ready"), sem("same_done")
        sh_in, r_in, cv_in = sem("sh_in"), sem("r_in"), sem("cv_in")
        whi_ready, w_ready = sem("w_exp_hi_ready"), sem("w_exp_ready")
        sh_split, cv_ps, cv_split = sem("sh_split"), sem("cv_ps"), sem("cv_split")
        ids_made, row_made = sem("ids_made"), sem("row_made")
        lg_ps, lg_max, lg_exp, cmb_ready, cT_ps, cT_ready = (sem("lg_ps"), sem("lg_max"), sem("lg_exp"), sem("cmb_ready"),
                                                             sem("cT_ps"), sem("cT_ready"))
        route_link = sem("route_link")
        gate_ps, up_ps, c_ps, sg_ready, t1_ready, t2_ready = (sem("gate_ps"), sem("up_ps"), sem("c_ps"), sem("sg_ready"),
                                                              sem("t1_ready"), sem("t2_ready"))
        hhi_ready, h_ready, down_done = sem("hhi_ready"), sem("h_ready"), sem("down_done")
        oT_ready, oB_ps, o_ready = sem("oT_ready"), sem("oB_ps"), sem("o_ready")
        stored = [sem(f"stored{i}") for i in range(2)]

        block = ctx.enter_context(nc.Block())

        @block.sync
        def _(sp_):
            sp_.wait_ge(r_zero, 1)
            sp_.dma_start(r_w[:, :, 0:NE], w["router_w"].rearrange("(k p) n -> p k n", p=P)).then_inc(r_in, 16)
            sp_.dma_start(r_b[:, :], w["router_bias"].rearrange("(a n) -> a n", a=1).to_broadcast([P, NE])).then_inc(r_in, 16)

            def load(e, slot):
                dst = w_raw[:, slot, :]
                n = KE * FI
                sp_.dma_start(dst[:, 0:n].rearrange("p (k n) -> p k n", k=KE),
                              w["expert_gate_w"][ds(e, 1), :, :].rearrange("a (k p) n -> p (a k) n", p=P)).then_inc(w_in[slot], 16)
                sp_.dma_start(dst[:, n:2 * n].rearrange("p (k n) -> p k n", k=KE),
                              w["expert_up_w"][ds(e, 1), :, :].rearrange("a (k p) n -> p (a k) n", p=P)).then_inc(w_in[slot], 16)
                sp_.dma_start(dst[:, 2 * n:], w["expert_down_w"][ds(e, 1), :, :].rearrange("a p n -> p (a n)")).then_inc(w_in[slot], 16)
            load(0, 0)
            sp_.dma_start(cv_raw[:, :, :], w["conv_w"]).then_inc(cv_in, 16)
            for e in range(1, RING):
                load(e, e)
            n = KE * FI
            sp_.dma_start(sh_raw[:, 0:n].rearrange("p (k n) -> p k n", k=KE),
                          w["shared_up_w"].rearrange("(k p) n -> p k n", p=P)).then_inc(sh_in, 16)
            sp_.dma_start(sh_raw[:, n:], w["shared_down_w"]).then_inc(sh_in, 16)
            with sp_.Fori(1, NX // RING) as E:
                for slot in range(RING):
                    sp_.wait_ge(w_ready, RING * E + slot - RING + 1)
                    load(RING * E + slot, slot)
            with sp_.Fori(0, NCH) as c:
                for t in range(2):
                    sp_.wait_ge(o_ready, 2 * c + t + 1)
                    sp_.dma_start(out[0, ds(c * BANK + t * 2 * P, 2 * P), :].rearrange("(n p) d -> p n d", p=P),
                                  o_sb[:, t, :, :]).then_inc(stored[t], 16)
            for t in range(2):
                sp_.wait_ge(stored[t], 16 * NCH)

        @block.gpsimd
        def _(pool):
            pool.memset(r_w[:, :, :], 0.0).then_inc(r_zero, 1)
            pool.iota(ids[:, :], pattern=[[1, NE]], base=0, channel_multiplier=0,
                      allow_small_or_imprecise_dtypes=True).then_inc(ids_made, 1)
            pool.memset(row[:, :, :].bitcast(F32), 0.0).then_inc(row_made, 1)
            for n in range(2):
                pool.wait_ge(row_made, n + 1)
                pool.affine_select(out=row[:, :, :], in_=row[:, :, :].bitcast(F32), compare_op=ALU.not_equal, fill=1.0, base=-NE * n,
                                   pattern=[[-1, NE], [0, P]], channel_multiplier=1).then_inc(row_made, 1)
            with pool.Fori(0, NX // RING) as E:
                for slot in range(RING):
                    e = RING * E + slot
                    pool.wait_ge(w_in[slot], 48 * (E + 1))
                    hi = w_hi[:, ds(e, 1), :].rearrange("p a n -> p (a n)")
                    lo = w_lo[:, ds(e, 1), :].rearrange("p a n -> p (a n)")
                    pool.wait_ge(whi_ready, e + 1)
                    pool.tensor_tensor(lo, w_raw[:, slot, :], hi.bitcast(F32), ALU.subtract).then_inc(w_ready, 1)

        @block.scalar
        def _(act):
            act.wait_ge(lgT_ps, 1)
            act.activation(sg[:, 0, :], bank[4], ACT.Copy).then_inc(lgT_ready, 1)
            act.wait_ge(lg_max, 1)
            act.activation(ex[:, :, :], ex[:, :, :], ACT.Exp).then_inc(lg_exp, 1)
            act.activation(pp[:, 1, :], pp[:, 1, :], ACT.Exp).then_inc(lg_exp, 1)
            act.wait_ge(cT_ps, 1)
            act.activation(cT[:, :], ps[0:2 * NE, 4 * BANK:8 * BANK], ACT.Copy).then_inc(cT_ready, 1)

            def hi_part(c, e):
                i = c * ITEMS + e
                act.wait_ge(t2_ready, i + 1)
                if e >= 2:
                    act.wait_ge(down_done, i - 1)
                act.activation(h_hi[:, e % 2, :], t1[:, e % 2, :], ACT.Copy).then_inc(hhi_ready, 1)

            def chunk(c):
                for e in range(ITEMS):
                    i = c * ITEMS + e
                    s = e % 2
                    act.wait_ge(gate_ps, i + 1)
                    if e >= 2:
                        act.wait_ge(t1_ready, i - 1)
                    act.activation(sg[:, s, :], psG[s], ACT.Silu).then_inc(sg_ready, 1)
                    hi_part(c, e)
                act.wait_ge(down_done, (c + 1) * ITEMS)
                act.activation(oT[:, :, :], ps[:, 6 * BANK:8 * BANK], ACT.Copy).then_inc(oT_ready, 1)
            chunk(0)
            with act.Fori(1, NCH) as c:
                chunk(c)

        @block.vector
        def _(dve):
            def routed_hi(e, slot, n):
                dve.wait_ge(w_in[slot], n)
                dve.tensor_copy(w_hi[:, ds(e, 1), :].rearrange("p a n -> p (a n)"), w_raw[:, slot, :]).then_inc(whi_ready, 1)
            routed_hi(0, 0, 48)
            for k in range(KE):
                src = bank[6 + k][:, 0:KS * P].rearrange("p (t n) -> p t n", t=KS)
                dve.wait_ge(cv_ps, k + 1)
                dve.tensor_copy(cv_hi[:, :, k, :], src).then_inc(cv_split, 1)
                dve.wait_ge(cv_split, 2 * k + 1)
                dve.tensor_tensor(cv_lo[:, :, k, :], src, cv_hi[:, :, k, :].bitcast(F32), ALU.subtract).then_inc(cv_split, 1)
            dve.wait_ge(lg_ps, 1)
            dve.wait_ge(r_in, 32)
            link, n = chain(dve, route_link, 0)
            link(dve.tensor_tensor(lg[:, :, :].rearrange("p (j r) e -> p r j e", r=CHT),
                                   bank[5].rearrange("p (r j e) -> p r j e", r=CHT, j=NCH)[:, :, :, 0:NE],
                                   r_b[:, :].unsqueeze(1).unsqueeze(1).to_broadcast([P, CHT, NCH, NE]), ALU.add))
            for t in range(NT):
                last = dve.max(top[:, t, :], lg[:, t, :])
            link(last)
            routed_hi(1, 1, 48)
            dve.tensor_tensor(ex[:, :, :], lg[:, :, :], top[:, :, 0:1].to_broadcast([P, NT, NE]), ALU.subtract)
            dve.tensor_tensor(pp[:, 1, :], top[:, :, 1], top[:, :, 0], ALU.subtract).then_inc(lg_max, 1)
            for t in range(NT):
                last = dve.max_index(top_at[:, t, :], top[:, t, :], lg[:, t, :])
            link(last)
            link(dve.tensor_copy(at_f[:, :, :], top_at[:, :, 0:2]))
            dve.wait_ge(lg_exp, 2)
            link(dve.reduce_sum(sm[:, :], ex[:, :, :], AXX))
            link(dve.reciprocal(pp[:, 0, :], sm[:, :]))
            link(dve.tensor_tensor(pp[:, 1, :], pp[:, 1, :], pp[:, 0, :], ALU.mult))
            link(dve.scalar_tensor_tensor(den[:, :], pp[:, 0, :], 1e-6, pp[:, 1, :], ALU.add, ALU.add))
            link(dve.reciprocal(den[:, :], den[:, :]))
            link(dve.tensor_tensor(pp[:, :, :], pp[:, :, :], den[:, :].unsqueeze(1).to_broadcast([P, 2, NT]), ALU.mult))
            dve.wait_ge(ids_made, 1)
            idb = ids[:, :].unsqueeze(1).to_broadcast([P, NT, NE])
            for n2, dst in ((0, cmb[:, :, 0:NE]), (1, ex[:, :, :])):
                link(dve.tensor_tensor(dst, idb, at_f[:, :, n2:n2 + 1].to_broadcast([P, NT, NE]), ALU.is_equal))
                link(dve.tensor_tensor(dst, dst, pp[:, n2, :].unsqueeze(2).to_broadcast([P, NT, NE]), ALU.mult))
            link(dve.tensor_tensor(cmb[:, :, 0:NE], cmb[:, :, 0:NE], ex[:, :, :], ALU.add))
            link(dve.tensor_copy(w_same[:, :], cmb[:, :, NX]))
            link(dve.tensor_copy(cmb_hi[:, :, :], cmb[:, :, 0:NE]))
            link(dve.tensor_tensor(cmb[:, :, NE:], cmb[:, :, 0:NE], cmb_hi[:, :, :].bitcast(F32), ALU.subtract))
            dve.tensor_copy(cmb[:, :, 0:NE], cmb_hi[:, :, :].bitcast(F32)).then_inc(cmb_ready, 1)
            for t in range(NT):
                dve.scalar_tensor_tensor(x_res[:, t, :], xn3[:, t, :], w_same[:, t:t + 1], x_res[:, t, :],
                                         ALU.mult, ALU.add).then_inc(same_done, 1)

            def beside(e):
                if e + 2 < NX:
                    routed_hi(e + 2, (e + 2) % RING, 48 * ((e + 2) // RING + 1))
                if e == NX - 4:
                    dve.wait_ge(sh_in, 32)
                    dve.tensor_copy(sh_hi[:, :], sh_raw[:, :]).then_inc(sh_split, 1)
                    dve.wait_ge(sh_split, 1)
                    dve.tensor_tensor(sh_lo[:, :], sh_raw[:, :], sh_hi[:, :].bitcast(F32), ALU.subtract).then_inc(sh_split, 1)

            def chunk(c):
                if isinstance(c, int):
                    dve.wait_ge(same_done, NT)
                    beside(0)
                for e in range(ITEMS):
                    i = c * ITEMS + e
                    s = e % 2
                    dve.wait_ge(up_ps, i + 1)
                    dve.wait_ge(sg_ready, i + 1)
                    dve.tensor_tensor(t1[:, s, :], sg[:, s, :], psU[s], ALU.mult).then_inc(t1_ready, 1)
                    dve.wait_ge(t1_ready, i + 1)
                    if e < NX:
                        dve.wait_ge(c_ps, c * NX + e + 1)
                        dve.tensor_tensor(t1[:, s, :], t1[:, s, :], psC[s], ALU.mult).then_inc(t2_ready, 1)
                    else:
                        dve.sem_inc(t2_ready, 1)
                    dve.wait_ge(hhi_ready, i + 1)
                    dve.tensor_tensor(h_lo[:, s, :], t1[:, s, :], h_hi[:, s, :].bitcast(F32), ALU.subtract).then_inc(h_ready, 1)
                    if isinstance(c, int):
                        beside(e + 1)
                for t in range(2):
                    dve.wait_ge(oB_ps, 2 * c + t + 1)
                    dve.tensor_tensor(o_sb[:, t, :, :], psC[t].rearrange("p (n d) -> p n d", n=2),
                                      x_res[:, ds(CHT * c + 2 * t, 2), :], ALU.add).then_inc(o_ready, 1)
                for t in range(2):
                    dve.wait_ge(stored[t], 16 * (c + 1))
            chunk(0)
            with dve.Fori(1, NCH) as c:
                chunk(c)

        @block.tensor
        def _(pe):
            def products(out, pairs, first, last):
                todo = [(st[a], mv_[b]) for st, mv_ in pairs for a, b in ((0, 0), (0, 1), (1, 0))]
                for n, (a, b) in enumerate(todo):
                    mm = pe.matmul(out, a, b, start=first and n == 0, stop=last and n == len(todo) - 1)
                return mm
            x3 = (x3_hi, x3_lo)
            pe.wait_ge(r_in, 32)
            parts = [(k, part) for k in range(KE) for part in x3]
            for n, (k, part) in enumerate(parts):
                for j in range(NCH):
                    cols = slice(KS - 1 + j * BANK, KS - 1 + (j + 1) * BANK)
                    last = pe.matmul(bank[4][32 * j:32 * j + 32, :], r_w[:, k, :], part[:, k, cols].bitcast(F32),
                                     start=(n == 0), stop=(n == len(parts) - 1))
            last.then_inc(lgT_ps, 1)
            pe.wait_ge(cv_in, 16)
            for k in range(KE):
                for tap in range(KS):
                    last = pe.transpose(bank[6 + k][:, tap * P:(tap + 1) * P], cv_raw[:, k * P:(k + 1) * P, tap], ident[:, :])
                last.then_inc(cv_ps, 1)
            pe.wait_ge(lgT_ready, 1)
            for t in range(CHT):
                last = pe.transpose(bank[5][:, t * P:(t + 1) * P], sg[:, 0, t * P:(t + 1) * P], ident[:, :])
            last.then_inc(lg_ps, 1)

            def weights_transposed():
                pe.wait_ge(cmb_ready, 1)
                pe.wait_ge(cv_split, 2 * KE)
                for t in range(NT):
                    last = pe.transpose(ps[0:2 * NE, 4 * BANK + t * P:4 * BANK + (t + 1) * P], cmb[:, t, :], ident[:, :])
                last.then_inc(cT_ps, 1)
                pe.wait_ge(cT_ready, 1)
                pe.wait_ge(row_made, 3)

            def chunk(c):
                def cols(shift=KS - 1):
                    return ds(c * BANK + shift, BANK)

                def down(e):
                    i = c * ITEMS + e
                    pe.wait_ge(h_ready, i + 1)
                    for m in range(KE):
                        sl = slice(2 * KE * FI + m * P, 2 * KE * FI + (m + 1) * P)
                        wd = ((w_hi[:, e, sl], w_lo[:, e, sl]) if e < NX else
                              (sh_hi[:, KE * FI + m * P:KE * FI + (m + 1) * P], sh_lo[:, KE * FI + m * P:KE * FI + (m + 1) * P]))
                        last = products(psO[m], [(wd, (h_hi[:, e % 2, :], h_lo[:, e % 2, :]))], e == 0, e == ITEMS - 1)
                    last.then_inc(down_done, 1)
                for e in range(ITEMS):
                    i = c * ITEMS + e
                    s = e % 2
                    mov = [(x3_hi[:, k, cols()], x3_lo[:, k, cols()]) for k in range(KE)]
                    if e < NX:
                        pe.wait_ge(w_ready, e + 1)
                        gate, up = ([(tuple(x[:, e, (o + k) * FI:(o + k + 1) * FI] for x in (w_hi, w_lo)), mov[k])
                                     for k in range(KE)] for o in (0, KE))
                    else:
                        if isinstance(c, int):
                            pe.wait_ge(sh_split, 2)
                        gate = [(tuple(x[:, tap, k, :] for x in (cv_hi, cv_lo)), (x3_hi[:, k, cols(tap)], x3_lo[:, k, cols(tap)]))
                                for tap in range(KS) for k in range(KE)]
                        up = [(tuple(x[:, k * FI:(k + 1) * FI] for x in (sh_hi, sh_lo)), mov[k]) for k in range(KE)]
                    if e >= 2:
                        pe.wait_ge(sg_ready, i - 1)
                    products(psG[s], gate, True, True).then_inc(gate_ps, 1)
                    if e >= 2:
                        pe.wait_ge(t2_ready, i - 1)
                    if e == 1 and not isinstance(c, int):
                        pe.wait_ge(t1_ready, i)
                    products(psU[s], up, True, True).then_inc(up_ps, 1)
                    if e == 1 and isinstance(c, int):
                        weights_transposed()
                    for n in ((), (0, 1), *((n,) for n in range(2, NX)), ())[e]:
                        pe.matmul(psC[n % 2], row[:, n, :], cT[:, ds(c * BANK, BANK)], start=True, stop=True).then_inc(c_ps, 1)
                    if e >= 1:
                        down(e - 1)
                down(ITEMS - 1)
                pe.wait_ge(oT_ready, c + 1)
                pe.wait_ge(t2_ready, c * ITEMS + ITEMS)
                for t in range(2):
                    for r in range(2):
                        for k in range(KE):
                            last = pe.transpose(psC[t][:, r * DM + k * P:r * DM + (k + 1) * P],
                                                oT[:, k, (2 * t + r) * P:(2 * t + r + 1) * P], ident[:, :])
                    last.then_inc(oB_ps, 1)
            chunk(0)
            with pe.Fori(1, NCH) as c:
                chunk(c)


def decoder_layer(nc, ins, out):
    with ExitStack() as keep:
        x_res = keep.enter_context(nc.sbuf_tensor("x_res", [P, NT, DM], F32))
        ident = keep.enter_context(nc.sbuf_tensor("ident", [P, P], F32))
        power = keep.enter_context(nc.sbuf_tensor("power", [P, CHT], F32))
        spare = keep.enter_context(nc.sbuf_tensor("spare", [P, 5], F32))
        ps = keep.enter_context(nc.psum_tensor("ps", [P, 8 * BANK], F32))

        def part(prefix):
            return {k[len(prefix):]: v for k, v in ins.items() if k.startswith(prefix)}
        scan_block(nc, ins["x"], part("L0_attn_"), x_res, ident, power, spare, ps)
        x3_hi = keep.enter_context(nc.sbuf_tensor("x3_hi", [P, KE, KS - 1 + SEQ], F32R))
        x3_lo = keep.enter_context(nc.sbuf_tensor("x3_lo", [P, KE, KS - 1 + SEQ], F32R))
        with nc.sbuf_tensor("xn3", [P, NT, DM], F32) as xn3:
            attention_block(nc, ins["ctx_1024"], ins["mask_BxSxS2_ik1"], part("L0_xattn_"), x_res, xn3, x3_hi, x3_lo,
                            ident, spare, ps)
        expert_block(nc, part("L0_ffn_"), x_res, xn3, x3_hi, x3_lo, ident, ps, out)


def kernel(**inputs):
    import numpy as _np
    import concourse.bacc as _bacc
    from concourse import mybir as _mybir
    from concourse.bass_utils import run_bass_kernel_spmd as _run

    nc = _bacc.Bacc("TRN2", target_bir_lowering=False, num_devices=1)
    arrays, ins = {}, {}
    for name, value in inputs.items():
        a = _np.ascontiguousarray(value)
        arrays[f"in_{name}_dram"] = a
        ins[name] = nc.dram_tensor(f"in_{name}_dram", a.shape, _mybir.dt.from_np(a.dtype), kind="ExternalInput").ap()
    out = nc.dram_tensor("out_0_dram", (1, SEQ, DM), F32, kind="ExternalOutput").ap()
    decoder_layer(nc, ins, out)
    r = _run(nc, [arrays], core_ids=[0])
    return r.results[0]["out_0_dram"]
```

```python
import concourse.bass as bass
from concourse import mybir
from contextlib import ExitStack

F32 = mybir.dt.float32
F32R = mybir.dt.float32r
I32 = mybir.dt.int32
U32 = mybir.dt.uint32
ALU = mybir.AluOpType
ACT = mybir.ActivationFunctionType
AXX = mybir.AxisListType.X
ds = bass.ds

P = 128
BANK = 512
SEQ = 2048
DM = 256
KE = DM // P
NT = SEQ // P
EPS = 1e-5

DI = 512
KM = DI // P
NS = 16
NTAP = 4
CH = BANK
CHT = CH // P
NQ = SEQ // CH
QC = P // 32
NG = NS // QC
TILES = KM * NG * QC
STEPS = KM * NG

PE_LAST = 58
NPU, NDA, NU, NH = 6, 8, 4, 3
PE_XNT, PE_X, PE_PROJ, PE_Z = 5, (9, 10, 12, 14), (14, 15, 19, 21), (21, 22, 27, 29)
PE_XS, PE_BT, PE_V, PE_UT = 38, 43, (44, 45, 46, 48), (54, 58, 61, 62)
ACT_HI, ACT_X, ACT_Z, ACT_SILU, ACT_XS = 5, (10, 12, 14, 16), (31, 33, 35, 37), 37, 42
ACT_BT, ACT_V, ACT_SP, ACT_UT = 46, (48, 50, 51, 52), 52, (58, 61, 62, 63)
DVE_LO, DVE_CONV, DVE_RES, DVE_DT = 5, (10, 12, 14, 16), (14, 17, 19, 21), 52
DVE_NEXT = 40
DVE_MOM, DVE_XN, POOL_RSTD = 44, 61, 0

SK = 1601
KC = (SK + P - 1) // P
SKP = KC * P
SKE = SK + SK % 2
NEG = -1.0e10
SCALE = 1.0 / 16.0

NE = 16
NX = NE - 1
FI = 128
KS = 3
NCH = SEQ // BANK
WE = 2 * KE * FI + DM
RING = 3


def plain(dve, spare, n):
    dve.memset(spare[:, n:n + 1], 0.0)


def chain(eng, sem, base):
    n = [0]

    def link(ins):
        n[0] += 1
        ins.then_inc(sem, 1)
        eng.wait_ge(sem, base + n[0])
    return link, n


def scan_block(nc, x, w, x_res, next_stats, shared, load_next, clear_next, ident, power, ps):
    with ExitStack() as ctx:
        def sb(name, shape, dt=F32, stack=ctx):
            return stack.enter_context(nc.sbuf_tensor(name, shape, dt))

        def sem(name):
            return ctx.enter_context(nc.semaphore(name))

        w_in_hi, w_in_lo, xnT_hi, xnT_lo = shared
        w_x = sb("w_x", [P, KM, 2 * NS])
        w_dt = sb("w_dt", [P, DI])
        b_dt = sb("b_dt", [P, KM])
        w_out = sb("w_out", [P, KM, DM])
        conv_w = sb("conv_w", [P, KM, NTAP])
        conv_b = sb("conv_b", [P, KM])
        d_skip = sb("d_skip", [P, KM])
        a_log = sb("a_log", [P, DI // 32, NS])
        neg_a = sb("neg_a", [P, TILES])
        pick = sb("pick", [P, 32])
        eps = sb("eps", [P, CHT])
        zs = sb("zs", [P, 2, KM, CH])
        xc = sb("xc", [P, 2, KM, CH])
        dt = sb("dt", [P, 2, KM, CH])
        ut = sb("ut", [P, 2, CHT, DI])
        bt = sb("bt", [P, 2, CHT, NS])
        hlast = sb("hlast", [P, TILES])
        xs = sb("xs", [P, CH])
        dt_rep = sb("dt_rep", [P, 2, QC, CH])
        xn = sb("xn", [P, CHT, DM])
        stats = sb("stats", [P, CHT, 6])
        mv = sb("mv", [P, CHT, 2])
        rstd = sb("rstd", [P, CHT])
        xp = sb("xp", [P, KM, NTAP - 1 + CH])
        sp = sb("sp", [P, KM, CH])
        u = sp
        pu = sb("pu", [P, NPU, CHT, P])
        da = sb("da", [P, NDA, CH])
        with ExitStack() as early:
            w_raw = sb("w_raw", [P, KE, 2 * DI], F32, early)
        with ExitStack() as late:
            h = sb("h", [P, NH * QC, CH], F32, late)
        psF = ps[:, 0:2 * BANK].rearrange("p (s n) -> p s n", s=2)
        psY = ps[:, 2 * BANK:4 * BANK].rearrange("p (s n) -> p s n", s=2)
        psU = ps[:, 4 * BANK:8 * BANK].rearrange("p (s n) -> p s n", s=NU)

        psL = [psF[:, 0, 0:DM], psF[:, 1, 0:DM], psY[:, 0, 0:DM], psU[:, 0, 0:DM]]

        x_in, x_rest, s_win, s_small, s_zero, s_alog = sem("x_in"), sem("x_rest"), [sem("w_x_in"), sem("w_z_in")], sem("small_in"), sem("zeroed"), sem("alog_in")
        pick_ready = sem("pick_ready")
        s_conv, s_wout = sem("conv_in"), sem("w_out_in")
        ident_made, ident_ok = sem("ident_made"), sem("ident_ok")
        hi_split, w_ready, a_exp, consts_ready = sem("w_in_hi_split"), sem("w_in_split"), sem("a_exp"), sem("consts_ready")
        dve_link, act_link = sem("dve_link"), sem("act_link")
        mv_ready, var_eps, rstd_ready = sem("mv_ready"), sem("var_eps"), sem("rstd_ready")
        xn_ready, xnT_ps, hi_ready, lo_ready = sem("xn_ready"), sem("xnT_ps"), sem("xnT_hi_ready"), sem("xnT_lo_ready")
        x_ps, x_evac, z_ps, z_evac = sem("x_ps"), sem("x_evac"), sem("z_ps"), sem("z_evac")
        tap_done, conv_done, xc_ready, zs_ready = sem("tap_done"), sem("conv_done"), sem("xc_ready"), sem("zs_ready")
        xs_ps, xs_ready, bt_ps, bt_ready = sem("xs_ps"), sem("xs_ready"), sem("bt_ps"), sem("bt_ready")
        exp_v, neg_abs, v_ps, v_evac, sp_ready, dt_ready, u_ready = sem("exp_v"), sem("neg_abs_ready"), sem("v_ps"), sem("v_evac"), sem("sp_ready"), sem("dt_ready"), sem("u_ready")
        uT_ps, ut_ready = sem("uT_ps"), sem("ut_ready")
        rep_in = [[sem(f"dt_rep_in{i}_{j}") for j in range(QC)] for i in range(2)]
        pu_ready, transposed, exp_ready, scanned = sem("pu_ready"), sem("transposed"), sem("exp_ready"), sem("scanned")
        saved, summed, gated = sem("saved"), sem("summed"), sem("gated")
        proj_ps, x1_done = sem("proj_ps"), sem("x1_done")

        block = ctx.enter_context(nc.Block())

        @block.sync
        def _(sp_):
            xv = x[0].rearrange("(n p) d -> p n d", p=P)
            sp_.dma_start(x_res[:, 0:CHT, :], xv[:, 0:CHT, :]).then_inc(x_in, 16)
            for part in range(2):
                cols = slice(part * DI, (part + 1) * DI)
                sp_.dma_start(w_raw[:, :, cols], w["W_in"][:, cols].rearrange("(k p) n -> p k n", p=P)).then_inc(s_win[part], 16)
            sp_.dma_start(conv_w[:, :, :], w["conv_w"].rearrange("(m p) k -> p m k", p=P)).then_inc(s_conv, 16)
            sp_.dma_start(conv_b[:, :], w["conv_b"].rearrange("(m p) -> p m", p=P), allow_slow_non_contiguous=True).then_inc(s_conv, 16)
            sp_.dma_start(d_skip[:, :], w["D"].rearrange("(m p) -> p m", p=P), allow_slow_non_contiguous=True).then_inc(s_small, 16)
            sp_.dma_start(w_x[:, :, :], w["W_x"].rearrange("(m p) n -> p m n", p=P)).then_inc(s_small, 16)
            sp_.wait_ge(s_zero, 1)
            for m in range(KM):
                sp_.dma_start(w_dt[32 * m:32 * m + NS, :], w["W_dt"]).then_inc(s_small, 16)
            sp_.dma_start(b_dt[:, :], w["b_dt"].rearrange("(m p) -> p m", p=P), allow_slow_non_contiguous=True).then_inc(s_small, 16)
            for q in range(QC):
                sp_.dma_start(a_log[32 * q:32 * q + 32, :, :],
                              w["A_log"].rearrange("(b p) n -> p b n", p=32)).then_inc(s_alog, 16)
            sp_.dma_start(x_res[:, CHT:, :], xv[:, CHT:, :]).then_inc(x_rest, 16)
            sp_.dma_start(w_out[:, :, :], w["W_out"].rearrange("(m p) n -> p m n", p=P)).then_inc(s_wout, 16)
            for q in range(NQ):
                for B in range(KM):
                    if q * KM + B == KM * NQ - 2:
                        sp_.wait_ge(z_ps, KM * NQ)
                        load_next(sp_)
                    sp_.wait_ge(dt_ready, KM * q + B + 1)
                    if q * KM + B >= 2:
                        sp_.wait_ge(exp_ready, TILES * q + 16 * (B - 1))
                    for j in range(QC):
                        for r in range(QC):
                            sp_.dma_start(dt_rep[32 * r:32 * r + 32, B % 2, j, :],
                                          dt[32 * j:32 * j + 32, q % 2, B, :]).then_inc(rep_in[B % 2][j], 16)

        @block.gpsimd
        def _(pool):
            pool.memset(w_dt[:, :], 0.0).then_inc(s_zero, 1)
            pool.memset(power[:, :], -0.5)
            pool.memset(eps[:, :], EPS)
            pool.memset(ident[:, :], 0.0).then_inc(ident_made, 1)
            pool.wait_ge(ident_made, 1)
            pool.affine_select(out=ident[:, :], in_=ident[:, :], compare_op=ALU.not_equal, fill=1.0, base=0,
                               pattern=[[-1, P]], channel_multiplier=1).then_inc(ident_ok, 1)

            def inverse_deviation(q):
                pool.wait_ge(mv_ready, q + 1)
                pool.wait_ge(xn_ready, q)
                pool.tensor_tensor(rstd[:, :], mv[:, :, 1], eps[:, :], ALU.add).then_inc(var_eps, 1)
                pool.wait_ge(var_eps, q + 1)
                pool.tensor_tensor(rstd[:, :], rstd[:, :], power[:, 0:CHT], ALU.pow).then_inc(rstd_ready, 1)

            inverse_deviation(0)
            inverse_deviation(1)
            for q in range(NQ):
                pool.wait_ge(bt_ready, q + 1)
                if q == NQ - 1:
                    pool.wait_ge(z_ps, KM * NQ)
                    clear_next(pool)
                for k in range(TILES):
                    g, t = QC * (k // QC % NG), TILES * q + k
                    b = k // 16 * QC + k % QC
                    if k % 16 == 0:
                        pool.wait_ge(ut_ready, KM * q + k // 16 + 1)
                    if t >= NPU:
                        pool.wait_ge(transposed, t - NPU + 1)
                    pool.tensor_tensor(
                        pu[:, t % NPU, :, :].rearrange("p t (n d) -> p t n d", n=QC),
                        ut[:, q % 2, :, 32 * b:32 * b + 32].unsqueeze(2).to_broadcast([P, CHT, QC, 32]),
                        bt[:, q % 2, :, g:g + QC].unsqueeze(3).to_broadcast([P, CHT, QC, 32]),
                        ALU.mult).then_inc(pu_ready, 1)
                    if k == POOL_RSTD and 1 <= q < NQ - 1:
                        inverse_deviation(q + 1)

        @block.scalar
        def _(act):
            link, _n = chain(act, act_link, 0)
            for part in range(2):
                cols = slice(part * DI, (part + 1) * DI)
                act.wait_ge(s_win[part], 16)
                act.activation(w_in_hi[:, :, cols], w_raw[:, :, cols], ACT.Copy).then_inc(hi_split, 1)

            def front(q, k):
                if k == ACT_HI:
                    act.wait_ge(xnT_ps, q + 1)
                    act.wait_ge(z_ps, KM * q)
                    act.activation(xnT_hi[:, :, :], psF, ACT.Copy).then_inc(hi_ready, 1)
                    act.wait_ge(conv_done, KM * q)
                    if q:
                        link(act.activation(xp[:, :, 0:NTAP - 1], xp[:, :, CH:], ACT.Copy))
                    else:
                        act.wait_ge(s_conv, 16 * 2)
                if k in ACT_X:
                    m = ACT_X.index(k)
                    act.wait_ge(x_ps, KM * q + m + 1)
                    act.activation(xp[:, m, NTAP - 1:], psF[:, m % 2, :], ACT.Copy).then_inc(x_evac, 1)
                    if q >= 2:
                        act.wait_ge(gated, KM * (q - 1))
                    act.wait_ge(x_evac, KM * q + m + 1)
                    act.activation(xc[:, q % 2, m, :], xp[:, m, 0:CH], ACT.Identity, bias=conv_b[:, m:m + 1],
                                   scale=conv_w[:, m, 0:1]).then_inc(tap_done, 1)
                if k in ACT_Z:
                    m = ACT_Z.index(k)
                    if q >= 2:
                        act.wait_ge(proj_ps, CHT * (q - 1))
                    act.wait_ge(z_ps, KM * q + m + 1)
                    act.activation(zs[:, q % 2, m, :], psF[:, m % 2, :], ACT.Copy).then_inc(z_evac, 1)
                if k == ACT_SILU and q == 0:
                    for m in range(KM):
                        act.wait_ge(conv_done, m + 1)
                        act.activation(xc[:, 0, m, :], xc[:, 0, m, :], ACT.Silu).then_inc(xc_ready, 1)
                elif k == ACT_SILU:
                    act.wait_ge(conv_done, KM * (q + 1))
                    act.activation(xc[:, q % 2, :, :], xc[:, q % 2, :, :], ACT.Silu).then_inc(xc_ready, KM)
                if k == ACT_XS:
                    act.wait_ge(xs_ps, q + 1)
                    act.wait_ge(v_ps, KM * q)
                    act.activation(xs[:, :], psF[:, 0, :], ACT.Copy).then_inc(xs_ready, 1)
                if k == ACT_BT:
                    act.wait_ge(bt_ps, q + 1)
                    if q >= 2:
                        act.wait_ge(pu_ready, TILES * (q - 1))
                    act.activation(bt[:, q % 2, :, :],
                                   psF[:, 1, 0:CHT * 32].rearrange("p (t n) -> p t n", t=CHT)[:, :, NS:2 * NS],
                                   ACT.Copy).then_inc(bt_ready, 1)
                if k == (ACT_SILU if q else ACT_BT):
                    act.wait_ge(z_evac, KM * (q + 1))
                    act.activation(zs[:, q % 2, :, :], zs[:, q % 2, :, :], ACT.Silu).then_inc(zs_ready, 1)
                if k in ACT_V:
                    m = ACT_V.index(k)
                    if q == 0:
                        act.wait_ge(neg_abs, m + 1)
                    else:
                        act.wait_ge(v_ps, KM * q + m + 1)
                        act.wait_ge(u_ready, KM * max(q - 1, 0))
                        act.activation(dt[:, q % 2, m, :], psF[:, m % 2, :], ACT.Identity, bias=b_dt[:, m:m + 1]).then_inc(v_evac, 1)
                        act.wait_ge(v_evac, KM * q + m + 1)
                        act.wait_ge(uT_ps, KM * q)
                        link(act.activation(sp[:, m, :], dt[:, q % 2, m, :], ACT.Abs))
                    act.activation(sp[:, m, :], sp[:, m, :], ACT.Exp, scale=-1.0 if q else 1.0).then_inc(exp_v, 1)
                if k == ACT_SP:
                    act.wait_ge(exp_v, KM * (q + 1))
                    for m in range(KM):
                        act.activation(sp[:, m, :], sp[:, m, :], ACT.Ln, bias=1.0).then_inc(sp_ready, 1)
                if k in ACT_UT:
                    m = ACT_UT.index(k)
                    act.wait_ge(uT_ps, KM * q + m + 1)
                    act.activation(ut[:, q % 2, :, m * P:(m + 1) * P],
                                   psF[:, m % 2, :].rearrange("p (t d) -> p t d", t=CHT), ACT.Copy).then_inc(ut_ready, 1)

            for k in range(TILES):
                if k == ACT_SILU:
                    act.wait_ge(s_alog, 16 * QC)
                    act.activation(a_log[:, :, :], a_log[:, :, :], ACT.Exp).then_inc(a_exp, 1)
                front(0, k)
            act.wait_ge(consts_ready, 1)
            for q in range(NQ):
                for k in range(TILES):
                    B, j, t = k // 16, k % QC, TILES * q + k
                    if k % 16 < QC:
                        act.wait_ge(rep_in[B % 2][j], (2 * q + B // 2 + 1) * 16 * QC)
                    if t >= NDA:
                        act.wait_ge(scanned, t - NDA + 1)
                    act.activation(da[:, t % NDA, :], dt_rep[:, B % 2, j, :], ACT.Exp,
                                   scale=neg_a[:, k:k + 1]).then_inc(exp_ready, 1)
                    if q + 1 < NQ:
                        front(q + 1, k)

        @block.vector
        def _(dve):
            link, _n = chain(dve, dve_link, 0)

            def moments(q):
                dve.wait_ge(x_in if q == 0 else x_rest, 16)
                for t in range(CHT):
                    last = dve.bn_stats(stats[:, t, :], x_res[:, q * CHT + t, :])
                link(last)
                for t in range(CHT):
                    last = dve.bn_aggr(mv[:, t, :], stats[:, t, :])
                last.then_inc(mv_ready, 1)

            def normalize(q):
                dve.wait_ge(rstd_ready, q + 1)
                dve.wait_ge(xnT_ps, q)
                for t in range(CHT):
                    last = dve.tensor_scalar(xn[:, t, :], x_res[:, q * CHT + t, :],
                                             mv[:, t, 0:1], rstd[:, t:t + 1], ALU.subtract, ALU.mult)
                last.then_inc(xn_ready, 1)

            def residual(t, out):
                row = x_res[:, t, :]
                dve.wait_ge(proj_ps, t + 1)
                dve.tensor_tensor(row, out, row, ALU.add).then_inc(x1_done, 1)

            def front(q, k):
                if k in DVE_RES and q >= 2:
                    t = DVE_RES.index(k)
                    residual(CHT * (q - 2) + t, psF[:, t % 2, 0:DM])
                if q == NQ:
                    return
                if k == DVE_LO:
                    dve.wait_ge(hi_ready, q + 1)
                    dve.tensor_tensor(xnT_lo[:, :, :], psF, xnT_hi[:, :, :].bitcast(F32),
                                      ALU.subtract).then_inc(lo_ready, 1)
                if k in DVE_CONV:
                    m = DVE_CONV.index(k)
                    acc = xc[:, q % 2, m, :]
                    dve.wait_ge(tap_done, KM * q + m + 1)
                    for n in range(1, NTAP):
                        last = dve.scalar_tensor_tensor(acc, xp[:, m, n:n + CH], conv_w[:, m, n:n + 1], acc,
                                                        ALU.mult, ALU.add)
                        if n < NTAP - 1:
                            link(last)
                    last.then_inc(conv_done, 1)
                if k == DVE_DT and q == 0:
                    for m in range(KM):
                        dve.wait_ge(v_ps, m + 1)
                        dve.tensor_scalar(dt[:, 0, m, :], psF[:, m % 2, :], b_dt[:, m:m + 1], None, ALU.add).then_inc(v_evac, 1)
                        dve.wait_ge(v_evac, m + 1)
                        dve.scalar_tensor_tensor(sp[:, m, :], dt[:, 0, m, :], -1.0, dt[:, 0, m, :], ALU.mult, ALU.min).then_inc(neg_abs, 1)
                if k == DVE_DT:
                    for m in range(KM):
                        d = dt[:, q % 2, m, :]
                        dve.wait_ge(sp_ready, KM * q + m + 1)
                        dve.scalar_tensor_tensor(d, d, 0.0, sp[:, m, :], ALU.max, ALU.add).then_inc(dt_ready, 1)
                        dve.wait_ge(dt_ready, KM * q + m + 1)
                        dve.tensor_tensor(u[:, m, :], d, xc[:, q % 2, m, :], ALU.mult).then_inc(u_ready, 1)
                if k == DVE_MOM and q + 1 < NQ:
                    moments(q + 1)
                if k == DVE_XN and q + 1 < NQ:
                    normalize(q + 1)

            def gate(B):
                q, m = B // KM, B % KM
                dve.wait_ge(summed, NG * (B + 1))
                dve.wait_ge(zs_ready, q + 1)
                if B == 0:
                    dve.wait_ge(s_small, 16 * 7)
                link(dve.scalar_tensor_tensor(xc[:, q % 2, m, :], xc[:, q % 2, m, :], d_skip[:, m:m + 1],
                                              psY[:, B % 2, :], ALU.mult, ALU.add))
                dve.tensor_tensor(zs[:, q % 2, m, :], xc[:, q % 2, m, :], zs[:, q % 2, m, :], ALU.mult).then_inc(gated, 1)

            dve.memset(xp[:, :, 0:NTAP - 1], 0.0)
            dve.memset(hlast[:, :], 0.0)
            moments(0)
            normalize(0)
            for part in range(2):
                cols = slice(part * DI, (part + 1) * DI)
                dve.wait_ge(hi_split, part + 1)
                dve.tensor_tensor(w_in_lo[:, :, cols], w_raw[:, :, cols], w_in_hi[:, :, cols].bitcast(F32),
                                  ALU.subtract).then_inc(w_ready, 1)
                if part == 0:
                    front(0, DVE_LO)
            dve.wait_ge(ident_ok, 1)
            for r in range(QC):
                last = dve.tensor_copy(pick[32 * r:32 * r + 32, :], ident[32 * r:32 * r + 32, 32 * r:32 * r + 32])
            last.then_inc(pick_ready, 1)
            for k in range(DVE_LO + 1, DVE_DT):
                front(0, k)
            dve.wait_ge(a_exp, 1)
            for r in range(QC):
                rows = slice(32 * r, 32 * r + 32)
                dst = neg_a[rows, :].rearrange("p (b g j) -> p b g j", b=KM, g=NG)
                src = a_log[rows, :, :].rearrange("p (b j) (g n) -> p n b g j", b=KM, n=QC)[:, r]
                last = dve.tensor_scalar(dst, src, -1.0, None, ALU.mult)
            last.then_inc(consts_ready, 1)
            for k in range(DVE_DT, TILES):
                front(0, k)
            for q in range(NQ):
                for k in range(TILES):
                    s, j, t = STEPS * q + k // QC, k % QC, TILES * q + k
                    if j == 0 and s >= NH:
                        dve.wait_ge(summed, s - NH + 1)
                        if s - NH < STEPS * (NQ - 1):
                            dve.wait_ge(saved, s - NH + 1)
                    dve.wait_ge(transposed, t + 1)
                    dve.wait_ge(exp_ready, t + 1)
                    dve.tensor_tensor_scan(h[:, QC * (s % NH) + j, :], da[:, t % NDA, :], psU[:, t % NU, :],
                                           hlast[:, k:k + 1], ALU.mult, ALU.add).then_inc(scanned, 1)
                    if j == 2 and 1 <= s <= STEPS * (NQ - 1):
                        e = s - 1
                        dve.wait_ge(scanned, QC * s)
                        dve.tensor_copy(hlast[:, QC * (e % STEPS):QC * (e % STEPS) + QC],
                                        h[:, QC * (e % NH):QC * (e % NH) + QC, CH - 1]).then_inc(saved, 1)
                    if k % 16 == 2 and t > 16:
                        gate(t // 16 - 1)
                    front(q + 1, k)
                    if q == NQ - 1 and k == DVE_NEXT:
                        dve.wait_ge(x1_done, NT - CHT)
                        for i in range(NT - CHT):
                            dve.bn_stats(next_stats[:, i, :], x_res[:, i, :])
            gate(KM * NQ - 1)
            for t in range(CHT):
                residual(CHT * (NQ - 1) + t, psL[t])

        @block.tensor
        def _(pe):
            def project(q, t):
                pe.wait_ge(gated, KM * (q + 1))
                pe.wait_ge(s_wout, 16)
                for m in range(KM):
                    last = pe.matmul(psF[:, t % 2, 0:DM], zs[:, q % 2, m, t * P:(t + 1) * P], w_out[:, m, :],
                                     start=(m == 0), stop=(m == KM - 1))
                last.then_inc(proj_ps, 1)

            def last_project(t, blocks):
                for m in blocks:
                    last = pe.matmul(psL[t], zs[:, (NQ - 1) % 2, m, t * P:(t + 1) * P], w_out[:, m, :],
                                     start=(m == 0), stop=(m == KM - 1))
                return last

            def w_in_product(q, m):
                i = 0
                for n in range(KE):
                    for a, b in ((w_in_hi, xnT_hi), (w_in_hi, xnT_lo), (w_in_lo, xnT_hi)):
                        last = pe.matmul(psF[:, m % 2, :], a[:, n, m * P:(m + 1) * P], b[:, n, :],
                                         start=(i == 0), stop=(i == 3 * KE - 1))
                        i += 1
                return last

            def front(q, k):
                if k in PE_PROJ and q >= 2:
                    t = PE_PROJ.index(k)
                    if q == NQ:
                        pe.wait_ge(ut_ready, KM * NQ)
                    elif t < 2:
                        pe.wait_ge(x_evac, KM * q + 3 + t)
                    if t >= 2:
                        pe.wait_ge(x1_done, CHT * (q - 2) + t - 1)
                    project(q - 2, t)
                if q == NQ:
                    return
                if k == PE_XNT:
                    pe.wait_ge(xn_ready, q + 1)
                    pe.wait_ge(ut_ready, KM * q)
                    for t in range(CHT):
                        for n in range(KE):
                            last = pe.transpose(psF[:, n, t * P:(t + 1) * P], xn[:, t, n * P:(n + 1) * P], ident[:, :])
                    last.then_inc(xnT_ps, 1)
                if k in PE_X:
                    m = PE_X.index(k)
                    pe.wait_ge(lo_ready, q + 1)
                    if q == 0:
                        pe.wait_ge(w_ready, 1)
                    if m >= 2:
                        pe.wait_ge(x_evac, KM * q + m - 1)
                    w_in_product(q, m).then_inc(x_ps, 1)
                if k in PE_Z:
                    m = PE_Z.index(k)
                    if q == 0:
                        pe.wait_ge(w_ready, 2)
                    if m < 2:
                        pe.wait_ge(x_evac, KM * q + 3 + m)
                        if q >= 2:
                            pe.wait_ge(x1_done, CHT * (q - 2) + 3 + m)
                    else:
                        pe.wait_ge(z_evac, KM * q + m - 1)
                    w_in_product(q, KM + m).then_inc(z_ps, 1)
                if k == PE_XS:
                    pe.wait_ge(xc_ready, KM * (q + 1))
                    pe.wait_ge(z_evac, KM * q + 3)
                    if q == 0:
                        pe.wait_ge(s_small, 16 * 7)
                    for m in range(KM):
                        last = pe.matmul(psF[32 * m:32 * m + 32, 0, :], w_x[:, m, :], xc[:, q % 2, m, :],
                                         start=True, stop=True)
                    last.then_inc(xs_ps, 1)
                if k == PE_BT:
                    pe.wait_ge(xs_ready, q + 1)
                    pe.wait_ge(z_evac, KM * q + 4)
                    if q == 0:
                        pe.wait_ge(pick_ready, 1)
                    for t in range(CHT):
                        last = pe.matmul(psF[:, 1, t * 32:(t + 1) * 32], xs[:, t * P:(t + 1) * P], pick[:, :],
                                         start=True, stop=True)
                    last.then_inc(bt_ps, 1)
                if k in PE_V:
                    m = PE_V.index(k)
                    if m == 1:
                        pe.wait_ge(bt_ready, q + 1)
                    if m >= 2:
                        pe.wait_ge(v_evac, KM * q + m - 1)
                    pe.matmul(psF[:, m % 2, :], w_dt[:, m * P:(m + 1) * P], xs[:, :], start=True,
                              stop=True).then_inc(v_ps, 1)
                if k in PE_UT:
                    m = PE_UT.index(k)
                    pe.wait_ge(u_ready, KM * q + m + 1)
                    if m < 2:
                        pe.wait_ge(v_evac, KM * q + 3 + m)
                    else:
                        pe.wait_ge(ut_ready, KM * q + m - 1)
                    for t in range(CHT):
                        last = pe.transpose(psF[:, m % 2, t * P:(t + 1) * P], u[:, m, t * P:(t + 1) * P], ident[:, :])
                    last.then_inc(uT_ps, 1)

            def add_states(s):
                B, g = s // NG, s % NG
                if g == 0 and B >= 2:
                    pe.wait_ge(gated, B - 1)
                pe.wait_ge(scanned, QC * (s + 1))
                for j in range(QC):
                    last = pe.matmul(psY[32 * j:32 * j + 32, B % 2, :], pick[:, :], h[:, QC * (s % NH) + j, :],
                                     start=(g == 0), stop=(g == NG - 1))
                last.then_inc(summed, 1)

            pe.wait_ge(ident_ok, 1)
            front(0, PE_XNT)
            for k in range(PE_XNT + 1, TILES):
                front(0, k)
            for q in range(NQ):
                for k in range(TILES):
                    s, j, t = STEPS * q + k // QC, k % QC, TILES * q + k
                    pe.wait_ge(pu_ready, t + 1)
                    if t >= NU:
                        pe.wait_ge(scanned, t - NU + 1)
                    for i in range(CHT):
                        last = pe.transpose(psU[:, t % NU, i * P:(i + 1) * P], pu[:, t % NPU, i, :], ident[:, :])
                    last.then_inc(transposed, 1)
                    if j == 0 and s >= 2:
                        add_states(s - 2)
                    front(q + 1, k)
                    if q == NQ - 1 and k == PE_LAST:
                        pe.wait_ge(x1_done, CHT * q)
                        pe.wait_ge(gated, KM * q + KM - 1)
                        for t in range(CHT - 1):
                            last_project(t, range(KM - 1))
            add_states(STEPS * NQ - 2)
            add_states(STEPS * NQ - 1)
            last_project(CHT - 1, range(KM - 1))
            pe.wait_ge(gated, KM * NQ)
            for t in range(CHT):
                last_project(t, (KM - 1,)).then_inc(proj_ps, 1)



def attention_block(nc, mask, x_res, stats, xn3, x3_hi, x3_lo, shared, loaded, load_next, clear_next, ident, spare, ps):
    GRP = [(g * 4, min(g * 4 + 4, KC)) for g in range((KC + 3) // 4)]
    NGRP = len(GRP)
    SPLIT = [(0, 2 * BANK), (2 * BANK, SK)]
    KCOL = [(a * P, min(b * P, SKP)) for a, b in GRP]
    SCOL = [(n * BANK, min((n + 1) * BANK, SKE)) for n in range(NGRP)]
    with ExitStack() as ctx:
        def sb(name, shape, dt=F32, stack=ctx):
            return stack.enter_context(nc.sbuf_tensor(name, shape, dt))

        def sem(name):
            return ctx.enter_context(nc.semaphore(name))

        k_hi, k_lo = sb("k_hi", [P, KE, SKP], F32R), sb("k_lo", [P, KE, SKP], F32R)
        v_hi, v_lo = sb("v_hi", [P, KC, DM], F32R), sb("v_lo", [P, KC, DM], F32R)
        c_raw, mask_sb, w_raw, bv, bq, bk, wqT, xn2 = shared
        xqT = sb("xqT", [P, KE, P])
        q_hi, q_lo = sb("q_hi", [P, 2, KE, P], F32R), sb("q_lo", [P, 2, KE, P], F32R)
        mv = sb("attn_mv", [P, NT, 2])
        xn3s = sb("xn3s", [P, 2, DM])
        stats3, mv3s, rstd3s = sb("stats3", [P, 2, 6]), sb("mv3s", [P, 2, 2]), sb("rstd3s", [P, 2])
        rstd = sb("attn_rstd", [P, NT])
        eps = sb("eps3", [P, 1])
        powers = sb("attn_powers", [P, NT])
        mx, nb, rs, rinv = sb("mx", [P, 2]), sb("nb", [P, 2]), sb("rs", [P, 2]), sb("rinv", [P, 2])
        with ExitStack() as prep:
            c_hi, c_lo = sb("c_hi", [P, KE, SKP], F32R, prep), sb("c_lo", [P, KE, SKP], F32R, prep)
            wk_hi, wk_lo = sb("wk_hi", [P, KE, DM], F32R, prep), sb("wk_lo", [P, KE, DM], F32R, prep)
            wv_hi, wv_lo = sb("wv_hi", [P, KE, DM], F32R, prep), sb("wv_lo", [P, KE, DM], F32R, prep)
        with ExitStack() as rings:
            sc = sb("sc", [P, 2, SK], F32, rings)
            pr = sb("pr", [P, 2, SKP], F32, rings)
            p_hi, p_lo = sb("p_hi", [P, 2, KC, P], F32R, rings), sb("p_lo", [P, 2, KC, P], F32R, rings)

        bank = [ps[:, n * BANK:(n + 1) * BANK] for n in range(8)]
        psS = ps[:, 0:4 * BANK]
        psP = bank[4:6]
        psA, psO = bank[6], bank[7]

        w_in, b_in, c_in = loaded
        mask_in = [sem(f"mask_in{i}") for i in range(2)]
        mv2, ve2, rstd2, xn2_ready, bv_added = sem("mv2"), sem("ve2"), sem("rstd2"), sem("xn2_ready"), sem("bv_added")
        prep_ps, prep_hi, prep_lo = sem("prep_ps"), sem("prep_hi"), sem("prep_lo")
        pad_zero = sem("pad_zeroed")
        xq_ps, xq_ready, q_ps, qhi_ready, qlo_ready = sem("xq_ps"), sem("xq_ready"), sem("q_ps"), sem("qhi_ready"), sem("qlo_ready")
        filled, scores_ps, masked, nb_ready, exp_done = sem("filled"), sem("scores_ps"), sem("masked"), sem("nb_ready"), sem("exp_done")
        pt_ps, pthi_ready, ptlo_ready, pv_ps = sem("pt_ps"), sem("pthi_ready"), sem("ptlo_ready"), sem("pv_ps")
        xn3_kept = sem("xn3_kept")
        x2_ready, mv3, ve3, rstd3, xn3_ready = sem("x2_ready"), sem("mv3"), sem("ve3"), sem("rstd3"), sem("xn3_ready")
        x3_ps, x3hi_ready, x3lo_ready = sem("x3_ps"), sem("x3hi_ready"), sem("x3lo_ready")
        dve_link = sem("dve_link_b")
        MASK_LINKS, X2_LINKS = 2, 3

        wq_items = [(bank[0].rearrange("p (k n) -> p k n", k=KE), wqT[:, :, :], None, None)]
        wkv_items = [(bank[n].rearrange("p (k n) -> p k n", k=KE), hi[:, :, :], lo[:, :, :], None)
                     for n, (hi, lo) in ((1, (wk_hi, wk_lo)), (2, (wv_hi, wv_lo)))]
        ctx_items = [(bank[(3 + n) % 8][:, 0:b - a], c_hi[:, k, a:b], c_lo[:, k, a:b], None)
                     for n, (k, (a, b)) in enumerate([(k, ab) for ab in KCOL for k in range(KE)])]
        k_items = [(bank[(3 + n) % 8][:, 0:b - a], k_hi[:, m, a:b], k_lo[:, m, a:b], bk[:, m:m + 1])
                   for n, (m, (a, b)) in enumerate([(m, ab) for ab in KCOL for m in range(KE)])]
        VBANKS = (3, 4, 5, 7, 0, 1, 2)
        v_items = [(bank[VBANKS[n % 7]][:, 0:DM], v_hi[:, c, :], v_lo[:, c, :], None) for n in range(KC) for c in [n]]
        items = wq_items + wkv_items + ctx_items + k_items + v_items
        lead_at = len(items) - len(v_items)
        bank_of = ([0, 1, 2] + [(3 + j) % 8 for j in range(len(ctx_items))] + [(3 + j) % 8 for j in range(len(k_items))]
                   + [VBANKS[j % 7] for j in range(len(v_items))])

        block = ctx.enter_context(nc.Block())

        def lead(step):
            for i in range(-2, 0):
                step(i, i // 2, i % 2)

        def tiles(eng, step):
            for i in range(4):
                step(i, i // 2, i % 2)
            with eng.Fori(2, NT // 2 - 1) as I:
                for p in range(2):
                    step(2 * I + p, I, p)
            for i in range(NT - 2, NT + 3):
                step(i, i // 2, i % 2)

        def on(i, d, lo=0, hi=NT):
            return not isinstance(i, int) or lo <= i + d < hi

        @block.sync
        def _(sp_):
            def step(i, n, par):
                if on(i, 0):
                    if not isinstance(i, int) or i >= 2:
                        sp_.wait_ge(masked, 2 * (i - 1))
                    sp_.dma_start(mask_sb[:, par, :], mask[0, ds(i * P, P), :]).then_inc(mask_in[par], 16)
            sp_.wait_ge(prep_ps, 3 + len(ctx_items))
            lead(step)
            tiles(sp_, step)
            sp_.wait_ge(masked, 2 * NT)
            load_next(sp_)

        @block.gpsimd
        def _(pool):
            pool.memset(eps[:, :], EPS)
            pool.memset(powers[:, :], -0.5).then_inc(ve2, 1)
            pool.wait_ge(mv2, 1)
            pool.tensor_scalar(rstd[:, :], mv[:, :, 1], EPS, None, ALU.add).then_inc(ve2, 1)
            pool.wait_ge(ve2, 2)
            pool.tensor_tensor(rstd[:, :], rstd[:, :], powers[:, :], ALU.pow).then_inc(rstd2, 1)
            pool.wait_ge(b_in, 48)
            pool.wait_ge(prep_lo, len(items) - 1)
            pool.wait_ge(prep_ps, len(items))
            for par in range(2):
                pool.memset(pr[:, par, SK:], 0.0).then_inc(pad_zero, 1)

            def step(i, n, par):
                if isinstance(i, int) and i == NT:
                    pool.wait_ge(masked, 2 * NT)
                    clear_next(pool)
                if on(i, 0):
                    if not isinstance(i, int) or i >= 1:
                        pool.wait_ge(exp_done, i)
                    pool.wait_ge(xn2_ready, i + 1)
                    row = x_res[:, ds(i, 1), :].rearrange("p a d -> p (a d)")
                    pool.tensor_tensor(row, row, bv[:, :], ALU.add).then_inc(bv_added, 1)
                if on(i, 1):
                    pool.memset(sc[:, 1 - par, :], NEG / SCALE).then_inc(filled, 1)
                if on(i, -2):
                    pool.wait_ge(mv3, i - 1)
                    pool.tensor_tensor(rstd3s[:, par:par + 1], mv3s[:, par, 1:2], eps[:, :], ALU.add).then_inc(ve3, 1)
                    pool.wait_ge(ve3, i - 1)
                    pool.tensor_tensor(rstd3s[:, par:par + 1], rstd3s[:, par:par + 1], powers[:, 0:1], ALU.pow).then_inc(rstd3, 1)
            lead(step)
            tiles(pool, step)

        @block.scalar
        def _(act):
            def p_high(i, par, first, last):
                if on(i, -1):
                    for g in range(first, last):
                        a, b = GRP[g]
                        act.wait_ge(pt_ps, NGRP * (i - 1) + g + 1)
                        act.activation(p_hi[:, 1 - par, a:b, :], psP[g % 2][:, 0:(b - a) * P], ACT.Copy).then_inc(pthi_ready, 1)

            def step(i, n, par):
                if on(i, -1) and (not isinstance(i, int) or i >= 3):
                    act.wait_ge(pv_ps, i - 2)
                p_high(i, par, 0, 2)
                if on(i, -3):
                    act.wait_ge(x3_ps, i - 2)
                    act.activation(x3_hi[:, :, ds((i - 3) * P + KS - 1, P)], psA[:, 0:KE * P].rearrange("p (k n) -> p k n", k=KE),
                                   ACT.Copy).then_inc(x3hi_ready, 1)
                p_high(i, par, 2, NGRP)
                if on(i, 1):
                    act.wait_ge(xq_ps, i + 2)
                    act.activation(xqT[:, :, :], psA[:, 0:KE * P].rearrange("p (k n) -> p k n", k=KE), ACT.Copy).then_inc(xq_ready, 1)
                    act.wait_ge(q_ps, i + 2)
                    if not isinstance(i, int) or i >= 1:
                        act.wait_ge(scores_ps, 2 * i)
                    for m in range(KE):
                        act.activation(q_hi[:, 1 - par, m, :], psA[:, (KE + m) * P:(KE + m + 1) * P], ACT.Identity,
                                       bias=bq[:, m:m + 1]).then_inc(qhi_ready, 1)
                if on(i, -3):
                    act.activation(xn3[:, ds(i - 3, 1), :].rearrange("p a d -> p (a d)"), xn3s[:, 1 - par, :],
                                   ACT.Copy).then_inc(xn3_kept, 1)
                if on(i, 0):
                    act.wait_ge(nb_ready, i + 1)
                    if isinstance(i, int) and i < 2:
                        act.wait_ge(pad_zero, 2)
                    else:
                        act.wait_ge(pt_ps, NGRP * (i - 1))
                    if not isinstance(i, int) or i >= 2:
                        act.wait_ge(x2_ready, i - 1)
                    act.activation(pr[:, par, 0:SK], sc[:, par, :], ACT.Exp, bias=nb[:, par:par + 1], scale=SCALE,
                                   accum_out=rs[:, par:par + 1]).then_inc(exp_done, 1)
            act.wait_ge(b_in, 48)
            for n, (src, hi, lo, bias) in enumerate(items):
                if n == lead_at:
                    lead(step)
                act.wait_ge(prep_ps, n + 1)
                if bias is None:
                    act.activation(hi, src, ACT.Copy).then_inc(prep_hi, 1)
                else:
                    act.activation(hi, src, ACT.Identity, bias=bias).then_inc(prep_hi, 1)
            tiles(act, step)

        @block.vector
        def _(dve):
            dve.memset(x3_hi[:, :, 0:KS - 1].bitcast(U32), 0)
            dve.memset(x3_lo[:, :, 0:KS - 1].bitcast(U32), 0)

            def moments():
                for t in range(NT - CHT, NT):
                    last = dve.bn_stats(stats[:, t, :], x_res[:, t, :])
                last.then_inc(dve_link, 1)
                dve.wait_ge(dve_link, 1)
                for t in range(NT):
                    last = dve.bn_aggr(mv[:, t, :], stats[:, t, :])
                last.then_inc(mv2, 1)

            x2_link = xn3_ready

            def p_low(i, par, first, last):
                if on(i, -1):
                    for g in range(first, last):
                        a, b = GRP[g]
                        dve.wait_ge(pthi_ready, NGRP * (i - 1) + g + 1)
                        dve.tensor_tensor(p_lo[:, 1 - par, a:b, :], psP[g % 2][:, 0:(b - a) * P],
                                          p_hi[:, 1 - par, a:b, :].bitcast(F32), ALU.subtract).then_inc(ptlo_ready, 1)

            def step(i, n, par):
                if on(i, -1) and (not isinstance(i, int) or i >= 3):
                    dve.wait_ge(pv_ps, i - 2)
                p_low(i, par, 0, 2)
                if on(i, -3):
                    dve.wait_ge(x3hi_ready, i - 2)
                    cols = ds((i - 3) * P + KS - 1, P)
                    dve.tensor_tensor(x3_lo[:, :, cols], psA[:, 0:KE * P].rearrange("p (k n) -> p k n", k=KE),
                                      x3_hi[:, :, cols].bitcast(F32), ALU.subtract).then_inc(x3lo_ready, 1)
                p_low(i, par, 2, NGRP)
                if on(i, -2):
                    row = x_res[:, ds(i - 2, 1), :].rearrange("p a d -> p (a d)")
                    dve.wait_ge(exp_done, i - 1)
                    dve.reciprocal(rinv[:, par:par + 1], rs[:, par:par + 1]).then_inc(x2_link, 1)
                    dve.wait_ge(x2_link, 3 * i - 5)
                    dve.wait_ge(pv_ps, i - 1)
                    dve.wait_ge(bv_added, i - 1)
                    dve.scalar_tensor_tensor(row, psO[:, 0:DM], rinv[:, par:par + 1], row, ALU.mult, ALU.add).then_inc(x2_ready, 1)
                    dve.wait_ge(x2_ready, i - 1)
                    plain(dve, spare, 3)
                    dve.bn_stats(stats3[:, par, :], row).then_inc(x2_link, 1)
                    dve.wait_ge(x2_link, 3 * i - 4)
                    plain(dve, spare, 4)
                    dve.bn_aggr(mv3s[:, par, :], stats3[:, par, :]).then_inc(mv3, 1)
                if on(i, 0):
                    dve.wait_ge(filled, i + 1)
                    dve.wait_ge(mask_in[par], 16 * (n + 1))
                    for s, (a, b) in enumerate(SPLIT):
                        dve.wait_ge(scores_ps, 2 * i + s + 1)
                        plain(dve, spare, 1 + s)
                        dve.copy_predicated(sc[:, par, a:b], mask_sb[:, par, a:b], psS[:, a:b]).then_inc(masked, 1)
                    dve.wait_ge(masked, 2 * i + 2)
                    dve.reduce_max(mx[:, par:par + 1], sc[:, par, :], AXX).then_inc(dve_link, 1)
                    dve.wait_ge(dve_link, i + 2)
                    dve.tensor_scalar(nb[:, par:par + 1], mx[:, par:par + 1], -SCALE, None, ALU.mult).then_inc(nb_ready, 1)
                if on(i, -2):
                    dve.wait_ge(mv3, i - 1)
                    dve.wait_ge(rstd3, i - 1)
                    if not isinstance(i, int) or i >= 4:
                        dve.wait_ge(x3_ps, i - 3)
                        dve.wait_ge(xn3_kept, i - 3)
                    dve.tensor_scalar(xn3s[:, par, :], x_res[:, ds(i - 2, 1), :].rearrange("p a d -> p (a d)"),
                                      mv3s[:, par, 0:1], rstd3s[:, par:par + 1],
                                      ALU.subtract, ALU.mult).then_inc(x2_link, 1)
                if on(i, 1):
                    dve.wait_ge(qhi_ready, KE * (i + 2))
                    for m in range(KE):
                        dve.scalar_tensor_tensor(q_lo[:, 1 - par, m, :], psA[:, (KE + m) * P:(KE + m + 1) * P], bq[:, m:m + 1],
                                                 q_hi[:, 1 - par, m, :].bitcast(F32), ALU.add, ALU.subtract).then_inc(qlo_ready, 1)
                if on(i, 2):
                    if not isinstance(i, int) or i >= 0:
                        dve.wait_ge(xq_ps, i + 1)
                    dve.tensor_scalar(xn2[:, par, :], x_res[:, ds(i + 2, 1), :].rearrange("p a d -> p (a d)"),
                                      mv[:, ds(i + 2, 1), 0:1].rearrange("p a d -> p (a d)"), rstd[:, ds(i + 2, 1)],
                                      ALU.subtract, ALU.mult).then_inc(xn2_ready, 1)
            for n, (src, hi, lo, bias) in enumerate(items):
                if lo is None:
                    continue
                if n == 3 + len(ctx_items):
                    moments()
                if n == lead_at:
                    dve.wait_ge(rstd2, 1)
                    lead(step)
                dve.wait_ge(prep_hi, n + 1)
                if bias is None:
                    dve.tensor_tensor(lo, src, hi.bitcast(F32), ALU.subtract).then_inc(prep_lo, 1)
                else:
                    dve.scalar_tensor_tensor(lo, src, bias, hi.bitcast(F32), ALU.add, ALU.subtract).then_inc(prep_lo, 1)
            tiles(dve, step)

        @block.tensor
        def _(pe):
            def products(out, stat, mov, first, last):
                for n, (a, b) in enumerate(((0, 0), (0, 1), (1, 0))):
                    mm = pe.matmul(out, stat[a], mov[b], start=first and n == 0, stop=last and n == 2)
                return mm

            n = [0]

            def take():
                at = n[0]
                before = [i for i in range(at) if bank_of[i] == bank_of[at]]
                if before:
                    pe.wait_ge(prep_hi, before[-1] + 1)
                    if before[-1] > 0:
                        pe.wait_ge(prep_lo, before[-1])
                n[0] += 1
                return items[at][0]
            def p_transposed(i, par, first, last_):
                if on(i, -1):
                    if first == 0:
                        pe.wait_ge(exp_done, i)
                    for g in range(first, last_):
                        a, b = GRP[g]
                        if not isinstance(i, int) or i > 1 or g > 1:
                            pe.wait_ge(ptlo_ready, NGRP * (i - 1) + g - 1)
                        for c in range(a, b):
                            last = pe.transpose(psP[g % 2][:, (c - a) * P:(c - a + 1) * P],
                                                pr[:, 1 - par, c * P:(c + 1) * P], ident[:, :])
                        last.then_inc(pt_ps, 1)

            def scores(i, par, first, last_):
                if on(i, 0):
                    if first == 0:
                        pe.wait_ge(qlo_ready, KE * (i + 1))
                    for s in range(first, last_):
                        a, b = SCOL[s]
                        if s % 2 == 0 and (not isinstance(i, int) or i >= 1):
                            pe.wait_ge(masked, 2 * (i - 1) + s // 2 + 1)
                        for k in range(KE):
                            last = products(psS[:, a:b], (q_hi[:, par, k, :], q_lo[:, par, k, :]),
                                            (k_hi[:, k, a:b], k_lo[:, k, a:b]), k == 0, k == KE - 1)
                        if s % 2 == 1:
                            last.then_inc(scores_ps, 1)

            def step(i, n, par):
                p_transposed(i, par, 0, 2)
                if on(i, -3):
                    pe.wait_ge(xn3_ready, 3 * (i - 2))
                    if on(i, 0):
                        pe.wait_ge(qlo_ready, KE * (i + 1))
                    if not isinstance(i, int) or i >= 4:
                        pe.wait_ge(x3lo_ready, i - 3)
                    for k in range(KE):
                        last = pe.transpose(psA[:, k * P:(k + 1) * P], xn3s[:, 1 - par, k * P:(k + 1) * P], ident[:, :])
                    last.then_inc(x3_ps, 1)
                scores(i, par, 0, 1)
                p_transposed(i, par, 2, NGRP)
                if on(i, 1):
                    if not isinstance(i, int) or i >= 3:
                        pe.wait_ge(x3lo_ready, i - 2)
                    if not isinstance(i, int) or i >= 0:
                        pe.wait_ge(qlo_ready, KE * (i + 1))
                    pe.wait_ge(xn2_ready, i + 2)
                    for k in range(KE):
                        last = pe.transpose(psA[:, k * P:(k + 1) * P], xn2[:, 1 - par, k * P:(k + 1) * P], ident[:, :])
                    last.then_inc(xq_ps, 1)
                scores(i, par, 1, NGRP)
                if on(i, 1):
                    pe.wait_ge(xq_ready, i + 2)
                    for m in range(KE):
                        for k in range(KE):
                            last = pe.matmul(psA[:, (KE + m) * P:(KE + m + 1) * P], wqT[:, k, m * P:(m + 1) * P], xqT[:, k, :],
                                             start=(k == 0), stop=(k == KE - 1))
                    last.then_inc(q_ps, 1)
                if on(i, -1):
                    if not isinstance(i, int) or i >= 2:
                        pe.wait_ge(x2_ready, i - 1)
                    for g, (a, b) in enumerate(GRP):
                        pe.wait_ge(ptlo_ready, NGRP * (i - 1) + g + 1)
                        for c in range(a, b):
                            last = products(psO[:, 0:DM], (p_hi[:, 1 - par, c, :], p_lo[:, 1 - par, c, :]),
                                            (v_hi[:, c, :], v_lo[:, c, :]), c == 0, c == KC - 1)
                    last.then_inc(pv_ps, 1)
            pe.wait_ge(w_in, 48)
            for m in range(3):
                out = take()
                for a in range(KE):
                    for k in range(KE):
                        last = pe.transpose(out[:, k, a * P:(a + 1) * P], w_raw[:, m, a, k * P:(k + 1) * P], ident[:, :])
                last.then_inc(prep_ps, 1)
            pe.wait_ge(c_in, 32)
            for a, b in GRP:
                for k in range(KE):
                    out = take()
                    for c in range(a, b):
                        last = pe.transpose(out[:, (c - a) * P:(c - a + 1) * P], c_raw[:, c, k * P:(k + 1) * P], ident[:, :])
                    last.then_inc(prep_ps, 1)
            for g, (a, b) in enumerate(KCOL):
                pe.wait_ge(prep_lo, 2 + KE * (g + 1))
                for m in range(KE):
                    out = take()
                    for k in range(KE):
                        last = products(out, (wk_hi[:, k, m * P:(m + 1) * P], wk_lo[:, k, m * P:(m + 1) * P]),
                                        (c_hi[:, k, a:b], c_lo[:, k, a:b]), k == 0, k == KE - 1)
                    last.then_inc(prep_ps, 1)
            for c in range(KC):
                if n[0] == lead_at:
                    q_last = max(i for i in range(lead_at) if bank_of[i] == 6)
                    pe.wait_ge(prep_hi, q_last + 1)
                    pe.wait_ge(prep_lo, q_last)
                    lead(step)
                out = take()
                for k in range(KE):
                    last = products(out, (c_hi[:, k, c * P:(c + 1) * P], c_lo[:, k, c * P:(c + 1) * P]),
                                    (wv_hi[:, k, :], wv_lo[:, k, :]), k == 0, k == KE - 1)
                last.then_inc(prep_ps, 1)
            pe.wait_ge(prep_hi, len(items))
            pe.wait_ge(prep_lo, len(items) - 1)

            tiles(pe, step)



def expert_block(nc, w, x_res, xn3, x3_hi, x3_lo, shared, r_in, row_made, w_in, load, ident, ps, out):
    ITEMS = NE
    with ExitStack() as ctx:
        def sb(name, shape, dt=F32, stack=ctx):
            return stack.enter_context(nc.sbuf_tensor(name, shape, dt))

        def sem(name):
            return ctx.enter_context(nc.semaphore(name))

        t1 = sb("t1", [P, 2, BANK])
        h_hi, h_lo = sb("h_hi", [P, 2, BANK], F32R), sb("h_lo", [P, 2, BANK], F32R)
        oT = sb("oT", [P, KE, BANK])
        w_raw, r_w, r_b, row, sg, sh_raw = shared
        w_hi, w_lo = sb("w_exp_hi", [P, NX, WE], F32R), sb("w_exp_lo", [P, NX, WE], F32R)
        cv_hi, cv_lo = sb("cv_hi", [P, KS, KE, FI], F32R), sb("cv_lo", [P, KS, KE, FI], F32R)
        sh_hi, sh_lo = sb("sh_hi", [P, KE * FI + DM], F32R), sb("sh_lo", [P, KE * FI + DM], F32R)
        lg = sb("lg", [P, NT, NE])
        top, top_at = sb("top", [P, NT, 8]), sb("top_at", [P, NT, 8], U32)
        at_f, ids = sb("at_f", [P, NT, 2]), sb("ids", [P, NE])
        ex = sb("ex", [P, NT, NE])
        sm, pp, den = sb("sm", [P, NT]), sb("pp", [P, 2, NT]), sb("den", [P, NT])
        w_same = sb("w_same", [P, NT])
        cmb, cmb_hi = sb("cmb", [P, NT, 2 * NE]), sb("cmb_hi", [P, NT, NE], F32R)
        cT = sb("cT", [2 * NE, SEQ], F32R)
        with ExitStack() as early:
            cv_raw = sb("cv_raw", [P, DM, KS], F32, early)
        o_sb = sb("o_sb", [P, 2, 2, DM])

        bank = [ps[:, n * BANK:(n + 1) * BANK] for n in range(8)]
        psG, psU, psC, psO = bank[0:2], bank[2:4], bank[4:6], bank[6:8]

        lgT_ps, lgT_ready, same_done = sem("lgT_ps"), sem("lgT_ready"), sem("same_done")
        sh_in, cv_in = sem("sh_in"), sem("cv_in")
        whi_ready, w_ready = sem("w_exp_hi_ready"), sem("w_exp_ready")
        sh_split, cv_ps, cv_split = sem("sh_split"), sem("cv_ps"), sem("cv_split")
        ids_made = sem("ids_made")
        lg_ps, lg_max, lg_exp, cmb_ready, cT_ps, cT_ready = (sem("lg_ps"), sem("lg_max"), sem("lg_exp"), sem("cmb_ready"),
                                                             sem("cT_ps"), sem("cT_ready"))
        route_link = sem("route_link")
        gate_ps, up_ps, c_ps, sg_ready, t1_ready, t2_ready = (sem("gate_ps"), sem("up_ps"), sem("c_ps"), sem("sg_ready"),
                                                              sem("t1_ready"), sem("t2_ready"))
        hhi_ready, h_ready, down_done = sem("hhi_ready"), sem("h_ready"), sem("down_done")
        oT_ready, oB_ps, o_ready = sem("oT_ready"), sem("oB_ps"), sem("o_ready")
        stored = [sem(f"stored{i}") for i in range(2)]

        block = ctx.enter_context(nc.Block())

        @block.sync
        def _(sp_):
            sp_.dma_start(cv_raw[:, :, :], w["conv_w"]).then_inc(cv_in, 16)
            n = KE * FI
            sp_.dma_start(sh_raw[:, 0:n].rearrange("p (k n) -> p k n", k=KE),
                          w["shared_up_w"].rearrange("(k p) n -> p k n", p=P)).then_inc(sh_in, 16)
            sp_.dma_start(sh_raw[:, n:], w["shared_down_w"]).then_inc(sh_in, 16)
            with sp_.Fori(1, NX // RING) as E:
                for slot in range(RING):
                    sp_.wait_ge(w_ready, RING * E + slot - RING + 1)
                    load(sp_, RING * E + slot, slot)
            with sp_.Fori(0, NCH) as c:
                for t in range(2):
                    sp_.wait_ge(o_ready, 2 * c + t + 1)
                    sp_.dma_start(out[0, ds(c * BANK + t * 2 * P, 2 * P), :].rearrange("(n p) d -> p n d", p=P),
                                  o_sb[:, t, :, :]).then_inc(stored[t], 16)
            for t in range(2):
                sp_.wait_ge(stored[t], 16 * NCH)

        @block.gpsimd
        def _(pool):
            pool.iota(ids[:, :], pattern=[[1, NE]], base=0, channel_multiplier=0,
                      allow_small_or_imprecise_dtypes=True).then_inc(ids_made, 1)
            with pool.Fori(0, NX // RING) as E:
                for slot in range(RING):
                    e = RING * E + slot
                    pool.wait_ge(w_in[slot], 48 * (E + 1))
                    hi = w_hi[:, ds(e, 1), :].rearrange("p a n -> p (a n)")
                    lo = w_lo[:, ds(e, 1), :].rearrange("p a n -> p (a n)")
                    pool.wait_ge(whi_ready, e + 1)
                    pool.tensor_tensor(lo, w_raw[:, slot, :], hi.bitcast(F32), ALU.subtract).then_inc(w_ready, 1)

        @block.scalar
        def _(act):
            act.wait_ge(lgT_ps, 1)
            act.activation(sg[:, 0, :], bank[4], ACT.Copy).then_inc(lgT_ready, 1)
            act.wait_ge(lg_max, 1)
            act.activation(ex[:, :, :], ex[:, :, :], ACT.Exp).then_inc(lg_exp, 1)
            act.activation(pp[:, 1, :], pp[:, 1, :], ACT.Exp).then_inc(lg_exp, 1)
            def hi_part(c, e):
                i = c * ITEMS + e
                act.wait_ge(t2_ready, i + 1)
                if isinstance(c, int) and e == 0:
                    act.wait_ge(same_done, NT // 2)
                if e >= 2 or not isinstance(c, int):
                    act.wait_ge(down_done, i - 1)
                act.activation(h_hi[:, e % 2, :], t1[:, e % 2, :], ACT.Copy).then_inc(hhi_ready, 1)

            def silu_gate(i, s):
                act.wait_ge(gate_ps, i + 1)
                act.activation(sg[:, s, :], psG[s], ACT.Silu).then_inc(sg_ready, 1)

            def take_output(c):
                act.wait_ge(down_done, (c + 1) * ITEMS)
                act.activation(oT[:, :, :], ps[:, 6 * BANK:8 * BANK], ACT.Copy).then_inc(oT_ready, 1)

            def chunk(c):
                for e in range(ITEMS):
                    i = c * ITEMS + e
                    if e >= 2 or not isinstance(c, int):
                        act.wait_ge(t1_ready, i - 1)
                        silu_gate(i, e % 2)
                    hi_part(c, e)
                    if e == 0 and not isinstance(c, int):
                        take_output(c - 1)
            for e in range(2):
                silu_gate(e, e)
            act.wait_ge(cT_ps, 1)
            act.activation(cT[:, :], ps[0:2 * NE, 4 * BANK:8 * BANK], ACT.Copy).then_inc(cT_ready, 1)
            chunk(0)
            act.wait_ge(same_done, NT)
            with act.Fori(1, NCH) as c:
                chunk(c)
            take_output(NCH - 1)

        @block.vector
        def _(dve):
            def routed_hi(e, slot, n):
                dve.wait_ge(w_in[slot], n)
                dve.tensor_copy(w_hi[:, ds(e, 1), :].rearrange("p a n -> p (a n)"), w_raw[:, slot, :]).then_inc(whi_ready, 1)
            routed_hi(0, 0, 48)
            routed_hi(1, 1, 48)
            for k in range(KE):
                src = bank[6 + k][:, 0:KS * P].rearrange("p (t n) -> p t n", t=KS)
                dve.wait_ge(cv_ps, k + 1)
                dve.tensor_copy(cv_hi[:, :, k, :], src).then_inc(cv_split, 1)
                dve.wait_ge(cv_split, 2 * k + 1)
                dve.tensor_tensor(cv_lo[:, :, k, :], src, cv_hi[:, :, k, :].bitcast(F32), ALU.subtract).then_inc(cv_split, 1)
            dve.wait_ge(lg_ps, 1)
            dve.wait_ge(r_in, 32)
            link, n = chain(dve, route_link, 0)
            link(dve.tensor_tensor(lg[:, :, :].rearrange("p (j r) e -> p r j e", r=CHT),
                                   bank[5].rearrange("p (r j e) -> p r j e", r=CHT, j=NCH)[:, :, :, 0:NE],
                                   r_b[:, :].unsqueeze(1).unsqueeze(1).to_broadcast([P, CHT, NCH, NE]), ALU.add))
            for t in range(NT):
                last = dve.max(top[:, t, :], lg[:, t, :])
            link(last)
            dve.tensor_tensor(ex[:, :, :], lg[:, :, :], top[:, :, 0:1].to_broadcast([P, NT, NE]), ALU.subtract)
            dve.tensor_tensor(pp[:, 1, :], top[:, :, 1], top[:, :, 0], ALU.subtract).then_inc(lg_max, 1)
            for t in range(NT):
                last = dve.max_index(top_at[:, t, :], top[:, t, :], lg[:, t, :])
            link(last)
            link(dve.tensor_copy(at_f[:, :, :], top_at[:, :, 0:2]))
            dve.wait_ge(ids_made, 1)
            for n2 in range(2):
                dve.tensor_tensor(cmb[:, :, n2 * NE:(n2 + 1) * NE], ids[:, :].unsqueeze(1).to_broadcast([P, NT, NE]),
                                  at_f[:, :, n2:n2 + 1].to_broadcast([P, NT, NE]), ALU.is_equal)
            dve.wait_ge(lg_exp, 2)
            link(dve.reduce_sum(sm[:, :], ex[:, :, :], AXX))
            link(dve.reciprocal(pp[:, 0, :], sm[:, :]))
            link(dve.tensor_tensor(pp[:, 1, :], pp[:, 1, :], pp[:, 0, :], ALU.mult))
            link(dve.scalar_tensor_tensor(den[:, :], pp[:, 0, :], 1e-6, pp[:, 1, :], ALU.add, ALU.add))
            link(dve.reciprocal(den[:, :], den[:, :]))
            link(dve.tensor_tensor(pp[:, :, :], pp[:, :, :], den[:, :].unsqueeze(1).to_broadcast([P, 2, NT]), ALU.mult))
            for n2 in range(2):
                part = cmb[:, :, n2 * NE:(n2 + 1) * NE]
                last = dve.tensor_tensor(part, part, pp[:, n2, :].unsqueeze(2).to_broadcast([P, NT, NE]), ALU.mult)
            link(last)
            link(dve.tensor_tensor(cmb[:, :, 0:NE], cmb[:, :, 0:NE], cmb[:, :, NE:], ALU.add))
            link(dve.tensor_copy(w_same[:, :], cmb[:, :, NX]))
            link(dve.tensor_copy(cmb_hi[:, :, :], cmb[:, :, 0:NE]))
            link(dve.tensor_tensor(cmb[:, :, NE:], cmb[:, :, 0:NE], cmb_hi[:, :, :].bitcast(F32), ALU.subtract))
            dve.tensor_copy(cmb[:, :, 0:NE], cmb_hi[:, :, :].bitcast(F32)).then_inc(cmb_ready, 1)

            def same(a, b):
                for t in range(a, b):
                    dve.scalar_tensor_tensor(x_res[:, t, :], xn3[:, t, :], w_same[:, t:t + 1], x_res[:, t, :],
                                             ALU.mult, ALU.add).then_inc(same_done, 1)

            same(0, NT // 2)

            def beside(e):
                if e + 2 < NX:
                    routed_hi(e + 2, (e + 2) % RING, 48 * ((e + 2) // RING + 1))
                if e == 2:
                    same(3 * NT // 4, NT)
                if e == NX - 4:
                    dve.wait_ge(sh_in, 32)
                    dve.tensor_copy(sh_hi[:, :], sh_raw[:, :]).then_inc(sh_split, 1)
                    dve.wait_ge(sh_split, 1)
                    dve.tensor_tensor(sh_lo[:, :], sh_raw[:, :], sh_hi[:, :].bitcast(F32), ALU.subtract).then_inc(sh_split, 1)

            def output(c):
                for t in range(2):
                    dve.wait_ge(oB_ps, 2 * c + t + 1)
                    dve.tensor_tensor(o_sb[:, t, :, :], psO[t].rearrange("p (n d) -> p n d", n=2),
                                      x_res[:, ds(CHT * c + 2 * t, 2), :], ALU.add).then_inc(o_ready, 1)
                for t in range(2):
                    dve.wait_ge(stored[t], 16 * (c + 1))

            def chunk(c):
                first = isinstance(c, int)
                if first:
                    dve.wait_ge(same_done, NT // 2)
                    beside(0)
                for e in range(ITEMS):
                    i = c * ITEMS + e
                    s = e % 2
                    dve.wait_ge(up_ps, i + 1)
                    dve.wait_ge(sg_ready, i + 1)
                    dve.tensor_tensor(t1[:, s, :], sg[:, s, :], psU[s], ALU.mult).then_inc(t1_ready, 1)
                    if first and e == 0:
                        same(NT // 2, 3 * NT // 4)
                    dve.wait_ge(t1_ready, i + 1)
                    if e < NX:
                        dve.wait_ge(c_ps, c * NX + e + 1)
                        dve.tensor_tensor(t1[:, s, :], t1[:, s, :], psC[s], ALU.mult).then_inc(t2_ready, 1)
                    else:
                        dve.sem_inc(t2_ready, 1)
                    if first and e == 0:
                        dve.wait_ge(same_done, 3 * NT // 4)
                    dve.wait_ge(hhi_ready, i + 1)
                    dve.tensor_tensor(h_lo[:, s, :], t1[:, s, :], h_hi[:, s, :].bitcast(F32), ALU.subtract).then_inc(h_ready, 1)
                    if isinstance(c, int):
                        beside(e + 1)
                    elif e == 1:
                        output(c - 1)
            chunk(0)
            with dve.Fori(1, NCH) as c:
                chunk(c)
            output(NCH - 1)

        @block.tensor
        def _(pe):
            def products(out, pairs, first, last):
                todo = [(st[a], mv_[b]) for st, mv_ in pairs for a, b in ((0, 0), (0, 1), (1, 0))]
                for n, (a, b) in enumerate(todo):
                    mm = pe.matmul(out, a, b, start=first and n == 0, stop=last and n == len(todo) - 1)
                return mm
            x3 = (x3_hi, x3_lo)
            pe.wait_ge(r_in, 32)
            parts = [(k, part) for k in range(KE) for part in x3]
            for n, (k, part) in enumerate(parts):
                for j in range(NCH):
                    cols = slice(KS - 1 + j * BANK, KS - 1 + (j + 1) * BANK)
                    last = pe.matmul(bank[4][32 * j:32 * j + 32, :], r_w[:, k, :], part[:, k, cols].bitcast(F32),
                                     start=(n == 0), stop=(n == len(parts) - 1))
            last.then_inc(lgT_ps, 1)
            pe.wait_ge(cv_in, 16)
            for k in range(KE):
                for tap in range(KS):
                    last = pe.transpose(bank[6 + k][:, tap * P:(tap + 1) * P], cv_raw[:, k * P:(k + 1) * P, tap], ident[:, :])
                last.then_inc(cv_ps, 1)
            pe.wait_ge(lgT_ready, 1)
            for t in range(CHT):
                last = pe.transpose(bank[5][:, t * P:(t + 1) * P], sg[:, 0, t * P:(t + 1) * P], ident[:, :])
            last.then_inc(lg_ps, 1)

            def weights_transposed():
                pe.wait_ge(cmb_ready, 1)
                pe.wait_ge(cv_split, 2 * KE)
                for t in range(NT):
                    last = pe.transpose(ps[0:2 * NE, 4 * BANK + t * P:4 * BANK + (t + 1) * P], cmb[:, t, :], ident[:, :])
                last.then_inc(cT_ps, 1)
                pe.wait_ge(cT_ready, 1)
                pe.wait_ge(row_made, 3)

            def down(c, e):
                i = c * ITEMS + e
                pe.wait_ge(h_ready, i + 1)
                for m in range(KE):
                    sl = slice(2 * KE * FI + m * P, 2 * KE * FI + (m + 1) * P)
                    wd = ((w_hi[:, e, sl], w_lo[:, e, sl]) if e < NX else
                          (sh_hi[:, KE * FI + m * P:KE * FI + (m + 1) * P], sh_lo[:, KE * FI + m * P:KE * FI + (m + 1) * P]))
                    last = products(psO[m], [(wd, (h_hi[:, e % 2, :], h_lo[:, e % 2, :]))], e == 0, e == ITEMS - 1)
                last.then_inc(down_done, 1)

            def output(c):
                pe.wait_ge(oT_ready, c + 1)
                for t in range(2):
                    for r in range(2):
                        for k in range(KE):
                            last = pe.transpose(psO[t][:, r * DM + k * P:r * DM + (k + 1) * P],
                                                oT[:, k, (2 * t + r) * P:(2 * t + r + 1) * P], ident[:, :])
                    last.then_inc(oB_ps, 1)

            def chunk(c):
                def cols(shift=KS - 1):
                    return ds(c * BANK + shift, BANK)

                for e in range(ITEMS):
                    i = c * ITEMS + e
                    s = e % 2
                    mov = [(x3_hi[:, k, cols()], x3_lo[:, k, cols()]) for k in range(KE)]
                    if e < NX:
                        pe.wait_ge(w_ready, e + 1)
                        gate, up = ([(tuple(x[:, e, (o + k) * FI:(o + k + 1) * FI] for x in (w_hi, w_lo)), mov[k])
                                     for k in range(KE)] for o in (0, KE))
                    else:
                        if isinstance(c, int):
                            pe.wait_ge(sh_split, 2)
                        gate = [(tuple(x[:, tap, k, :] for x in (cv_hi, cv_lo)), (x3_hi[:, k, cols(tap)], x3_lo[:, k, cols(tap)]))
                                for tap in range(KS) for k in range(KE)]
                        up = [(tuple(x[:, k * FI:(k + 1) * FI] for x in (sh_hi, sh_lo)), mov[k]) for k in range(KE)]
                    if e >= 2 or not isinstance(c, int):
                        pe.wait_ge(sg_ready, i - 1)
                    products(psG[s], gate, True, True).then_inc(gate_ps, 1)
                    if e >= 2 or not isinstance(c, int):
                        pe.wait_ge(t2_ready, i - 1)
                    products(psU[s], up, True, True).then_inc(up_ps, 1)
                    first = isinstance(c, int)
                    if e == 0 and not first:
                        down(c - 1, ITEMS - 1)
                    if e == 1 and first:
                        weights_transposed()
                    for n in (((), (0, 1))[e] if first and e < 2 else (e,) if e < NX else ()):
                        pe.matmul(psC[n % 2], row[:, n, :], cT[:, ds(c * BANK, BANK)], start=True, stop=True).then_inc(c_ps, 1)
                    if e == 1 and not first:
                        output(c - 1)
                    if e == 2:
                        if not first:
                            pe.wait_ge(o_ready, 2 * c)
                        down(c, 0)
                    if e >= 2:
                        down(c, e - 1)

            chunk(0)
            with pe.Fori(1, NCH) as c:
                chunk(c)
            down(NCH - 1, ITEMS - 1)
            output(NCH - 1)


def decoder_layer(nc, ins, out):
    def part(prefix):
        return {k[len(prefix):]: v for k, v in ins.items() if k.startswith(prefix)}
    w_attn, w_xattn, w_ffn = part("L0_attn_"), part("L0_xattn_"), part("L0_ffn_")
    context = ins["ctx_1024"]

    with ExitStack() as keep:
        def sb(name, shape, dt=F32, stack=keep):
            return stack.enter_context(nc.sbuf_tensor(name, shape, dt))

        def sem(name):
            return keep.enter_context(nc.semaphore(name))

        x_res = sb("x_res", [P, NT, DM])
        ident = sb("ident", [P, P])
        power = sb("power", [P, CHT])
        spare = sb("spare", [P, 5])
        stats2 = sb("stats2", [P, NT, 6])
        ps = keep.enter_context(nc.psum_tensor("ps", [P, 8 * BANK], F32))
        with ExitStack() as third:
            w_exp_raw = sb("w_exp_raw", [P, RING, WE], F32, third)
            r_w, r_b = sb("r_w", [P, KE, 32], F32, third), sb("r_b", [P, NE], F32, third)
            row = sb("row", [2 * NE, NE, P], F32R, third)
            sg = sb("sg", [P, 2, BANK], F32, third)
            sh_raw = sb("sh_raw", [P, KE * FI + DM], F32, third)
        with ExitStack() as masks:
            mask_sb = sb("mask_sb", [P, 2, SK], I32, masks)
        with ExitStack() as second:
            c_raw = sb("c_raw", [P, KC, DM], F32, second)
            w_qkv_raw = sb("w_qkv_raw", [P, 3, KE, DM], F32, second)
            bv = sb("bv", [P, DM], F32, second)
            wqT = sb("wqT", [P, KE, DM], F32, second)
            xn2 = sb("xn2", [P, 2, DM], F32, second)
        w_in_hi, w_in_lo = sb("w_in_hi", [P, KE, 2 * DI], F32R), sb("w_in_lo", [P, KE, 2 * DI], F32R)
        xnT_hi, xnT_lo = sb("xnT_hi", [P, KE, CH], F32R), sb("xnT_lo", [P, KE, CH], F32R)
        bq, bk = sb("bq", [P, KE]), sb("bk", [P, KE])

        c_zero, c_in, w_qkv_in, b_in = sem("ctx_zeroed"), sem("ctx_in"), sem("w_qkv_in"), sem("b_qkv_in")

        def clear_context(pool):
            pool.memset(c_raw[:, KC - 1, :], 0.0).then_inc(c_zero, 1)

        def load_context(sp_):
            for n, name in enumerate(("Wq", "Wk", "Wv")):
                sp_.dma_start(w_qkv_raw[:, n, :, :], w_xattn[name].rearrange("(k p) e -> p k e", p=P)).then_inc(w_qkv_in, 16)
            sp_.wait_ge(c_zero, 1)
            sp_.dma_start(c_raw[:, 0:KC - 1, :], context[0, 0:(KC - 1) * P, :].rearrange("(n p) d -> p n d", p=P)).then_inc(c_in, 16)
            sp_.dma_start(c_raw[0:SK - (KC - 1) * P, KC - 1, :], context[0, (KC - 1) * P:, :]).then_inc(c_in, 16)
            for t, name in ((bq, "bq"), (bk, "bk")):
                sp_.dma_start(t[:, :], w_xattn[name].rearrange("(k p) -> p k", p=P), allow_slow_non_contiguous=True).then_inc(b_in, 16)
            sp_.dma_start(bv[:, :], w_xattn["bv"].rearrange("(a n) -> a n", a=1).to_broadcast([P, DM])).then_inc(b_in, 16)

        row_made = sem("row_made")
        r_zero, r_in, w_exp_in = sem("r_zeroed"), sem("r_in"), [sem(f"w_exp_in{i}") for i in range(RING)]

        def clear_router(pool):
            pool.memset(r_w[:, :, :], 0.0).then_inc(r_zero, 1)
            pool.memset(row[:, :, :].bitcast(F32), 0.0).then_inc(row_made, 1)
            for n in range(2):
                pool.wait_ge(row_made, n + 1)
                pool.affine_select(out=row[:, :, :], in_=row[:, :, :].bitcast(F32), compare_op=ALU.not_equal, fill=1.0, base=-NE * n,
                                   pattern=[[-1, NE], [0, P]], channel_multiplier=1).then_inc(row_made, 1)

        def load_expert(sp_, e, slot):
            dst, n = w_exp_raw[:, slot, :], KE * FI
            for i, name in enumerate(("expert_gate_w", "expert_up_w")):
                sp_.dma_start(dst[:, i * n:(i + 1) * n].rearrange("p (k n) -> p k n", k=KE),
                              w_ffn[name][ds(e, 1), :, :].rearrange("a (k p) n -> p (a k) n", p=P)).then_inc(w_exp_in[slot], 16)
            sp_.dma_start(dst[:, 2 * n:], w_ffn["expert_down_w"][ds(e, 1), :, :].rearrange("a p n -> p (a n)")).then_inc(w_exp_in[slot], 16)

        def load_router(sp_):
            sp_.wait_ge(r_zero, 1)
            sp_.dma_start(r_w[:, :, 0:NE], w_ffn["router_w"].rearrange("(k p) n -> p k n", p=P)).then_inc(r_in, 16)
            sp_.dma_start(r_b[:, :], w_ffn["router_bias"].rearrange("(a n) -> a n", a=1).to_broadcast([P, NE])).then_inc(r_in, 16)
            for e in range(RING):
                load_expert(sp_, e, e)

        scan_block(nc, ins["x"], w_attn, x_res, stats2, (w_in_hi, w_in_lo, xnT_hi, xnT_lo), load_context, clear_context,
                   ident, power, ps)
        x3_hi = sb("x3_hi", [P, KE, KS - 1 + SEQ], F32R)
        x3_lo = sb("x3_lo", [P, KE, KS - 1 + SEQ], F32R)
        with nc.sbuf_tensor("xn3", [P, NT, DM], F32) as xn3:
            attention_block(nc, ins["mask_BxSxS2_ik1"], x_res, stats2, xn3, x3_hi, x3_lo,
                            (c_raw, mask_sb, w_qkv_raw, bv, bq, bk, wqT, xn2), (w_qkv_in, b_in, c_in), load_router, clear_router,
                            ident, spare, ps)
        expert_block(nc, w_ffn, x_res, xn3, x3_hi, x3_lo, (w_exp_raw, r_w, r_b, row, sg, sh_raw), r_in, row_made, w_exp_in, load_expert,
                     ident, ps, out)


def kernel(**inputs):
    import numpy as _np
    import concourse.bacc as _bacc
    from concourse import mybir as _mybir
    from concourse.bass_utils import run_bass_kernel_spmd as _run

    nc = _bacc.Bacc("TRN2", target_bir_lowering=False, num_devices=1)
    arrays, ins = {}, {}
    for name, value in inputs.items():
        a = _np.ascontiguousarray(value)
        arrays[f"in_{name}_dram"] = a
        ins[name] = nc.dram_tensor(f"in_{name}_dram", a.shape, _mybir.dt.from_np(a.dtype), kind="ExternalInput").ap()
    out = nc.dram_tensor("out_0_dram", (1, SEQ, DM), F32, kind="ExternalOutput").ap()
    decoder_layer(nc, ins, out)
    r = _run(nc, [arrays], core_ids=[0])
    return r.results[0]["out_0_dram"]
```
